# Optimizing a Trainium2 kernel written in Bass

```python
import numpy as np
import jax
import jax.numpy as jnp

def _softmax(x, axis=-1):
    return jax.nn.softmax(x, axis=axis)

def _gelu(x):
    return jax.nn.gelu(x, approximate=True)

def _silu(x):
    return jax.nn.silu(x)

def _sigmoid(x):
    return jax.nn.sigmoid(x)

def _layernorm(x, axis=-1, eps=1e-05):
    m = jnp.mean(x, axis=axis, keepdims=True)
    v = jnp.var(x, axis=axis, keepdims=True)
    return (x - m) / jnp.sqrt(v + eps)

def _scatter_add(tgt, idx, src, axis=0):
    return tgt.at[idx].add(src)

def _segment_sum(src, seg, n):
    return jax.ops.segment_sum(src, seg, n)
kernel_name = 'mk_recurrent_d2_jaxref_r8_859c8b'

def setup_inputs(seed: int=0):
    np.random.seed(seed)
    _w = jnp.asarray

    def _L0_attn_setup():
        import jax, jax.numpy as jnp
        import numpy as np
        B, N, E = (4, 512, 256)
        H_DIM = 256
        HEADS = 16
        DH = H_DIM // HEADS
        LN_EPS = 1e-05

        def _heads(t):
            b, n, _ = t.shape
            return t.reshape(b, n, HEADS, DH).transpose(0, 2, 1, 3)

        def _layernorm(x, g, b):
            mu = jnp.mean(x, axis=-1, keepdims=True)
            var = jnp.mean(jnp.square(x - mu), axis=-1, keepdims=True)
            return (x - mu) * jax.lax.rsqrt(var + LN_EPS) * g + b
        key = jax.random.key(seed)
        ks = jax.random.split(key, 10)
        s = 1.0 / np.sqrt(E)
        so = 1.0 / np.sqrt(H_DIM)
        return {'x': jax.random.normal(ks[0], (B, N, E), jnp.float32), 'Wqk': jax.random.normal(ks[1], (E, H_DIM), jnp.float32) * s, 'bqk': jnp.zeros((H_DIM,), jnp.float32), 'Wv': jax.random.normal(ks[2], (E, H_DIM), jnp.float32) * s, 'bv': jnp.zeros((H_DIM,), jnp.float32), 'Wu': jax.random.normal(ks[3], (E, H_DIM), jnp.float32) * s, 'bu': jnp.zeros((H_DIM,), jnp.float32), 'Wo': jax.random.normal(ks[4], (H_DIM, E), jnp.float32) * so, 'bo': jnp.zeros((E,), jnp.float32), 'ln_g': jnp.ones((H_DIM,), jnp.float32), 'ln_b': jnp.zeros((H_DIM,), jnp.float32)}
    _L0_attn_in = _L0_attn_setup()

    def _L0_ffn_setup():
        import jax, jax.numpy as jnp
        import numpy as np
        H = 256
        I = 128
        E = 32
        K = 4
        N_SHARED = 1
        EPS = 1e-06

        def _rmsnorm(x, w, eps=EPS):
            var = jnp.mean(jnp.square(x), axis=-1, keepdims=True)
            return x * jax.lax.rsqrt(var + eps) * w

        def _moe_core(x, gate_w, w13, w2):
            T = x.shape[0]
            N = T * K
            C = 2 * N // E
            logits = jnp.einsum('th,eh->te', x.astype(jnp.float32), gate_w.astype(jnp.float32))
            scores = jax.nn.softmax(logits, axis=-1)
            topk_w, topk_ids = jax.lax.top_k(scores, K)
            topk_w = topk_w / jnp.sum(topk_w, axis=-1, keepdims=True)
            flat_ids = topk_ids.reshape(-1)
            flat_w = topk_w.reshape(-1)
            order = jnp.argsort(flat_ids)
            sorted_eid = flat_ids[order]
            tok = order // K
            counts = jnp.zeros((E,), jnp.int32).at[flat_ids].add(1)
            starts = jnp.cumsum(counts) - counts
            pos = jnp.arange(N) - starts[sorted_eid]
            buf = jnp.zeros((E, C, x.shape[1]), x.dtype).at[sorted_eid, pos].set(x[tok], mode='drop')
            gu = jnp.einsum('ech,ehf->ecf', buf, w13)
            g, u = jnp.split(gu, 2, axis=-1)
            act = jax.nn.silu(g) * u
            eo = jnp.einsum('eci,eih->ech', act, w2)
            out_slots = eo[sorted_eid, pos]
            routed = jnp.zeros_like(x).at[tok].add(out_slots * flat_w[order][:, None])
            return routed
        key = jax.random.key(seed)
        ks = jax.random.split(key, 8)
        s = 1.0 / np.sqrt(H)
        si = 1.0 / np.sqrt(I)
        return {'hidden_states': jax.random.normal(ks[0], (1, 512, H), jnp.float32), 'norm_w': jnp.ones((H,), jnp.float32), 'gate_w': jax.random.normal(ks[1], (E, H), jnp.float32) * s, 'w13': jax.random.normal(ks[2], (E, H, 2 * I), jnp.float32) * s, 'w2': jax.random.normal(ks[3], (E, I, H), jnp.float32) * si, 'shared_gate_w': jax.random.normal(ks[4], (H, I * N_SHARED), jnp.float32) * s, 'shared_up_w': jax.random.normal(ks[5], (H, I * N_SHARED), jnp.float32) * s, 'shared_down_w': jax.random.normal(ks[6], (I * N_SHARED, H), jnp.float32) * si}
    _L0_ffn_in = _L0_ffn_setup()

    def _L1_attn_setup():
        import jax, jax.numpy as jnp
        import numpy as np
        BSZ, T, D, N, R = (2, 256, 256, 16, 128)
        key = jax.random.key(seed)
        ks = jax.random.split(key, 5)
        x = jax.random.normal(ks[0], (BSZ, T, D), dtype=jnp.float32)
        W_xproj = jax.random.normal(ks[1], (R + 2 * N, D), dtype=jnp.float32) * 0.02
        W_dt = jax.random.normal(ks[2], (D, R), dtype=jnp.float32) * 0.02
        b_dt = jnp.exp(jax.random.uniform(ks[3], (D,), minval=np.log(0.001), maxval=np.log(0.1)).astype(jnp.float32))
        A_log = jax.random.normal(ks[4], (D, N), dtype=jnp.float32) * 0.01
        D_param = jnp.ones((D,), dtype=jnp.float32)
        return {'x': x, 'W_xproj': W_xproj, 'W_dt': W_dt, 'b_dt': b_dt, 'A_log': A_log, 'D_param': D_param}
    _L1_attn_in = _L1_attn_setup()

    def _L1_ffn_setup():
        import jax, jax.numpy as jnp
        import numpy as np
        B, S, DIM = (2, 256, 256)
        E, K = (8, 2)
        H = DIM * 4 // 3
        key = jax.random.key(seed)
        ks = jax.random.split(key, 8)
        s = 0.02
        x = jax.random.normal(ks[0], (B, S, DIM), dtype=jnp.float32)
        sw1 = jax.random.normal(ks[1], (H, DIM), dtype=jnp.float32) * s
        sw2 = jax.random.normal(ks[2], (DIM, H), dtype=jnp.float32) * s
        sw3 = jax.random.normal(ks[3], (H, DIM), dtype=jnp.float32) * s
        ew1 = jax.random.normal(ks[4], (E, H, DIM), dtype=jnp.float32) * s
        ew2 = jax.random.normal(ks[5], (E, DIM, H), dtype=jnp.float32) * s
        ew3 = jax.random.normal(ks[6], (E, H, DIM), dtype=jnp.float32) * s
        wr = jax.random.normal(ks[7], (E, DIM), dtype=jnp.float32) * s
        return {'x': x, 'sw1': sw1, 'sw2': sw2, 'sw3': sw3, 'ew1': ew1, 'ew2': ew2, 'ew3': ew3, 'wr': wr}
    _L1_ffn_in = _L1_ffn_setup()
    _d = {'L0_attn_x': _L0_attn_in['x'], 'L0_attn_Wqk': _L0_attn_in['Wqk'], 'L0_attn_bqk': _L0_attn_in['bqk'], 'L0_attn_Wv': _L0_attn_in['Wv'], 'L0_attn_bv': _L0_attn_in['bv'], 'L0_attn_Wu': _L0_attn_in['Wu'], 'L0_attn_bu': _L0_attn_in['bu'], 'L0_attn_Wo': _L0_attn_in['Wo'], 'L0_attn_bo': _L0_attn_in['bo'], 'L0_attn_ln_g': _L0_attn_in['ln_g'], 'L0_attn_ln_b': _L0_attn_in['ln_b'], 'L0_ffn_norm_w': _L0_ffn_in['norm_w'], 'L0_ffn_gate_w': _L0_ffn_in['gate_w'], 'L0_ffn_w13': _L0_ffn_in['w13'], 'L0_ffn_w2': _L0_ffn_in['w2'], 'L0_ffn_shared_gate_w': _L0_ffn_in['shared_gate_w'], 'L0_ffn_shared_up_w': _L0_ffn_in['shared_up_w'], 'L0_ffn_shared_down_w': _L0_ffn_in['shared_down_w'], 'L1_attn_W_xproj': _L1_attn_in['W_xproj'], 'L1_attn_W_dt': _L1_attn_in['W_dt'], 'L1_attn_b_dt': _L1_attn_in['b_dt'], 'L1_attn_A_log': _L1_attn_in['A_log'], 'L1_attn_D_param': _L1_attn_in['D_param'], 'L1_ffn_sw1': _L1_ffn_in['sw1'], 'L1_ffn_sw2': _L1_ffn_in['sw2'], 'L1_ffn_sw3': _L1_ffn_in['sw3'], 'L1_ffn_ew1': _L1_ffn_in['ew1'], 'L1_ffn_ew2': _L1_ffn_in['ew2'], 'L1_ffn_ew3': _L1_ffn_in['ew3'], 'L1_ffn_wr': _L1_ffn_in['wr']}
    _x0 = _d['L0_attn_x']
    _d['L0_attn_x'] = jax.random.normal(jax.random.fold_in(jax.random.key(seed), 1), (2, 1024, 256), dtype=_x0.dtype)
    del _x0
    return _d

def reference(L0_attn_x, L0_attn_Wqk, L0_attn_bqk, L0_attn_Wv, L0_attn_bv, L0_attn_Wu, L0_attn_bu, L0_attn_Wo, L0_attn_bo, L0_attn_ln_g, L0_attn_ln_b, L0_ffn_norm_w, L0_ffn_gate_w, L0_ffn_w13, L0_ffn_w2, L0_ffn_shared_gate_w, L0_ffn_shared_up_w, L0_ffn_shared_down_w, L1_attn_W_xproj, L1_attn_W_dt, L1_attn_b_dt, L1_attn_A_log, L1_attn_D_param, L1_ffn_sw1, L1_ffn_sw2, L1_ffn_sw3, L1_ffn_ew1, L1_ffn_ew2, L1_ffn_ew3, L1_ffn_wr):

    def _L0_attn_ref(x, Wqk, bqk, Wv, bv, Wu, bu, Wo, bo, ln_g, ln_b):
        import jax, jax.numpy as jnp
        import numpy as np
        B, N, E = (4, 512, 256)
        H_DIM = 256
        HEADS = 16
        DH = H_DIM // HEADS
        LN_EPS = 1e-05

        def _heads(t):
            b, n, _ = t.shape
            return t.reshape(b, n, HEADS, DH).transpose(0, 2, 1, 3)

        def _layernorm(x, g, b):
            mu = jnp.mean(x, axis=-1, keepdims=True)
            var = jnp.mean(jnp.square(x - mu), axis=-1, keepdims=True)
            return (x - mu) * jax.lax.rsqrt(var + LN_EPS) * g + b
        q = x @ Wqk + bqk
        k = x @ Wqk + bqk
        v = jax.nn.silu(x @ Wv + bv)
        u = jax.nn.silu(x @ Wu + bu)
        q = jax.nn.elu(_heads(q))
        kh = jax.nn.elu(_heads(k))
        vh = _heads(v)
        kv = jnp.einsum('bhnd,bhne->bhde', kh, vh)
        out = jnp.einsum('bhnd,bhde->bhne', q, kv)
        out = out.transpose(0, 2, 1, 3).reshape(x.shape[0], x.shape[1], H_DIM)
        out = _layernorm(out, ln_g, ln_b)
        out = u * out
        return out @ Wo + bo

    def _L0_ffn_ref(hidden_states, norm_w, gate_w, w13, w2, shared_gate_w, shared_up_w, shared_down_w):
        import jax, jax.numpy as jnp
        import numpy as np
        H = 256
        I = 128
        E = 32
        K = 4
        N_SHARED = 1
        EPS = 1e-06

        def _rmsnorm(x, w, eps=EPS):
            var = jnp.mean(jnp.square(x), axis=-1, keepdims=True)
            return x * jax.lax.rsqrt(var + eps) * w

        def _moe_core(x, gate_w, w13, w2):
            T = x.shape[0]
            N = T * K
            C = 2 * N // E
            logits = jnp.einsum('th,eh->te', x.astype(jnp.float32), gate_w.astype(jnp.float32))
            scores = jax.nn.softmax(logits, axis=-1)
            topk_w, topk_ids = jax.lax.top_k(scores, K)
            topk_w = topk_w / jnp.sum(topk_w, axis=-1, keepdims=True)
            flat_ids = topk_ids.reshape(-1)
            flat_w = topk_w.reshape(-1)
            order = jnp.argsort(flat_ids)
            sorted_eid = flat_ids[order]
            tok = order // K
            counts = jnp.zeros((E,), jnp.int32).at[flat_ids].add(1)
            starts = jnp.cumsum(counts) - counts
            pos = jnp.arange(N) - starts[sorted_eid]
            buf = jnp.zeros((E, C, x.shape[1]), x.dtype).at[sorted_eid, pos].set(x[tok], mode='drop')
            gu = jnp.einsum('ech,ehf->ecf', buf, w13)
            g, u = jnp.split(gu, 2, axis=-1)
            act = jax.nn.silu(g) * u
            eo = jnp.einsum('eci,eih->ech', act, w2)
            out_slots = eo[sorted_eid, pos]
            routed = jnp.zeros_like(x).at[tok].add(out_slots * flat_w[order][:, None])
            return routed
        B, S, Hd = hidden_states.shape
        residual = hidden_states
        h = _rmsnorm(hidden_states, norm_w)
        x = h.reshape(-1, Hd)
        routed = _moe_core(x, gate_w, w13, w2)
        shared = jax.nn.silu(x @ shared_gate_w) * (x @ shared_up_w) @ shared_down_w
        out = residual + (routed + shared).reshape(B, S, Hd)
        return out

    def _L1_attn_ref(x, W_xproj, W_dt, b_dt, A_log, D_param):
        import jax, jax.numpy as jnp
        import numpy as np
        BSZ, T, D, N, R = (2, 256, 256, 16, 128)
        r = W_dt.shape[1]
        n = A_log.shape[1]
        xz = jnp.einsum('btd,rd->btr', x, W_xproj)
        delta_r = xz[..., :r]
        B_mat = xz[..., r:r + n]
        C_mat = xz[..., r + n:]
        delta = jax.nn.softplus(jnp.einsum('btr,dr->btd', delta_r, W_dt) + b_dt)
        A = -jnp.exp(A_log)
        dA = jnp.exp(delta[..., None] * A)
        Bu = delta[..., None] * B_mat[:, :, None, :] * x[..., None]

        def step(h, inp):
            dA_t, Bu_t, C_t = inp
            h = dA_t * h + Bu_t
            y = jnp.sum(h * C_t[:, None, :], axis=-1)
            return (h, y)
        h0 = jnp.zeros((x.shape[0], x.shape[2], n), dtype=Bu.dtype)
        _, ys = jax.lax.scan(step, h0, (dA.swapaxes(0, 1), Bu.swapaxes(0, 1), C_mat.swapaxes(0, 1)))
        y = ys.swapaxes(0, 1)
        return y + x * D_param

    def _L1_ffn_ref(x, sw1, sw2, sw3, ew1, ew2, ew3, wr):
        import jax, jax.numpy as jnp
        import numpy as np
        B, S, DIM = (2, 256, 256)
        E, K = (8, 2)
        H = DIM * 4 // 3
        shared = jax.nn.silu(x @ sw1.T) * (x @ sw3.T) @ sw2.T
        logits = x @ wr.T
        probs = jax.nn.softmax(logits, axis=-1)
        top_p, top_i = jax.lax.top_k(probs, K)
        top_p = top_p / jnp.sum(top_p, axis=-1, keepdims=True)
        gates = jnp.sum(jax.nn.one_hot(top_i, E, dtype=x.dtype) * top_p[..., None], axis=-2)
        u = jnp.einsum('bsd,ehd->bseh', x, ew1)
        v = jnp.einsum('bsd,ehd->bseh', x, ew3)
        h = jax.nn.silu(u) * v
        eo = jnp.einsum('bseh,edh->bsed', h, ew2)
        return shared + jnp.einsum('bsed,bse->bsd', eo, gates)
    x = L0_attn_x
    xn = _layernorm(x, axis=-1)
    s = _L0_attn_ref(xn, L0_attn_Wqk, L0_attn_bqk, L0_attn_Wv, L0_attn_bv, L0_attn_Wu, L0_attn_bu, L0_attn_Wo, L0_attn_bo, L0_attn_ln_g, L0_attn_ln_b)
    g = _silu(_L0_ffn_ref(xn, L0_ffn_norm_w, L0_ffn_gate_w, L0_ffn_w13, L0_ffn_w2, L0_ffn_shared_gate_w, L0_ffn_shared_up_w, L0_ffn_shared_down_w))
    x = x + s * g
    xn = _layernorm(x, axis=-1)
    s = _L1_attn_ref(xn, L1_attn_W_xproj, L1_attn_W_dt, L1_attn_b_dt, L1_attn_A_log, L1_attn_D_param)
    g = _silu(_L1_ffn_ref(xn, L1_ffn_sw1, L1_ffn_sw2, L1_ffn_sw3, L1_ffn_ew1, L1_ffn_ew2, L1_ffn_ew3, L1_ffn_wr))
    x = x + s * g
    return x

_drawn_inputs = setup_inputs


def setup_inputs(seed=0):
    import zlib

    import numpy as np

    out = dict(_drawn_inputs(seed))
    spreads = {'L0_attn_bqk': (0.0, 0.1),
     'L0_attn_bv': (0.0, 0.1),
     'L0_attn_bu': (0.0, 0.1),
     'L0_attn_bo': (0.0, 0.1),
     'L0_attn_ln_g': (1.0, 0.2),
     'L0_attn_ln_b': (0.0, 0.1),
     'L0_ffn_norm_w': (1.0, 0.2),
     'L1_attn_D_param': (1.0, 0.6)}
    factors = {'L1_attn_W_xproj': 8.0,
     'L1_attn_W_dt': 8.0,
     'L1_attn_b_dt': 8.0,
     'L1_attn_A_log': 8.0,
     'L1_ffn_sw1': 5.425,
     'L1_ffn_sw2': 5.031,
     'L1_ffn_sw3': 5.024,
     'L1_ffn_ew1': 8.0,
     'L1_ffn_ew2': 8.0,
     'L1_ffn_ew3': 8.0,
     'L1_ffn_wr': 8.0}
    for name, (base, spread) in spreads.items():
        noise = np.random.default_rng([zlib.crc32(name.encode()), seed]).standard_normal(out[name].shape)
        drawn = base * np.exp(spread * noise) if base else spread * noise
        out[name] = jnp.asarray(drawn.astype(out[name].dtype))
    for name, factor in factors.items():
        out[name] = (out[name] * factor).astype(out[name].dtype)
    return out
```

```python
from contextlib import ExitStack

import concourse.bass as bass
from concourse import mybir

F32 = mybir.dt.float32
BF16 = mybir.dt.bfloat16
I32 = mybir.dt.int32
U32 = mybir.dt.uint32
ALU = mybir.AluOpType
ACT = mybir.ActivationFunctionType
AX_X = mybir.AxisListType.X

P = 128
D = 256
KD = D // P
BATCH, SEQ = 2, 1024
TOK = BATCH * SEQ
NT = TOK // P
HEAD = 16

E0, K0 = 32, 4
CAP0 = 2 * TOK * K0 // E0
I0 = 128
E1, K1 = 8, 2
H1 = D * 4 // 3
HB = -(-H1 // 3)
H1P = 3 * HB
N_STATE = 16
RANK = 128

EPS_LN = 1e-5
EPS_RMS = 1e-6
DROPPED = float(1 << 20)


def routed_tiles(experts, choices, multiple):
    n = (TOK * choices + experts * (P - 1)) // P
    return -(-n // multiple) * multiple


UNROLL = 4
R0 = routed_tiles(E0, K0, UNROLL)
R1 = routed_tiles(E1, K1, UNROLL)
TILES0 = NT + R0
TILES1 = NT + R1
WIDTH0 = KD * 2 * I0 + D
WIDTH1 = KD * 2 * H1P + 3 * D
SLOTS0 = E0 + 1
SLOTS1 = E1 + 1
LATE0 = SLOTS0 - 13
UNITS = N_STATE * BATCH * KD


def later(t, k):
    assert isinstance(t, int) or t.min_val >= k, (t.min_val, k)
    return not isinstance(t, int) or t >= k


def pipeline(eng, n, unroll, *stages):
    peel = 1 if min(lead for lead, _ in stages) >= 0 else 2
    def step(i, c):
        for lead, f in stages:
            if not isinstance(i, int) or 0 <= i + lead < n:
                f(i + lead, (c + lead) % unroll)

    for i in range(-max(lead for lead, _ in stages), peel * unroll):
        step(i, i)
    last = n - unroll
    if last > peel * unroll:
        with eng.Fori(peel, last // unroll, 1) as block:
            for c in range(unroll):
                step(block * unroll + c, c)
    for i in range(last, n - min(lead for lead, _ in stages)):
        step(i, i)


def two_layers(nc, x, w_qvu, b_qvu, w_o, rows4, gate0, moe0, moe1, w_xproj, w_dt, per_channel, wr, out):
    rows0 = nc.dram_tensor("rows0", [TILES0 * P, D], F32, kind="Internal").ap()
    outs0 = nc.dram_tensor("outs0", [TILES0 * P, D], F32, kind="Internal").ap()
    rows1 = nc.dram_tensor("rows1", [TILES1 * P, D], F32, kind="Internal").ap()
    outs1 = nc.dram_tensor("outs1", [TILES1 * P, D], F32, kind="Internal").ap()

    with ExitStack() as ctx:
        def sb(name, shape, dt=F32):
            return ctx.enter_context(nc.sbuf_tensor(name, shape, dt))

        def sem(name):
            return ctx.enter_context(nc.semaphore(name))

        class Area:
            def __init__(self, tensor, at=0):
                self.tensor, self.at = tensor, at

            def take(self, *shape, dt=F32, parts=P):
                n = 1
                for s in shape:
                    n *= s
                floats = n if dt in (F32, I32, U32) else n // 2
                v = self.tensor[0:parts, self.at:self.at + floats]
                self.at += floats
                if dt != F32:
                    v = v.bitcast(dt)
                if len(shape) == 2:
                    v = v.rearrange("p (a b) -> p a b", a=shape[0])
                if len(shape) == 3:
                    v = v.rearrange("p (a b c) -> p a b c", a=shape[0], b=shape[1])
                return v

        W = sb("W", [P, SLOTS0 * WIDTH0])
        X = sb("X", [P, NT, D])
        AR_H = sb("AR_H", [P, NT * D])
        AR_T = sb("AR_T", [P, NT * D])
        AR_U = sb("AR_U", [P, NT * D])
        R = sb("R", [P, 6144])
        H = AR_H[:, :].rearrange("p (t d) -> p t d", t=NT)
        U = AR_U[:, :].rearrange("p (t d) -> p t d", t=NT)
        XT = AR_T[:, :].rearrange("p (k n) -> p k n", k=KD)
        DELTA = AR_H[:, :].rearrange("p (k n) -> p k n", k=KD)
        DU = AR_U[:, :].rearrange("p (k n) -> p k n", k=KD)

        MB = Area(sb("MB", [P, 1024 + 512 + 2 * H1P + 2 * 3 * P + 1024]))
        ROWS = MB.take(4, D)
        ROWS_T = MB.take(2, D)
        HID = MB.take(2, H1P)
        HID_T = MB.take(2, 3 * P)
        OUTS = MB.take(4, D)

        CO = Area(sb("CO", [P, 1138]))
        IDENT = CO.take(P)
        BLOCKS = CO.take(P)
        BELOW = CO.take(P, dt=BF16)
        ONES = CO.take(P, dt=BF16)
        PICK = CO.take(2 * N_STATE, dt=BF16)
        IOTA_E = CO.take(E0)
        IOTA_T = CO.take(R0)
        STEPS = CO.take(NT)
        WEIGHT = CO.take(NT, K0)
        SLOT_IN = CO.take(K0, NT, dt=I32)
        SLOT_OUT = CO.take(K0, NT, dt=I32)
        EXPERT = CO.take(TILES0, dt=I32)
        STAT = CO.take(4, 6)
        AGGR = CO.take(4, 2)
        MEAN_VAR = CO.take(NT, 2)
        RSTD = CO.take(NT)
        TOTAL = CO.take(NT)
        RRMS = CO.take(NT)
        A_NEG = CO.take(KD, N_STATE)
        B_DT = CO.take(KD)
        D_SKIP = CO.take(KD)
        VARS = CO.take(2, 4)
        ROOTS = CO.take(2, 4)
        PRODS = CO.take(2, 4)
        EPS_COL = CO.take(1)
        assert CO.at <= 1138

        RA = Area(R)
        W_QVU = RA.take(KD, 3 * D)
        W_O = RA.take(KD, D)
        GATE0 = RA.take(KD, E0)
        B_QVU = RA.take(3 * D)
        ROW4 = RA.take(4, D)
        B_O, LN_G, LN_B, NORM_W = (ROW4[:, i, :] for i in range(4))
        TOP = RA.take(NT, 8)
        TOP_ID = RA.take(NT, 8, dt=U32)
        TOP_IDF = RA.take(NT, 8)
        XN_S = RA.take(2, D)
        H_S = RA.take(2, D)
        HT_S = RA.take(2, D)
        SMALL = RA.take(5, E0)
        assert RA.at <= 6144
        RC = Area(R)
        GOT = RC.take(2, K0 + 1, D)
        ACC = RC.take(2, D)
        TANH = RC.take(2, D)
        XN1_S = RC.take(2, D)
        XT1_S = RC.take(2, D)
        ST1 = RC.take(6)
        TOP1 = RC.take(NT, 8)
        TOP1_ID = RC.take(NT, 8, dt=U32)
        TOP1_IDF = RC.take(NT, 8)
        SMALL1 = RC.take(5, E1)
        RT1 = RC.at
        assert RC.at + 2 * NT * E1 + 2 * NT * E1 <= 6144
        RS = Area(R)
        C_SB = RS.take(2, SEQ)
        DA = RS.take(2, SEQ)
        Z = RS.take(2, SEQ)
        RD = Area(R)
        DELTA_R = RD.take(TOK)
        BC = RD.take(TOK)
        BC_HI = RD.take(TOK, dt=BF16)
        assert RD.at <= 6144

        WA = Area(W, LATE0 * WIDTH0)
        XT_S = WA.take(2, D)
        PRE = WA.take(2, 3 * D)
        ELU = WA.take(2, D)
        TH = WA.take(2, 2 * D)
        Q_S = WA.take(2, D)
        V_S = WA.take(2, D)
        QT_S = WA.take(2, D)
        Z_S = WA.take(2, D)
        ZT_S = WA.take(2, D)
        KV = WA.take(BATCH * KD, P)
        RT0 = WA.at
        assert RT0 + R0 * (E0 + 1) <= SLOTS0 * WIDTH0

        WB = Area(W, SLOTS1 * WIDTH1)
        XN1 = WB.take(NT, D)
        W_DT = WB.take(D)
        W_XP = WB.take(KD, RANK + 96)
        WR = WB.take(KD, E1)
        BC3 = WB.take(TOK, dt=BF16)
        assert WB.at <= SLOTS0 * WIDTH0

        PS = ctx.enter_context(nc.psum_tensor("PS", [P, 8, 512], F32))

        MIX_BANKS = ({"rows": (0, 5), "up": (1, 2), "hid": 3, "outs": (4, 6)},
                     {"rows": (0, 0), "up": (1, 1), "hid": 3, "outs": (4, 4)})
        C_BANK, B_BANK = 5, 6

        x_loaded, small_loaded, attn_w_loaded = sem("x_loaded"), sem("small_loaded"), sem("attn_w_loaded")
        w0_loaded, w0_late = sem("w0_loaded"), sem("w0_late")
        zero_ready, zero_filled = sem("zero_ready"), sem("zero_filled")
        consts_ready, consts_cleared = sem("consts_ready"), sem("consts_cleared")
        rows_copied, h_stored = sem("rows_copied"), sem("h_stored")
        v_step = sem("v_step")
        h_ready, turned0, evac0, logits0 = sem("h_ready"), sem("turned0"), sem("evac0"), sem("logits0")
        st_a, st_b, st_c, xn_s_done = sem("st_a"), sem("st_b"), sem("st_c"), sem("xn_s_done")

        class Routing:
            def __init__(self, n):
                self.top, self.top_id = sem(f"top{n}"), sem(f"top_id{n}")
                self.diff, self.exps = sem(f"diff{n}"), sem(f"exps{n}")
                self.mask, self.ranks = sem(f"mask{n}"), sem(f"ranks{n}")
                self.slots, self.experts = sem(f"slots{n}"), sem(f"experts{n}")
                self.scattered = sem(f"scattered{n}")

        r0, r1 = Routing(0), Routing(1)

        xt_staged, qvu_ready, pre_ready, th_ready = sem("xt_staged"), sem("qvu_ready"), sem("pre_ready"), sem("th_ready")
        pre_done, elu_step, qv_ready = sem("pre_done"), sem("elu_step"), sem("qv_ready")
        kv_added, q_turned, qt_saved, kv_ready = sem("kv_added"), sem("q_turned"), sem("qt_saved"), sem("kv_ready")
        qt_staged, o_ready, z_step, z_ready = sem("qt_staged"), sem("o_ready"), sem("z_step"), sem("z_ready")
        z_turned, zt_ready, wo_done, s_ready = sem("z_turned"), sem("zt_ready"), sem("wo_done"), sem("s_ready")

        o_sums, o_stats, o_dev = sem("o_sums"), sem("o_stats"), sem("o_dev")

        class Mixture:
            def __init__(self, n):
                self.loaded = [sem(f"m{n}_loaded{i}") for i in range(2)]
                self.stored = [sem(f"m{n}_stored{i}") for i in range(2)]
                self.turned = sem(f"m{n}_turned")
                self.rows_t = sem(f"m{n}_rows_t")
                self.hidden = sem(f"m{n}_hidden")
                self.tanh = sem(f"m{n}_tanh")
                self.half = sem(f"m{n}_half")
                self.gated = sem(f"m{n}_gated")
                self.hid_turned = sem(f"m{n}_hid_turned")
                self.hid_t = sem(f"m{n}_hid_t")
                self.down = sem(f"m{n}_down")
                self.outs = sem(f"m{n}_outs")

        m0, m1 = Mixture(0), Mixture(1)

        class Combine:
            def __init__(self, n):
                self.got = [sem(f"c{n}_got{i}") for i in range(2)]
                self.shared = [sem(f"c{n}_shared{i}") for i in range(2)]
                self.step = sem(f"c{n}_step")
                self.acc = sem(f"c{n}_acc")
                self.tanh = sem(f"c{n}_tanh")
                self.x = sem(f"c{n}_x")
                if n == 0:
                    self.xn = sem("c0_xn")
                    self.turned = sem("c0_turned")
                    self.xt = sem("c0_xt")
                    self.logits = sem("c0_logits")
                else:
                    self.y_staged = sem("c1_y_staged")
                    self.y_rows = sem("c1_y_rows")

        c0, c1 = Combine(0), Combine(1)
        w1_loaded, small1_loaded, xn1_stored, out_stored = sem("w1_loaded"), sem("small1_loaded"), sem("xn1_stored"), sem("out_stored")
        xz_ready, dr_ready, bc_copied, bc_step, bc3_ready = sem("xz_ready"), sem("dr_ready"), sem("bc_copied"), sem("bc_step"), sem("bc3_ready")
        dl_psum, dl_exp, dl_max, dl_ln, dl_step, du_ready = sem("dl_psum"), sem("dl_exp"), sem("dl_max"), sem("dl_ln"), sem("dl_step"), sem("du_ready")
        a_exp, a_ready, act_step = sem("a_exp"), sem("a_ready"), sem("act_step")
        c_spread, b_spread, c_copied, da_ready = sem("c_spread"), sem("b_spread"), sem("c_copied"), sem("da_ready")
        bu_ready, scanned, hc_ready, y_added = sem("bu_ready"), sem("scanned"), sem("hc_ready"), sem("y_added")

        block = ctx.enter_context(nc.Block())

        def tiles_of(dram, t, n):
            return dram[bass.ds(t * P, n * P), :].rearrange("(j p) d -> p j d", p=P)

        @block.sync
        def _(sp):
            sp.dma_start(X[:, :, :], x).then_inc(x_loaded, 16)
            sp.dma_start(ROW4, rows4[None, :, :].broadcast_to([P, 4, D])).then_inc(small_loaded, 16)
            sp.dma_start(GATE0, gate0).then_inc(small_loaded, 16)
            sp.dma_start(W_QVU, w_qvu).then_inc(attn_w_loaded, 16)
            sp.dma_start(B_QVU, b_qvu[None, :].broadcast_to([P, 3 * D])).then_inc(attn_w_loaded, 16)
            sp.dma_start(W_O, w_o).then_inc(attn_w_loaded, 16)
            sp.wait_ge(zero_ready, 1)
            for j in range(R0 // 4):
                sp.dma_start(tiles_of(rows0, NT + 4 * j, 4), OUTS).then_inc(zero_filled, 16)
            for j in range(R1 // 4):
                sp.dma_start(tiles_of(rows1, NT + 4 * j, 4), OUTS).then_inc(zero_filled, 16)
            sp.dma_start(W[:, 0:LATE0 * WIDTH0], moe0[:, 0:LATE0 * WIDTH0]).then_inc(w0_loaded, 16)
            sp.wait_ge(rows_copied, NT)
            sp.dma_start(tiles_of(rows0, 0, NT), H).then_inc(h_stored, 16)
            sp.wait_ge(s_ready, NT)
            sp.dma_start(W[:, LATE0 * WIDTH0:], moe0[:, LATE0 * WIDTH0:]).then_inc(w0_late, 16)

            def run_mixture(m, rows, outs, tiles, first_ready, routed_ready):
                def load(t, c):
                    if later(t, 4):
                        sp.wait_ge(m.turned, t - 2)
                    sp.dma_start(ROWS[:, c:c + 2, :], tiles_of(rows, t, 2)).then_inc(m.loaded[c // 2], 16)

                def store(t, c):
                    sp.wait_ge(m.outs, t + 2)
                    sp.dma_start(tiles_of(outs, t, 2), OUTS[:, c:c + 2, :]).then_inc(m.stored[c // 2], 16)

                first_ready()
                load(0, 0)
                load(2, 2)
                load(4, 0)
                load(6, 2)

                def four_tiles(b):
                    store(4 * b - 4, 0)
                    load(4 * b + 4, 0)
                    store(4 * b - 2, 2)
                    load(4 * b + 6, 2)

                with sp.Fori(1, NT // 4 - 1, 1) as b:
                    four_tiles(b)
                routed_ready()
                with sp.Fori(NT // 4 - 1, tiles // 4 - 1, 1) as b:
                    four_tiles(b)
                for t in (tiles - 8, tiles - 6, tiles - 4, tiles - 2):
                    store(t, t % 4)

            def combine(c, outs):
                for i in range(0, 2):
                    sp.dma_start(GOT[:, i, 0, :], outs[i * P:(i + 1) * P, :]).then_inc(c.shared[i], 16)
                with sp.Fori(1, NT // 2, 1) as b:
                    for i in range(2):
                        sp.wait_ge(c.acc, 2 * b + (i - 1))
                        sp.dma_start(GOT[:, i, 0, :], outs[bass.ds((2 * b + i) * P, P), :]).then_inc(c.shared[i], 16)

            def first0():
                sp.wait_ge(h_stored, 16)

            def routed0():
                sp.wait_ge(zero_filled, 16 * (R0 + R1) // 4)
                sp.wait_ge(r0.scattered, 16 * NT * K0)
                sp.wait_ge(h_stored, 16)

            run_mixture(m0, rows0, outs0, TILES0, first0, routed0)

            sp.wait_ge(m0.down, TILES0)
            sp.dma_start(W[:, 0:SLOTS1 * WIDTH1], moe1).then_inc(w1_loaded, 16)
            sp.dma_start(W_DT, w_dt).then_inc(small1_loaded, 16)
            sp.dma_start(W_XP, w_xproj).then_inc(small1_loaded, 16)
            sp.dma_start(WR, wr).then_inc(small1_loaded, 16)
            sp.dma_start(A_NEG, per_channel[:, 2 * KD:].rearrange("p (k n) -> p k n", k=KD)).then_inc(small1_loaded, 16)
            sp.dma_start(B_DT, per_channel[:, 0:KD]).then_inc(small1_loaded, 16)
            sp.dma_start(D_SKIP, per_channel[:, KD:2 * KD]).then_inc(small1_loaded, 16)
            for i in range(2):
                sp.wait_ge(m0.stored[i], 4 * TILES0)
            combine(c0, outs0)
            sp.wait_ge(c0.xn, NT)
            sp.dma_start(tiles_of(rows1, 0, NT), XN1).then_inc(xn1_stored, 16)

            def first1():
                sp.wait_ge(xn1_stored, 16)

            def routed1():
                sp.wait_ge(r1.scattered, 16 * NT * K1)

            run_mixture(m1, rows1, outs1, TILES1, first1, routed1)
            sp.wait_ge(y_added, UNITS)
            for i in range(2):
                sp.wait_ge(m1.stored[i], 4 * TILES1)
            combine(c1, outs1)
            for g in range(4):
                sp.wait_ge(c1.x, 4 * g + 4)
                sp.dma_start(out[:, 4 * g:4 * g + 4, :], X[:, 4 * g:4 * g + 4, :]).then_inc(out_stored, 16)
            sp.wait_ge(out_stored, 64)

        @block.gpsimd
        def _(pool):
            pool.memset(OUTS, 0.0).then_inc(zero_ready, 1)
            pool.memset(IDENT, 0.0)
            pool.memset(BLOCKS, 0.5)
            pool.memset(BELOW, 0.0)
            pool.memset(ONES, 1.0)
            pool.memset(EPS_COL, EPS_LN)
            pool.memset(EXPERT[0:1, :], 0)
            pool.memset(PICK, 0.0).then_inc(consts_cleared, 1)
            pool.wait_ge(consts_cleared, 1)
            pool.affine_select(out=IDENT, in_=IDENT, compare_op=ALU.not_equal, fill=1.0, base=0,
                               pattern=[[-1, P]], channel_multiplier=1)
            pool.affine_select(out=BELOW, in_=BELOW, compare_op=ALU.is_ge, fill=1.0, base=0,
                               pattern=[[-1, P]], channel_multiplier=1)
            v = BLOCKS.rearrange("p (b j) -> p b j", j=HEAD)
            pool.affine_select(out=v, in_=v, compare_op=ALU.is_ge, fill=0.0, base=0,
                               pattern=[[-HEAD, P // HEAD], [0, HEAD]], channel_multiplier=1).then_inc(consts_cleared, 1)
            pool.wait_ge(consts_cleared, 2)
            for q in range(3):
                w = PICK[32 * q:32 * q + 32, :]
                pool.affine_select(out=w, in_=w, compare_op=ALU.not_equal, fill=1.0, base=0,
                                   pattern=[[-1, 2 * N_STATE]], channel_multiplier=1).then_inc(consts_cleared, 1)
                pool.wait_ge(consts_cleared, 3 + q)
            pool.affine_select(out=v, in_=v, compare_op=ALU.is_ge, fill=0.0, base=HEAD - 1,
                               pattern=[[HEAD, P // HEAD], [0, HEAD]], channel_multiplier=-1)
            pool.iota(IOTA_E, pattern=[[1, E0]], base=0, channel_multiplier=0, allow_small_or_imprecise_dtypes=True)
            pool.iota(IOTA_T, pattern=[[1, R0]], base=0, channel_multiplier=0, allow_small_or_imprecise_dtypes=True)
            pool.iota(STEPS, pattern=[[P, NT]], base=0, channel_multiplier=0,
                      allow_small_or_imprecise_dtypes=True).then_inc(consts_ready, 1)

            def keep_h(t, c):
                pool.wait_ge(h_ready, t + 1)
                pool.wait_ge(consts_ready, 1)
                pool.tensor_copy(H[:, bass.ds(t, 1), :], H_S[:, c:c + 1, :]).then_inc(rows_copied, 1)

            pipeline(pool, NT, 2, (0, keep_h))

            def scatter(src, rows, choices, tiles, done):
                for t in range(NT):
                    for k in range(choices):
                        pool.indirect_dma_start(
                            out=rows, out_offset=bass.IndirectOffsetOnAxis(ap=SLOT_IN[:, k, t:t + 1], axis=0),
                            in_=src[:, t, :], in_offset=None,
                            bounds_check=tiles * P - 1, oob_is_err=False).then_inc(done, 16)

            pool.wait_ge(r0.slots, 1)
            pool.wait_ge(zero_filled, 16 * (R0 + R1) // 4)
            pool.wait_ge(rows_copied, NT)
            scatter(H, rows0, K0, TILES0, r0.scattered)

            def gather(c, outs, choices):
              for t in range(NT):
                i = t % 2
                if t >= 2:
                    pool.wait_ge(c.acc, t - 1)
                for k in range(choices):
                    pool.indirect_dma_start(
                        out=GOT[:, i, 1 + k, :], out_offset=None, in_=outs,
                        in_offset=bass.IndirectOffsetOnAxis(ap=SLOT_OUT[:, k, t:t + 1], axis=0)).then_inc(c.got[i], 16)

            for i in range(2):
                pool.wait_ge(m0.stored[i], 4 * TILES0)
            gather(c0, outs0, K0)

            pool.wait_ge(r1.slots, 1)
            pool.wait_ge(c0.xn, NT)
            scatter(XN1, rows1, K1, TILES1, r1.scattered)

            def times_c(u, c):
                pool.wait_ge(scanned, u + 1)
                pool.wait_ge(c_copied, u + 2 - c % 2)
                pool.tensor_tensor(Z[:, c % 2, :], Z[:, c % 2, :], C_SB[:, c // 2, :], ALU.mult).then_inc(hc_ready, 1)

            pipeline(pool, UNITS, 4, (0, times_c))
            pool.wait_ge(y_added, UNITS)
            for i in range(2):
                pool.wait_ge(m1.stored[i], 4 * TILES1)
            gather(c1, outs1, K1)

        def mixture_scalar(act, m, hidden, blocks, part):
            bank = MIX_BANKS[m is m1]

            def copy_rows_t(t, c):
                act.wait_ge(m.turned, t + 1)
                if later(t, 2):
                    act.wait_ge(m.hidden, t - 1)
                act.copy(ROWS_T[:, c % 2, :], PS[:, bank["rows"][c % 2], 0:D]).then_inc(m.rows_t, 1)

            def tanh(t, c):
                act.wait_ge(m.hidden, t + 1)
                if later(t, 2):
                    act.wait_ge(m.hid_turned, t - 1)
                act.activation(HID[:, c % 2, 0:hidden], PS[:, bank["up"][c % 2], 0:hidden], ACT.Tanh,
                               scale=0.5).then_inc(m.tanh, 1)

            def copy_hid_t(t, c):
                act.wait_ge(m.hid_turned, t + 1)
                if later(t, 2):
                    act.wait_ge(m.down, t - 1)
                act.copy(HID_T[0:part, c % 2, 0:blocks * P], PS[0:part, bank["hid"], 0:blocks * P]).then_inc(m.hid_t, 1)

            return copy_rows_t, tanh, copy_hid_t

        @block.scalar
        def _(act):
            def save_t(t, c):
                act.wait_ge(turned0, t + 1)
                if later(t, 2):
                    act.wait_ge(logits0, t - 1)
                act.copy(HT_S[:, c, :], PS[:, c, D:2 * D])
                act.copy(XT[:, :, bass.ds(t * P, P)],
                         PS[:, c, 0:D].rearrange("p (k n) -> p k n", k=KD)).then_inc(evac0, 1)

            pipeline(act, NT, 2, (0, save_t))

            def softmax(r, top, choices):
                act.wait_ge(r.diff, 1)
                act.activation(WEIGHT[:, :, 0:choices], WEIGHT[:, :, 0:choices], ACT.Exp).then_inc(r.exps, 1)

            softmax(r0, TOP, K0)

            def stage_xt(t, c):
                if later(t, 2):
                    act.wait_ge(qvu_ready, t - 1)
                act.wait_ge(evac0, NT)
                act.copy(XT_S[:, c, :].rearrange("p (k n) -> p k n", k=KD),
                         XT[:, :, bass.ds(t * P, P)]).then_inc(xt_staged, 1)

            def tables(t, c):
                act.wait_ge(pre_ready, t + 1)
                if later(t, 2):
                    act.wait_ge(qv_ready, t - 1)
                act.activation(TH[:, c, :], PRE[:, c, D:3 * D], ACT.Tanh, scale=0.5)
                act.activation(ELU[:, c, :], ELU[:, c, :], ACT.Exp).then_inc(th_ready, 1)

            def save_qt(t, c):
                act.wait_ge(q_turned, t + 1)
                act.wait_ge(xt_staged, t + 1)
                act.wait_ge(evac0, NT)
                act.copy(XT[:, :, bass.ds(t * P, P)],
                         PS[:, 6 + c, 0:D].rearrange("p (k n) -> p k n", k=KD)).then_inc(qt_saved, 1)

            pipeline(act, NT, 2, (2, stage_xt), (0, tables), (-1, save_qt))

            def stage_qt(t, c):
                if later(t, 2):
                    act.wait_ge(o_ready, t - 1)
                act.wait_ge(qt_saved, NT)
                act.copy(QT_S[:, c, :].rearrange("p (k n) -> p k n", k=KD),
                         XT[:, :, bass.ds(t * P, P)]).then_inc(qt_staged, 1)

            def copy_zt(t, c):
                act.wait_ge(z_turned, t + 1)
                if later(t, 2):
                    act.wait_ge(wo_done, t - 1)
                act.copy(ZT_S[:, c, :], PS[:, 2 + c, 0:D]).then_inc(zt_ready, 1)

            def deviation(t, c):
                act.wait_ge(o_stats, t + 1)
                act.activation(STAT[:, 2 + c, 2:3], STAT[:, 2 + c, 1:2], ACT.Sqrt, bias=EPS_COL).then_inc(o_dev, 1)

            pipeline(act, NT, 2, (2, stage_qt), (1, deviation), (0, copy_zt))

            rows_t, tanh, hid_t = mixture_scalar(act, m0, I0, 1, P)
            pipeline(act, TILES0, UNROLL, (2, rows_t), (1, tanh), (0, hid_t))

            def tanh_acc(cm, t, i):
                act.wait_ge(cm.acc, t + 1)
                if later(t, 2):
                    act.wait_ge(cm.x, t - 1)
                act.activation(TANH[:, i, :], ACC[:, i, :], ACT.Tanh, scale=0.5).then_inc(cm.tanh, 1)

            def save_xt1(t, i):
                act.wait_ge(c0.turned, t + 1)
                if later(t, 2):
                    act.wait_ge(c0.logits, t - 1)
                act.copy(XT1_S[:, i, :], PS[:, i, 0:D])
                act.copy(XT[:, :, bass.ds(t * P, P)],
                         PS[:, i, 0:D].rearrange("p (k n) -> p k n", k=KD)).then_inc(c0.xt, 1)

            pipeline(act, NT, 4, (0, lambda t, c: tanh_acc(c0, t, c % 2)), (-4, lambda t, c: save_xt1(t, c % 2)))

            act.wait_ge(small1_loaded, 96)
            act.activation(A_NEG, A_NEG, ACT.Exp).then_inc(a_exp, 1)
            softmax(r1, TOP1, K1)
            for j in range(4):
                act.wait_ge(xz_ready, j + 1)
                act.wait_ge(r1.slots, 1)
                act.copy(DELTA_R[:, 512 * j:512 * j + 512], PS[:, j % 2, :])
                act.copy(BC[0:96, 512 * j:512 * j + 512], PS[0:96, 2 + j % 2, :]).then_inc(dr_ready, 1)
            for k in range(KD):
                for j in range(4):
                    n = 4 * k + j
                    act.wait_ge(dl_max, n + 1)
                    part = DU[:, k, 512 * j:512 * j + 512]
                    act.activation(part, PS[:, 4 + n % 4, :], ACT.Abs, bias=B_DT[:, k:k + 1]).then_inc(act_step, 1)
                    act.wait_ge(act_step, n + 1)
                    act.activation(part, part, ACT.Exp, scale=-1.0).then_inc(dl_exp, 1)
            act.wait_ge(dl_step, KD)
            for k in range(KD):
                act.activation(DU[:, k, :], DU[:, k, :], ACT.Ln).then_inc(dl_ln, 1)

            def copy_c(u, c):
                act.wait_ge(c_spread, u + 1)
                if later(u, 4):
                    act.wait_ge(hc_ready, u - c % 2 - 2)
                h = 512 * (c % 2)
                act.copy(C_SB[:, c // 2, h:h + 512], PS[:, C_BANK, :]).then_inc(c_copied, 1)

            def decay(u, c):
                act.wait_ge(a_ready, 1)
                act.wait_ge(du_ready, 1)
                if later(u, 2):
                    act.wait_ge(scanned, u - 1)
                n = (u - c) // 4
                act.activation(DA[:, c % 2, :], DELTA[:, c % 2, (c // 2) * SEQ:(c // 2 + 1) * SEQ], ACT.Exp,
                               scale=A_NEG[:, c % 2, bass.ds(n, 1)]).then_inc(da_ready, 1)

            rows_t, tanh, hid_t = mixture_scalar(act, m1, H1P, 3, HB)
            pipeline(act, TILES1, UNROLL, (2, rows_t), (1, tanh), (0, hid_t), (2, copy_c), (1, decay))
            for u in range(TILES1, UNITS):
                copy_c(u, u % 4)
                decay(u, u % 4)

            def stage_y(t, i):
                if later(t, 2):
                    act.wait_ge(c1.y_rows, t - 1)
                act.wait_ge(y_added, UNITS)
                act.copy(XT1_S[:, i, :].rearrange("p (k n) -> p k n", k=KD),
                         XT[:, :, bass.ds(t * P, P)]).then_inc(c1.y_staged, 1)

            pipeline(act, NT, 2, (1, stage_y), (0, lambda t, i: tanh_acc(c1, t, i)))

        def mixture_vector(dve, m, up, scale_cols):
            bank = MIX_BANKS[m is m1]

            def gate(t, c):
                dve.wait_ge(m.tanh, t + 1)
                hid = HID[:, c % 2, 0:scale_cols]
                dve.scalar_tensor_tensor(out=hid, in0=hid, scalar=1.0, in1=PS[:, bank["up"][c % 2], 0:scale_cols],
                                         op0=ALU.add, op1=ALU.mult).then_inc(m.half, 1)
                dve.wait_ge(m.half, t + 1)
                dve.tensor_tensor(hid, hid, up(c), ALU.mult).then_inc(m.gated, 1)

            def copy_outs(t, c):
                dve.wait_ge(m.down, t + 1)
                if later(t, 4):
                    dve.wait_ge(m.stored[c // 2], 4 * t - 4 * c)
                dve.tensor_copy(OUTS[:, c, :], PS[:, bank["outs"][c % 2], 0:D]).then_inc(m.outs, 1)

            return gate, copy_outs

        @block.vector
        def _(dve):
            steps = [0]

            def link(ins):
                steps[0] += 1
                ins.then_inc(v_step, 1)
                dve.wait_ge(v_step, steps[0])

            dve.wait_ge(x_loaded, 16)
            dve.wait_ge(small_loaded, 32)

            def chain(sem, start):
                n = [0]

                def then(ins):
                    n[0] += 1
                    ins.then_inc(sem, 1)
                    dve.wait_ge(consts_ready, 1)
                    dve.wait_ge(sem, start + n[0])
                return then, n

            def rsqrt(then, y, v, tmp):
                then(dve.tensor_scalar(y.bitcast(I32), v.bitcast(I32), 1, None, ALU.logical_shift_right))
                then(dve.tensor_scalar(y.bitcast(I32), y.bitcast(I32), -1.0, float(0x5f3759df), ALU.mult, ALU.add))
                for _ in range(3):
                    then(dve.tensor_tensor(tmp, y, y, ALU.mult))
                    then(dve.tensor_tensor(tmp, tmp, v, ALU.mult))
                    then(dve.tensor_scalar(tmp, tmp, -0.5, 1.5, ALU.mult, ALU.add))
                    then(dve.tensor_tensor(y, y, tmp, ALU.mult))

            def move(out, src):
                return dve.tensor_scalar(out, src, 1.0, None, ALU.mult)

            NORM_STEPS = 19

            def norms(g, c):
                four = bass.ds(4 * g, 4)
                then, n = chain(st_c, NORM_STEPS * g)
                for j in range(4):
                    dve.bn_stats(STAT[:, j, :], X[:, 4 * g + j, :]).then_inc(st_a, 1)
                dve.wait_ge(consts_ready, 1)
                dve.wait_ge(st_a, 4 * g + 4)
                for j in range(4):
                    dve.bn_aggr(AGGR[:, j, :], STAT[:, j, :]).then_inc(st_b, 1)
                dve.wait_ge(st_b, 4 * g + 4)
                move(MEAN_VAR[:, four, :], AGGR)
                var = AGGR[:, :, 1]
                then(dve.tensor_scalar(VARS[:, 0, :], var, EPS_LN, None, ALU.add))
                then(dve.reciprocal(PRODS[:, 0, :], VARS[:, 0, :]))
                then(dve.tensor_tensor(VARS[:, 1, :], PRODS[:, 0, :], var, ALU.mult))
                then(dve.tensor_scalar(VARS[:, 1, :], VARS[:, 1, :], EPS_RMS, None, ALU.add))
                rsqrt(then, ROOTS, VARS, PRODS)
                move(RSTD[:, four], ROOTS[:, 0, :])
                then(move(RRMS[:, four], ROOTS[:, 1, :]))
                assert n[0] == NORM_STEPS
                for j in range(4):
                    t = 4 * g + j
                    if later(t, 2):
                        dve.wait_ge(turned0, t - 1)
                        dve.wait_ge(rows_copied, t - 1)
                    dve.tensor_scalar(XN_S[:, j % 2, :], X[:, t, :], MEAN_VAR[:, t, 0:1], RSTD[:, bass.ds(t, 1)],
                                      ALU.subtract, ALU.mult).then_inc(xn_s_done, 1)
                    dve.wait_ge(xn_s_done, t + 1)
                    dve.scalar_tensor_tensor(out=H_S[:, j % 2, :], in0=XN_S[:, j % 2, :], scalar=RRMS[:, bass.ds(t, 1)],
                                             in1=NORM_W, op0=ALU.mult, op1=ALU.mult).then_inc(h_ready, 1)

            for g in range(NT // 4):
                norms(g, 0)

            def routing(r, logits, logits_ready, experts, choices, cap, routed, top, top_id, top_idf, small, area,
                        rank, count):
                dve.wait_ge(logits_ready, NT)

                def pick(t):
                    dve.max(top[:, t, :], logits[:, t * experts:(t + 1) * experts]).then_inc(r.top, 1)
                    dve.wait_ge(r.top, t + 1)
                    dve.max_index(top_id[:, t, :], top[:, t, :],
                                  logits[:, t * experts:(t + 1) * experts]).then_inc(r.top_id, 1)

                for t in range(NT):
                    pick(t)
                dve.wait_ge(r.top_id, NT)
                a = Area(*area)
                chosen = a.take(choices, NT, experts)
                slot = a.take(NT, experts)
                cut = a.take(NT, experts)
                mask = cut.rearrange("p t e -> p (t e)")[:, 0:NT * experts // 2].bitcast(BF16)
                w = WEIGHT[:, :, 0:choices]
                dve.tensor_tensor(w, top[:, :, 0:choices], top[:, :, 0:1].broadcast_to([P, NT, choices]),
                                  ALU.subtract).then_inc(r.diff, 1)
                link(dve.tensor_copy(top_idf, top_id))
                for k in range(choices):
                    last = dve.tensor_tensor(chosen[:, k, :, :], IOTA_E[:, None, 0:experts].broadcast_to([P, NT, experts]),
                                             top_idf[:, :, k:k + 1].broadcast_to([P, NT, experts]), ALU.is_equal)
                link(last)
                mask3 = mask.rearrange("p (t e) -> p t e", e=experts)
                if choices == 4:
                    dve.tensor_tensor(slot, chosen[:, 0, :, :], chosen[:, 1, :, :], ALU.add)
                    last = dve.tensor_tensor(cut, chosen[:, 2, :, :], chosen[:, 3, :, :], ALU.add)
                    link(last)
                    link(dve.tensor_tensor(slot, slot, cut, ALU.add))
                    dve.tensor_copy(mask3, slot).then_inc(r.mask, 1)
                else:
                    dve.tensor_tensor(mask3, chosen[:, 0, :, :], chosen[:, 1, :, :], ALU.add).then_inc(r.mask, 1)
                dve.wait_ge(r.exps, 1)
                total = small[:, 0, 0:NT] if experts >= NT else TOTAL
                link(dve.tensor_reduce(total, w, AX_X, ALU.add))
                link(dve.reciprocal(total, total))
                link(dve.tensor_scalar(total, total, 0.5, None, ALU.mult))
                link(dve.tensor_tensor(w, w, total[:, :, None].broadcast_to([P, NT, choices]), ALU.mult))
                dve.wait_ge(r.ranks, 1)
                counts, tiles, ends, start, ones = (small[:, i, :] for i in range(5))
                most = cap // P
                link(dve.tensor_scalar(counts, count, float(cap), None, ALU.min))
                above = slot.rearrange("p t e -> p (t e)")[:, 0:experts * most].rearrange("p (e m) -> p e m", m=most)
                link(dve.tensor_tensor(above, counts[:, :, None].broadcast_to([P, experts, most]),
                                       STEPS[:, None, 0:most].broadcast_to([P, experts, most]), ALU.is_gt))
                link(dve.tensor_reduce(tiles, above, AX_X, ALU.add))
                link(dve.memset(ones, 1.0))
                link(dve.tensor_tensor_scan(ends, ones, tiles, 0.0, ALU.mult, ALU.add))
                link(dve.tensor_tensor(start, ends, tiles, ALU.subtract))
                link(dve.tensor_scalar(start, start, float(P), float(TOK), ALU.mult, ALU.add))
                rank3 = rank.rearrange("p (t e) -> p t e", e=experts)
                if cap < TOK:
                    link(dve.tensor_scalar(cut, rank3, float(cap - 1), DROPPED, ALU.is_gt, ALU.mult))
                    link(dve.scalar_tensor_tensor(out=slot, in0=rank3, scalar=float(cap - 1), in1=cut,
                                                  op0=ALU.min, op1=ALU.add))
                    link(dve.tensor_tensor(slot, slot, start[:, None, :].broadcast_to([P, NT, experts]), ALU.add))
                else:
                    link(dve.tensor_tensor(slot, rank3, start[:, None, :].broadcast_to([P, NT, experts]), ALU.add))
                for k in range(choices):
                    last = dve.tensor_tensor(chosen[:, k, :, :], chosen[:, k, :, :], slot, ALU.mult)
                link(last)
                flat = slot.rearrange("p t e -> p (t e)")
                mine = flat[:, 0:choices * NT].rearrange("p (k t) -> p k t", k=choices)
                over = cut.rearrange("p t e -> p (t e)")[:, 0:choices * NT].rearrange("p (k t) -> p k t", k=choices)
                link(dve.tensor_reduce(mine, chosen, AX_X, ALU.add))
                if cap < TOK:
                    dve.tensor_scalar(over, mine, DROPPED, -DROPPED, ALU.is_ge, ALU.mult)
                    link(dve.tensor_copy(SLOT_IN[:, 0:choices, :], mine))
                    link(dve.tensor_tensor(mine, mine, over, ALU.add))
                    link(dve.tensor_copy(SLOT_OUT[:, 0:choices, :], mine))
                else:
                    dve.tensor_copy(SLOT_IN[:, 0:choices, :], mine)
                    link(dve.tensor_copy(SLOT_OUT[:, 0:choices, :], mine))
                b = Area(*area)
                past = b.take(routed, experts)[0:1, :, :]
                dve.tensor_tensor(past, IOTA_T[0:1, 0:routed, None].broadcast_to([1, routed, experts]),
                                  ends[0:1, None, :].broadcast_to([1, routed, experts]), ALU.is_ge).then_inc(r.slots, 1)
                dve.wait_ge(r.slots, 1)
                which = b.take(routed)[0:1, :]
                link(dve.tensor_reduce(which, past, AX_X, ALU.add))
                link(dve.tensor_scalar(which, which, float(experts - 1), 1.0, ALU.min, ALU.add))
                dve.tensor_copy(EXPERT[0:1, NT:NT + routed], which).then_inc(r.experts, 1)

            dve.wait_ge(consts_ready, 1)
            routing(r0, PS[:, 7, :], logits0, E0, K0, CAP0, R0, TOP, TOP_ID, TOP_IDF, SMALL, (W, RT0),
                    PS[:, 6, :], PS[:, 5, 0:E0])

            dve.wait_ge(attn_w_loaded, 48)
            dve.wait_ge(r0.experts, 1)

            def bias_qvu(t, c):
                dve.wait_ge(qvu_ready, t + 1)
                if later(t, 2):
                    dve.wait_ge(qv_ready, t - 1)
                for lo, hi, bank in ((0, 2 * D, 0), (2 * D, 3 * D, 1)):
                    last = dve.tensor_tensor(PRE[:, c, lo:hi], PS[:, 2 * c + bank, 0:hi - lo], B_QVU[:, lo:hi], ALU.add)
                last.then_inc(pre_done, 1)
                dve.wait_ge(pre_done, t + 1)
                dve.tensor_scalar(ELU[:, c, :], PRE[:, c, 0:D], 0.0, None, ALU.min).then_inc(pre_ready, 1)

            def make_qvu(t, c):
                dve.wait_ge(th_ready, t + 1)
                if later(t, 2):
                    dve.wait_ge(kv_added, t - 1)
                dve.scalar_tensor_tensor(out=Q_S[:, c, :], in0=PRE[:, c, 0:D], scalar=0.0, in1=ELU[:, c, :],
                                         op0=ALU.max, op1=ALU.add).then_inc(elu_step, 1)
                dve.scalar_tensor_tensor(out=V_S[:, c, :], in0=TH[:, c, 0:D], scalar=1.0, in1=PRE[:, c, D:2 * D],
                                         op0=ALU.add, op1=ALU.mult)
                dve.scalar_tensor_tensor(out=U[:, t, :], in0=TH[:, c, D:2 * D], scalar=1.0, in1=PRE[:, c, 2 * D:3 * D],
                                         op0=ALU.add, op1=ALU.mult)
                dve.wait_ge(elu_step, t + 1)
                dve.tensor_scalar(Q_S[:, c, :], Q_S[:, c, :], -1.0, None, ALU.add).then_inc(qv_ready, 1)
                if isinstance(t, int) and t % (NT // BATCH) == NT // BATCH - 1:
                    keep_heads(t // (NT // BATCH))

            def keep_heads(b):
                dve.wait_ge(kv_added, (b + 1) * NT // BATCH)
                for k in range(KD):
                    last = dve.tensor_tensor(KV[:, b * KD + k, :], PS[:, 4 + k, 0:P], BLOCKS, ALU.mult)
                last.then_inc(kv_ready, 1)

            half = NT // BATCH
            for b in range(BATCH):
                pipeline(dve, half, 2, (1, lambda t, c: bias_qvu(t + b * half, c)),
                         (0, lambda t, c: make_qvu(t + b * half, c)))

            def stats_o(t, c):
                dve.wait_ge(o_ready, t + 1)
                if later(t, 2):
                    dve.wait_ge(z_step, 4 * t - 4)
                dve.bn_stats(STAT[:, c, :], PS[:, c, 0:D]).then_inc(o_sums, 1)
                dve.wait_ge(consts_ready, 1)
                dve.wait_ge(o_sums, t + 1)
                dve.bn_aggr(STAT[:, 2 + c, 0:2], STAT[:, c, :]).then_inc(o_stats, 1)

            def normed(t, c):
                dve.wait_ge(o_dev, t + 1)
                if later(t, 2):
                    dve.wait_ge(z_turned, t - 1)
                o = PS[:, c, 0:D]
                z = Z_S[:, c, :]
                then, n = chain(z_step, 4 * t)
                then(dve.reciprocal(STAT[:, 2 + c, 2:3], STAT[:, 2 + c, 2:3]))
                then(dve.tensor_scalar(z, o, STAT[:, 2 + c, 0:1], STAT[:, 2 + c, 2:3], ALU.subtract, ALU.mult))
                then(dve.tensor_tensor(z, z, LN_G, ALU.mult))
                then(dve.tensor_tensor(z, z, LN_B, ALU.add))
                dve.scalar_tensor_tensor(out=z, in0=z, scalar=0.5, in1=U[:, t, :], op0=ALU.mult, op1=ALU.mult)\
                    .then_inc(z_ready, 1)

            def make_s(t, c):
                dve.wait_ge(wo_done, t + 1)
                dve.wait_ge(z_ready, t + 1)
                dve.tensor_tensor(U[:, t, :], PS[:, 4 + c, 0:D], B_O, ALU.add).then_inc(s_ready, 1)

            pipeline(dve, NT, 2, (1, stats_o), (0, normed), (-1, make_s))

            dve.wait_ge(zero_filled, 16 * (R0 + R1) // 4)
            gate, copy_outs = mixture_vector(dve, m0, lambda c: PS[:, 1 + c % 2, I0:2 * I0], I0)
            pipeline(dve, TILES0, UNROLL, (1, gate), (-1, copy_outs))

            def sum_rows(cm, t, i, choices, base):
                if later(t, 2):
                    dve.wait_ge(cm.x, t - 1)
                dve.wait_ge(cm.shared[i], 8 * t - 8 * i + 16)
                base(t, i)
                for k in range(choices):
                    if k == 0:
                        dve.wait_ge(cm.got[i], 8 * choices * (t - i) + 16 * choices)
                    dve.wait_ge(cm.step, choices * t + 1 + k)
                    ins = dve.scalar_tensor_tensor(out=ACC[:, i, :], in0=GOT[:, i, 1 + k, :],
                                                   scalar=WEIGHT[:, t, k:k + 1], in1=ACC[:, i, :],
                                                   op0=ALU.mult, op1=ALU.add)
                    if k < choices - 1:
                        ins.then_inc(cm.step, 1)
                ins.then_inc(cm.acc, 1)

            xn_again = sem("xn_again")

            def base0(t, i):
                dve.tensor_scalar(ACC[:, i, :], X[:, t, :], MEAN_VAR[:, t, 0:1], RSTD[:, bass.ds(t, 1)],
                                  ALU.subtract, ALU.mult).then_inc(xn_again, 1)
                dve.wait_ge(xn_again, t + 1)
                dve.scalar_tensor_tensor(out=ACC[:, i, :], in0=GOT[:, i, 0, :], scalar=0.5, in1=ACC[:, i, :],
                                         op0=ALU.mult, op1=ALU.add).then_inc(c0.step, 1)

            def base1(t, i):
                dve.tensor_scalar(ACC[:, i, :], GOT[:, i, 0, :], 0.5, None, ALU.mult).then_inc(c1.step, 1)

            gated, sg_done = sem("gated"), sem("sg_done")

            def new_x(cm, t, i, s, gated, sg_done):
                dve.wait_ge(cm.tanh, t + 1)
                dve.scalar_tensor_tensor(out=TANH[:, i, :], in0=TANH[:, i, :], scalar=1.0, in1=ACC[:, i, :],
                                         op0=ALU.add, op1=ALU.mult).then_inc(gated, 1)
                dve.wait_ge(gated, t + 1)
                s(t, i).then_inc(sg_done, 1)
                dve.wait_ge(sg_done, t + 1)
                dve.scalar_tensor_tensor(out=X[:, t, :], in0=TANH[:, i, :], scalar=0.5, in1=X[:, t, :],
                                         op0=ALU.mult, op1=ALU.add).then_inc(cm.x, 1)

            xn1_made, n1, n1_sums = sem("xn1_made"), sem("n1"), sem("n1_sums")
            GROUP_STEPS = 1 + 1 + 14 + 1

            def norm1(t, i):
                if i % 4 != 3:
                    return
                first = t - 3
                then, n = chain(n1, first // 4 * GROUP_STEPS)
                dve.wait_ge(consts_ready, 1)
                dve.wait_ge(c0.x, t + 1)
                for j in range(4):
                    last = dve.bn_stats(STAT[:, j, :], X[:, first + j, :])
                last.then_inc(n1_sums, 4)
                dve.wait_ge(consts_ready, 1)
                dve.wait_ge(n1_sums, t + 1)
                for j in range(4):
                    last = dve.bn_aggr(AGGR[:, j, :], STAT[:, j, :])
                then(last)
                move(MEAN_VAR[:, bass.ds(first, 4), :], AGGR)
                then(dve.tensor_scalar(VARS[:, 0, :], AGGR[:, :, 1], EPS_LN, None, ALU.add))
                rsqrt(then, ROOTS[:, 0, :], VARS[:, 0, :], PRODS[:, 0, :])
                then(move(RSTD[:, bass.ds(first, 4)], ROOTS[:, 0, :]))
                assert n[0] == GROUP_STEPS
                for j in range(4):
                    u = first + j
                    if later(u, 2):
                        dve.wait_ge(c0.turned, u - 1)
                    dve.tensor_scalar(XN1_S[:, j % 2, :], X[:, u, :], MEAN_VAR[:, u, 0:1], RSTD[:, bass.ds(u, 1)],
                                      ALU.subtract, ALU.mult).then_inc(xn1_made, 1)
                    dve.wait_ge(xn1_made, u + 1)
                    move(XN1[:, u, :], XN1_S[:, j % 2, :]).then_inc(c0.xn, 1)

            pipeline(dve, NT, 4, (1, lambda t, c: sum_rows(c0, t, c % 2, K0, base0)),
                     (0, lambda t, c: new_x(c0, t, c % 2, lambda t, i: dve.tensor_tensor(
                         TANH[:, i, :], TANH[:, i, :], U[:, t, :], ALU.mult), gated, sg_done)),
                     (0, norm1))

            dve.wait_ge(a_exp, 1)
            dve.tensor_scalar(A_NEG, A_NEG, -1.0, None, ALU.mult).then_inc(a_ready, 1)
            routing(r1, PS[:, 7, :], c0.logits, E1, K1, TOK, R1, TOP1, TOP1_ID, TOP1_IDF, SMALL1, (R, RT1),
                    PS[:, 6, 0:NT * E1], PS[:, 5, 0:E1])

            for q in range(3):
                if q == 0:
                    dve.wait_ge(dr_ready, 4)
                link(dve.tensor_copy(BC_HI[0:96, :], BC[0:96, :]))
                part = BC3[32 * q:32 * q + 32, :]
                ins = dve.tensor_copy(part, BC_HI[32 * q:32 * q + 32, :])
                if q < 2:
                    link(dve.tensor_tensor(BC[0:96, :], BC[0:96, :], BC_HI[0:96, :], ALU.subtract))
                else:
                    ins.then_inc(bc3_ready, 1)
            for k in range(KD):
                for j in range(4):
                    n = 4 * k + j
                    dve.wait_ge(dl_psum, n + 1)
                    dve.tensor_scalar(DELTA[:, k, 512 * j:512 * j + 512], PS[:, 4 + n % 4, :], B_DT[:, k:k + 1], 0.0,
                                      ALU.add, ALU.max).then_inc(dl_max, 1)
            for k in range(KD):
                dve.wait_ge(dl_exp, 4 * (k + 1))
                dve.tensor_scalar(DU[:, k, :], DU[:, k, :], 1.0, None, ALU.add).then_inc(dl_step, 1)
            for k in range(KD):
                dve.wait_ge(dl_ln, k + 1)
                link(dve.tensor_tensor(DELTA[:, k, :], DELTA[:, k, :], DU[:, k, :], ALU.add))
                link(dve.tensor_tensor(DU[:, k, :], DELTA[:, k, :], XT[:, k, :], ALU.mult))
                ins = dve.tensor_scalar(XT[:, k, :], XT[:, k, :], D_SKIP[:, k:k + 1], None, ALU.mult)
            ins.then_inc(du_ready, 1)
            dve.wait_ge(du_ready, 1)

            def input_b(u, c):
                dve.wait_ge(b_spread, u + 2 - c % 2)
                if later(u, 2):
                    dve.wait_ge(y_added, u - 1)
                lo = (c // 2) * SEQ
                dve.tensor_tensor(Z[:, c % 2, :].rearrange("p (a b) -> p a b", a=2),
                                  DU[:, c % 2, lo:lo + SEQ].rearrange("p (a b) -> p a b", a=2),
                                  PS[:, B_BANK:B_BANK + 2, :], ALU.mult).then_inc(bu_ready, 1)

            def scan(u, c):
                dve.wait_ge(da_ready, u + 1)
                dve.wait_ge(bu_ready, u + 1)
                dve.tensor_tensor_scan(Z[:, c % 2, :], DA[:, c % 2, :], Z[:, c % 2, :], 0.0,
                                       ALU.mult, ALU.add).then_inc(scanned, 1)

            def add_y(u, c):
                dve.wait_ge(hc_ready, u + 1)
                if later(u, 2):
                    dve.wait_ge(y_added, u - 2)
                y = XT[:, c % 2, (c // 2) * SEQ:(c // 2 + 1) * SEQ]
                dve.tensor_tensor(y, y, Z[:, c % 2, :], ALU.add).then_inc(y_added, 1)

            gate, copy_outs = mixture_vector(dve, m1, lambda c: PS[:, 2, 0:H1P], H1P)
            pipeline(dve, TILES1, UNROLL, (-2, add_y), (0, input_b), (0, scan), (1, gate), (-1, copy_outs))
            for u in range(TILES1, UNITS + 2):
                if u - 2 >= TILES1:
                    add_y(u - 2, (u - 2) % 4)
                if u < UNITS:
                    input_b(u, u % 4)
                    scan(u, u % 4)

            gated1, sg1_done = sem("gated1"), sem("sg1_done")

            def s1(t, i):
                dve.wait_ge(c1.y_rows, t + 1)
                return dve.tensor_tensor(TANH[:, i, :], TANH[:, i, :], PS[:, i, 0:D], ALU.mult)

            pipeline(dve, NT, 2, (1, lambda t, i: sum_rows(c1, t, i, K1, base1)),
                     (0, lambda t, i: new_x(c1, t, i, s1, gated1, sg1_done)))

        def mixture_tensor(pe, m, hidden, blocks, part, width, banks):
            bank = MIX_BANKS[m is m1]
            two = 2 if m is m0 else 1

            def turn(t, c):
                pe.wait_ge(m.loaded[c // 2], 4 * t - 4 * c + 16)
                if later(t, two):
                    pe.wait_ge(m.rows_t, t + 1 - two)
                for k in range(KD):
                    last = pe.transpose(PS[:, bank["rows"][c % 2], k * P:(k + 1) * P], ROWS[:, c, k * P:(k + 1) * P], IDENT)
                last.then_inc(m.turned, 1)

            slots = SLOTS0 if m is m0 else SLOTS1

            def up(t, c):
                e = pe.value_load(EXPERT[0:1, bass.ds(t, 1)], min_val=0, max_val=slots - 1)
                pe.wait_ge(m.rows_t, t + 1)
                if m is m0:
                    if later(t, 2):
                        pe.wait_ge(m.gated, t - 1)
                    for k in range(KD):
                        last = pe.matmul(PS[:, 1 + c % 2, 0:2 * hidden], ROWS_T[:, c % 2, k * P:(k + 1) * P],
                                         W[:, bass.ds(e * width + 2 * k * hidden, 2 * hidden)], start=(k == 0), stop=(k == KD - 1))
                else:
                    if later(t, 1):
                        pe.wait_ge(m.gated, t)
                    for half in range(2):
                        for k in range(KD):
                            last = pe.matmul(PS[:, 1 + half, 0:hidden], ROWS_T[:, c % 2, k * P:(k + 1) * P],
                                             W[:, bass.ds(e * width + (2 * k + half) * hidden, hidden)],
                                             start=(k == 0), stop=(k == KD - 1))
                last.then_inc(m.hidden, 1)

            def turn_hidden(t, c):
                pe.wait_ge(m.gated, t + 1)
                if later(t, 1):
                    pe.wait_ge(m.hid_t, t)
                for k in range(blocks):
                    last = pe.transpose(PS[0:part, bank["hid"], k * P:(k + 1) * P], HID[:, c % 2, k * part:(k + 1) * part], IDENT)
                last.then_inc(m.hid_turned, 1)

            def down(t, c):
                e = pe.value_load(EXPERT[0:1, bass.ds(t, 1)], min_val=0, max_val=slots - 1)
                pe.wait_ge(m.hid_t, t + 1)
                if later(t, two):
                    pe.wait_ge(m.outs, t + 1 - two)
                for k in range(blocks):
                    last = pe.matmul(PS[:, bank["outs"][c % 2], 0:D], HID_T[0:part, c % 2, k * P:(k + 1) * P],
                                     W[0:part, bass.ds(e * width + KD * 2 * hidden + k * D, D)],
                                     start=(k == 0), stop=(k == blocks - 1))
                last.then_inc(m.down, 1)

            return turn, up, turn_hidden, down

        @block.tensor
        def _(pe):
            pe.wait_ge(consts_ready, 1)

            def turn0(t, c):
                pe.wait_ge(h_ready, t + 1)
                if later(t, 2):
                    pe.wait_ge(evac0, t - 1)
                for i, rows in enumerate((XN_S, H_S)):
                    for k in range(KD):
                        last = pe.transpose(PS[:, c, i * D + k * P:i * D + (k + 1) * P],
                                            rows[:, c, k * P:(k + 1) * P], IDENT)
                last.then_inc(turned0, 1)

            def logits(t, c):
                pe.wait_ge(evac0, t + 1)
                for k in range(KD):
                    last = pe.matmul(PS[:, 7, bass.ds(t * E0, E0)], HT_S[:, c, k * P:(k + 1) * P], GATE0[:, k, :],
                                     start=(k == 0), stop=(k == KD - 1))
                last.then_inc(logits0, 1)

            pe.wait_ge(small_loaded, 32)
            pipeline(pe, NT, 2, (1, turn0), (0, logits))

            def ranks(r, area, experts, choices, rank, count):
                a = Area(*area)
                a.take(choices, NT, experts)
                a.take(NT, experts)
                mask = a.take(NT, experts).rearrange("p t e -> p (t e)")[:, 0:NT * experts // 2].bitcast(BF16)
                pe.wait_ge(r.mask, 1)
                pe.matmul(rank, BELOW, mask, start=True, stop=False)
                for i in range(NT - 1):
                    m = mask[:, i * experts:(i + 1) * experts]
                    pe.matmul(rank[:, (i + 1) * experts:].rearrange("p (t e) -> p t e", e=experts), ONES,
                              m[:, None, :].broadcast_to([P, NT - 1 - i, experts]), start=False, stop=(i == NT - 2))
                for i in range(NT):
                    last = pe.matmul(count, ONES, mask[:, i * experts:(i + 1) * experts],
                                     start=(i == 0), stop=(i == NT - 1))
                last.then_inc(r.ranks, 1)

            ranks(r0, (W, RT0), E0, K0, PS[:, 6, :], PS[:, 5, 0:E0])

            pe.wait_ge(attn_w_loaded, 48)
            pe.wait_ge(evac0, NT)

            def qvu(t, c):
                pe.wait_ge(xt_staged, t + 1)
                if later(t, 2):
                    pe.wait_ge(pre_ready, t - 1)
                for lo, hi, bank in ((0, 2 * D, 0), (2 * D, 3 * D, 1)):
                    for k in range(KD):
                        last = pe.matmul(PS[:, 2 * c + bank, 0:hi - lo], XT_S[:, c, k * P:(k + 1) * P],
                                         W_QVU[:, k, lo:hi], start=(k == 0), stop=(k == KD - 1))
                last.then_inc(qvu_ready, 1)

            half = NT // BATCH

            def add_kv(t, c):
                pe.wait_ge(qv_ready, t + 1)
                if later(t, 2):
                    pe.wait_ge(qt_saved, t - 1)
                if isinstance(t, int) and t == 0:
                    pe.wait_ge(r0.slots, 1)
                if isinstance(t, int) and t == half:
                    pe.wait_ge(kv_ready, 1)
                for k in range(KD):
                    last = pe.transpose(PS[:, 6 + c, k * P:(k + 1) * P], Q_S[:, c, k * P:(k + 1) * P], IDENT)
                last.then_inc(q_turned, 1)
                for k in range(KD):
                    last = pe.matmul(PS[:, 4 + k, 0:P], Q_S[:, c, k * P:(k + 1) * P], V_S[:, c, k * P:(k + 1) * P],
                                     start=(isinstance(t, int) and t % half == 0),
                                     stop=(isinstance(t, int) and t % half == half - 1), skip_group_check=True)
                last.then_inc(kv_added, 1)

            for b in range(BATCH):
                pipeline(pe, half, 2, (1, lambda t, c: qvu(t + b * half, c)), (0, lambda t, c: add_kv(t + b * half, c)))

            pe.wait_ge(kv_ready, 2)

            def out_heads(t, c):
                pe.wait_ge(qt_staged, t + 1)
                if later(t, 2):
                    pe.wait_ge(z_ready, t - 1)
                for k in range(KD):
                    last = pe.matmul(PS[:, c, k * P:(k + 1) * P], QT_S[:, c, k * P:(k + 1) * P],
                                     KV[:, t // half * KD + k, :], start=True, stop=True)
                last.then_inc(o_ready, 1)

            def turn_z(t, c):
                pe.wait_ge(z_ready, t + 1)
                if later(t, 2):
                    pe.wait_ge(zt_ready, t - 1)
                for k in range(KD):
                    last = pe.transpose(PS[:, 2 + c, k * P:(k + 1) * P], Z_S[:, c, k * P:(k + 1) * P], IDENT)
                last.then_inc(z_turned, 1)

            def out_proj(t, c):
                pe.wait_ge(zt_ready, t + 1)
                if later(t, 2):
                    pe.wait_ge(s_ready, t - 1)
                for k in range(KD):
                    last = pe.matmul(PS[:, 4 + c, 0:D], ZT_S[:, c, k * P:(k + 1) * P], W_O[:, k, :],
                                     start=(k == 0), stop=(k == KD - 1))
                last.then_inc(wo_done, 1)

            pipeline(pe, NT, 2, (1, out_heads), (0, turn_z), (0, out_proj))

            pe.wait_ge(w0_loaded, 16)
            pe.wait_ge(s_ready, NT)
            pe.wait_ge(r0.experts, 1)
            turn, up, turn_hidden, down = mixture_tensor(pe, m0, I0, 1, P, WIDTH0, 2)

            def late_up(t, c):
                if isinstance(t, int) and t == UNROLL:
                    pe.wait_ge(w0_late, 16)
                up(t, c)

            pipeline(pe, TILES0, UNROLL, (2, turn), (1, late_up), (0, turn_hidden), (-1, down))

            pe.wait_ge(small1_loaded, 96)
            pe.wait_ge(m0.outs, TILES0)

            def turn1(t, c):
                pe.wait_ge(c0.xn, t + 1)
                if later(t, 2):
                    pe.wait_ge(c0.xt, t - 1)
                for k in range(KD):
                    last = pe.transpose(PS[:, c, k * P:(k + 1) * P], XN1_S[:, c, k * P:(k + 1) * P], IDENT)
                last.then_inc(c0.turned, 1)

            def logits1(t, c):
                pe.wait_ge(c0.xt, t + 1)
                for k in range(KD):
                    last = pe.matmul(PS[:, 7, bass.ds(t * E1, E1)], XT1_S[:, c, k * P:(k + 1) * P], WR[:, k, :],
                                     start=(k == 0), stop=(k == KD - 1))
                last.then_inc(c0.logits, 1)

            pipeline(pe, NT, 2, (0, turn1), (-1, logits1))
            ranks(r1, (R, RT1), E1, K1, PS[:, 6, 0:NT * E1], PS[:, 5, 0:E1])

            for j in range(4):
                if j >= 2:
                    pe.wait_ge(dr_ready, j - 1)
                for lo, hi, bank in ((0, RANK, j % 2), (RANK, RANK + 96, 2 + j % 2)):
                    for k in range(KD):
                        last = pe.matmul(PS[0:hi - lo, bank, :], W_XP[:, k, lo:hi], XT[:, k, 512 * j:512 * j + 512],
                                         start=(k == 0), stop=(k == KD - 1))
                last.then_inc(xz_ready, 1)
            pe.wait_ge(r1.slots, 1)
            for k in range(KD):
                for j in range(4):
                    n = 4 * k + j
                    if n < 4:
                        pe.wait_ge(dr_ready, j + 1)
                    else:
                        pe.wait_ge(act_step, n - 3)
                        pe.wait_ge(dl_max, n - 3)
                    pe.matmul(PS[:, 4 + n % 4, :], W_DT[:, k * P:(k + 1) * P], DELTA_R[:, 512 * j:512 * j + 512],
                              start=True, stop=True).then_inc(dl_psum, 1)

            pe.wait_ge(bc3_ready, 1)
            pe.wait_ge(dl_exp, 8)
            pe.wait_ge(dl_max, 8)
            pe.wait_ge(w1_loaded, 16)
            pe.wait_ge(r1.experts, 1)

            def spread(row, part, bank):
                return pe.matmul(PS[:, bank, :], PICK[0:96, bass.ds(row, 1)].broadcast_to([96, P]),
                                 BC3[0:96, part:part + 512], start=True, stop=True)

            def spread_b(u, c):
                if c % 2:
                    return
                if later(u, 2):
                    pe.wait_ge(bu_ready, u)
                for h in range(2):
                    last = spread((u - c) // 4, (c // 2) * SEQ + 512 * h, B_BANK + h)
                last.then_inc(b_spread, 2)

            def spread_c(u, c):
                if later(u, 1):
                    pe.wait_ge(c_copied, u)
                spread((u - c) // 4 + N_STATE, c * 512, C_BANK).then_inc(c_spread, 1)

            turn, up, turn_hidden, down = mixture_tensor(pe, m1, H1P, 3, HB, WIDTH1, 1)
            pipeline(pe, TILES1, UNROLL, (1, spread_b), (2, spread_c), (2, turn), (1, up), (0, turn_hidden), (-1, down))
            for u in range(TILES1, UNITS):
                spread_b(u, u % 4)
                spread_c(u, u % 4)

            pe.wait_ge(m1.outs, TILES1)

            def turn_y(t, c):
                pe.wait_ge(c1.y_staged, t + 1)
                if later(t, 2):
                    pe.wait_ge(c1.x, t - 1)
                for k in range(KD):
                    last = pe.transpose(PS[:, c, k * P:(k + 1) * P], XT1_S[:, c, k * P:(k + 1) * P], IDENT)
                last.then_inc(c1.y_rows, 1)

            pipeline(pe, NT, 2, (0, turn_y))


def kernel(**inputs):
    import numpy as np
    import concourse.bacc as bacc
    from concourse.bass_utils import run_bass_kernel_spmd

    g = {k: np.asarray(v) for k, v in inputs.items()}

    def blocks(w):
        return w.reshape(-1, P, w.shape[1]).transpose(1, 0, 2)

    def expert0(w13, w2):
        return np.concatenate([blocks(w13).reshape(P, -1), blocks(w2).reshape(P, -1)], axis=1)

    def expert1(w1, w3, w2):
        z = np.zeros((P, KD, 2, H1P), np.float32)
        z[:, :, 0, :H1] = blocks(w1.T)
        z[:, :, 1, :H1] = blocks(w3.T)
        d = np.zeros((H1P, D), np.float32)
        d[:H1] = w2.T
        e = np.zeros((P, 3, D), np.float32)
        e[:HB] = d.reshape(3, HB, D).transpose(1, 0, 2)
        return np.concatenate([z.reshape(P, -1), e.reshape(P, -1)], axis=1)

    shared0 = expert0(np.concatenate([g["L0_ffn_shared_gate_w"], g["L0_ffn_shared_up_w"]], axis=1),
                      g["L0_ffn_shared_down_w"])
    moe0 = np.concatenate([shared0] + [expert0(g["L0_ffn_w13"][e], g["L0_ffn_w2"][e]) for e in range(E0)], axis=1)
    shared1 = expert1(g["L1_ffn_sw1"], g["L1_ffn_sw3"], g["L1_ffn_sw2"])
    moe1 = np.concatenate([shared1] + [expert1(g["L1_ffn_ew1"][e], g["L1_ffn_ew3"][e], g["L1_ffn_ew2"][e])
                                       for e in range(E1)], axis=1)
    xp = g["L1_attn_W_xproj"].T
    bc = xp[:, RANK:]

    def halves(v):
        return v.reshape(KD, P, -1).transpose(1, 0, 2).reshape(P, -1)

    arrays = {
        "x": g["L0_attn_x"].reshape(NT, P, D).transpose(1, 0, 2),
        "w_qvu": blocks(np.concatenate([g["L0_attn_Wqk"], g["L0_attn_Wv"], g["L0_attn_Wu"]], axis=1)),
        "b_qvu": np.concatenate([g["L0_attn_bqk"], g["L0_attn_bv"], g["L0_attn_bu"]]),
        "w_o": blocks(g["L0_attn_Wo"]),
        "rows4": np.stack([g["L0_attn_bo"], g["L0_attn_ln_g"], g["L0_attn_ln_b"], g["L0_ffn_norm_w"]]),
        "gate0": blocks(g["L0_ffn_gate_w"].T),
        "moe0": moe0,
        "moe1": moe1,
        "w_xproj": blocks(np.concatenate([xp[:, :RANK], bc, bc, bc], axis=1)),
        "w_dt": g["L1_attn_W_dt"].T,
        "per_channel": np.concatenate([halves(g["L1_attn_b_dt"]), halves(g["L1_attn_D_param"]),
                                       halves(g["L1_attn_A_log"])], axis=1),
        "wr": blocks(g["L1_ffn_wr"].T),
    }
    arrays = {f"{k}_dram": np.ascontiguousarray(v) for k, v in arrays.items()}
    nc = bacc.Bacc("TRN2", target_bir_lowering=False, num_devices=1)
    args = [nc.dram_tensor(k, a.shape, mybir.dt.from_np(a.dtype), kind="ExternalInput").ap() for k, a in arrays.items()]
    out = nc.dram_tensor("out_dram", (P, NT, D), F32, kind="ExternalOutput").ap()
    two_layers(nc, *args, out)
    r = run_bass_kernel_spmd(nc, [arrays], core_ids=[0])
    return np.ascontiguousarray(r.results[0]["out_dram"].transpose(1, 0, 2)).reshape(BATCH, SEQ, D)
```

```python
from contextlib import ExitStack

import concourse.bass as bass
from concourse import mybir

F32 = mybir.dt.float32
BF16 = mybir.dt.bfloat16
I32 = mybir.dt.int32
U32 = mybir.dt.uint32
ALU = mybir.AluOpType
ACT = mybir.ActivationFunctionType
AX_X = mybir.AxisListType.X

P = 128
D = 256
KD = D // P
BATCH, SEQ = 2, 1024
TOK = BATCH * SEQ
NT = TOK // P
HEAD = 16

E0, K0 = 32, 4
CAP0 = 2 * TOK * K0 // E0
I0 = 128
E1, K1 = 8, 2
H1 = D * 4 // 3
HB = -(-H1 // 3)
H1P = 3 * HB
N_STATE = 16
RANK = 128

EPS_LN = 1e-5
EPS_RMS = 1e-6
DROPPED = float(1 << 20)


def routed_tiles(experts, choices, multiple):
    n = (TOK * choices + experts * (P - 1)) // P
    return -(-n // multiple) * multiple


UNROLL = 4
R0 = routed_tiles(E0, K0, UNROLL)
R1 = routed_tiles(E1, K1, UNROLL)
TILES0 = NT + R0
TILES1 = NT + R1
WIDTH0 = KD * 2 * I0 + D
WIDTH1 = KD * 2 * H1P + 3 * D
SLOTS0 = E0 + 1
SLOTS1 = E1 + 1
LATE0 = SLOTS0 - 13
UNITS = N_STATE * BATCH * KD


def later(t, k):
    assert isinstance(t, int) or t.min_val >= k, (t.min_val, k)
    return not isinstance(t, int) or t >= k


def pipeline(eng, n, unroll, *stages, pause=None):
    peel = 1 if min(lead for lead, _ in stages) >= 0 else 2
    def step(i, c):
        for lead, f in stages:
            if not isinstance(i, int) or 0 <= i + lead < n:
                f(i + lead, (c + lead) % unroll)

    for i in range(-max(lead for lead, _ in stages), peel * unroll):
        step(i, i)
    last = n - unroll
    cut = pause[0] // unroll if pause else peel
    for lo, hi in ((peel, cut), (cut, last // unroll)):
        if hi > lo:
            with eng.Fori(lo, hi, 1) as block:
                for c in range(unroll):
                    step(block * unroll + c, c)
        if pause and lo == peel:
            pause[1]()
    for i in range(last, n - min(lead for lead, _ in stages)):
        step(i, i)


def two_layers(nc, x, w_qvu, b_qvu, w_o, rows4, gate0, moe0, moe1, w_xproj, w_dt, per_channel, wr, out):
    rows0 = rows1 = nc.dram_tensor("rows", [TILES0 * P, D], F32, kind="Internal").ap()
    outs0 = nc.dram_tensor("outs0", [TILES0 * P, D], F32, kind="Internal").ap()
    outs1 = nc.dram_tensor("outs1", [TILES1 * P, D], F32, kind="Internal").ap()

    with ExitStack() as ctx:
        def sb(name, shape, dt=F32):
            return ctx.enter_context(nc.sbuf_tensor(name, shape, dt))

        def sem(name):
            return ctx.enter_context(nc.semaphore(name))

        class Area:
            def __init__(self, tensor, at=0):
                self.tensor, self.at = tensor, at

            def take(self, *shape, dt=F32, parts=P):
                n = 1
                for s in shape:
                    n *= s
                floats = n if dt in (F32, I32, U32) else n // 2
                v = self.tensor[0:parts, self.at:self.at + floats]
                self.at += floats
                if dt != F32:
                    v = v.bitcast(dt)
                if len(shape) == 2:
                    v = v.rearrange("p (a b) -> p a b", a=shape[0])
                if len(shape) == 3:
                    v = v.rearrange("p (a b c) -> p a b c", a=shape[0], b=shape[1])
                return v

        W = sb("W", [P, SLOTS0 * WIDTH0])
        X = sb("X", [P, NT, D])
        AR_H = sb("AR_H", [P, NT * D])
        AR_T = sb("AR_T", [P, NT * D])
        AR_U = sb("AR_U", [P, NT * D])
        R = sb("R", [P, 6144])
        H = AR_H[:, :].rearrange("p (t d) -> p t d", t=NT)
        U = AR_U[:, :].rearrange("p (t d) -> p t d", t=NT)
        XT = AR_T[:, :].rearrange("p (k n) -> p k n", k=KD)
        DELTA = AR_H[:, :].rearrange("p (k n) -> p k n", k=KD)
        DU = AR_U[:, :].rearrange("p (k n) -> p k n", k=KD)

        MB_SIZE = 1024 + 512 + 2 * H1P + 2 * 3 * P + 1024
        MB = Area(sb("MB", [P, MB_SIZE]))
        ROWS = MB.take(4, D)
        ROWS_T = MB.take(2, D)
        HID = MB.take(2, H1P)
        HID_T = MB.take(2, 3 * P)
        OUTS = MB.take(4, D)

        MC = Area(MB.tensor)
        DIAG = MC.take(2, K0 * P)
        BASE = MC.take(2, D)
        XN1_S = MC.take(4, D)
        TOP1 = MC.take(NT, 8)
        TOP1_ID = MC.take(NT, 8, dt=U32)
        TOP1_IDF = MC.take(NT, 8)
        SMALL1 = MC.take(5, E1)
        RT1 = MC.at
        assert RT1 + 4 * NT * E1 <= MB_SIZE

        CO = Area(sb("CO", [P, 1138 + P]))
        IDENT = CO.take(P)
        HALF = CO.take(P)
        BLOCKS = CO.take(P)
        BELOW = CO.take(P, dt=BF16)
        ONES = CO.take(P, dt=BF16)
        PICK = CO.take(2 * N_STATE, dt=BF16)
        IOTA_E = CO.take(E0)
        IOTA_T = CO.take(R0)
        STEPS = CO.take(NT)
        WEIGHT = CO.take(NT, K0)
        SLOT_IN = CO.take(K0, NT, dt=I32)
        SLOT_OUT = CO.take(K0, NT, dt=I32)
        W_AT = CO.take(TILES0 + 4, dt=I32)
        STAT = CO.take(4, 6)
        AGGR = CO.take(4, 2)
        MEAN_VAR = CO.take(NT, 2)
        RSTD = CO.take(NT)
        TOTAL = CO.take(NT)
        RRMS = CO.take(NT)
        A_NEG = CO.take(KD, N_STATE)
        B_DT = CO.take(KD)
        D_SKIP = CO.take(KD)
        VARS = CO.take(2, 4)
        ROOTS = CO.take(2, 4)
        PRODS = CO.take(2, 4)
        EPS_COL = CO.take(1)
        assert CO.at <= 1138 + P

        RA = Area(R)
        W_QVU = RA.take(KD, 3 * D)
        W_O = RA.take(KD, D)
        GATE0 = RA.take(KD, E0)
        B_QVU = RA.take(3 * D)
        ROW4 = RA.take(4, D)
        B_O, LN_G, LN_B, NORM_W = (ROW4[:, i, :] for i in range(4))
        TOP = RA.take(NT, 8)
        TOP_ID = RA.take(NT, 8, dt=U32)
        TOP_IDF = RA.take(NT, 8)
        XN_S = RA.take(2, D)
        H_S = RA.take(2, D)
        HT_S = RA.take(2, D)
        SMALL = RA.take(5, E0)
        assert RA.at <= 6144
        RC = Area(R)
        GOT = RC.take(4, K0 + 1, D)
        TANH = RC.take(2, D)
        XT1_S = RC.take(2, D)
        assert RC.at <= 6144
        RS = Area(R)
        C_SB = RS.take(2, SEQ)
        DA = RS.take(2, SEQ)
        Z = RS.take(2, SEQ)
        RD = Area(R)
        DELTA_R = RD.take(TOK)
        BC = RD.take(TOK)
        BC_HI = RD.take(TOK, dt=BF16)
        assert RD.at <= 6144

        WA = Area(W, LATE0 * WIDTH0)
        XT_S = WA.take(2, D)
        PRE = WA.take(2, 3 * D)
        ELU = WA.take(2, D)
        TH = WA.take(2, 2 * D)
        Q_S = WA.take(2, D)
        V_S = WA.take(2, D)
        QT_S = WA.take(2, D)
        Z_S = WA.take(2, D)
        ZT_S = WA.take(2, D)
        KV = WA.take(BATCH * KD, P)
        RT0 = WA.at
        assert RT0 + R0 * (E0 + 1) <= SLOTS0 * WIDTH0

        WB = Area(W, SLOTS1 * WIDTH1)
        XN1 = WB.take(NT, D)
        W_DT = WB.take(D)
        W_XP = WB.take(KD, RANK + 96)
        WR = WB.take(KD, E1)
        BC3 = WB.take(TOK, dt=BF16)
        assert WB.at <= SLOTS0 * WIDTH0

        PS = ctx.enter_context(nc.psum_tensor("PS", [P, 8, 512], F32))

        MIX_BANKS = ({"rows": (0, 5), "up": (1, 2), "hid": 3, "outs": (4, 6)},
                     {"rows": (0, 0), "up": (1, 1), "hid": 3, "outs": (4, 4)})
        O_BANKS = (0, 1, 6, 7)
        SUM_BANK = 2
        Y_BANKS = (0, 1, 6, 7)
        C_BANK, B_BANK = 5, 6

        x_loaded, small_loaded, attn_w_loaded = sem("x_loaded"), sem("small_loaded"), sem("attn_w_loaded")
        w0_loaded, w0_late = sem("w0_loaded"), sem("w0_late")
        zero_ready, zero_filled = sem("zero_ready"), sem("zero_filled")
        consts_ready, consts_cleared = sem("consts_ready"), sem("consts_cleared")
        rows_copied, h_stored = sem("rows_copied"), sem("h_stored")
        v_step = sem("v_step")
        h_ready, turned0, evac0, logits0 = sem("h_ready"), sem("turned0"), sem("evac0"), sem("logits0")
        st_a, st_b, st_c, xn_s_done = sem("st_a"), sem("st_b"), sem("st_c"), sem("xn_s_done")

        class Routing:
            def __init__(self, n):
                self.top, self.top_id = sem(f"top{n}"), sem(f"top_id{n}")
                self.diff, self.exps = sem(f"diff{n}"), sem(f"exps{n}")
                self.mask, self.ranks = sem(f"mask{n}"), sem(f"ranks{n}")
                self.slots, self.experts = sem(f"slots{n}"), sem(f"experts{n}")
                self.scattered = sem(f"scattered{n}")

        r0, r1 = Routing(0), Routing(1)

        xt_staged, qvu_ready, pre_ready, th_ready = sem("xt_staged"), sem("qvu_ready"), sem("pre_ready"), sem("th_ready")
        pre_done, elu_step, qv_ready = sem("pre_done"), sem("elu_step"), sem("qv_ready")
        kv_added, q_turned, qt_saved, kv_ready = sem("kv_added"), sem("q_turned"), sem("qt_saved"), sem("kv_ready")
        qt_staged, o_ready, z_step, z_ready = sem("qt_staged"), sem("o_ready"), sem("z_step"), sem("z_ready")
        z_turned, zt_ready, wo_done, s_ready = sem("z_turned"), sem("zt_ready"), sem("wo_done"), sem("s_ready")

        o_sums, o_stats, o_dev = sem("o_sums"), sem("o_stats"), sem("o_dev")

        class Mixture:
            def __init__(self, n):
                self.loaded = [sem(f"m{n}_loaded{i}") for i in range(2)]
                self.stored = [sem(f"m{n}_stored{i}") for i in range(2)]
                self.turned = sem(f"m{n}_turned")
                self.rows_t = sem(f"m{n}_rows_t")
                self.hidden = sem(f"m{n}_hidden")
                self.tanh = sem(f"m{n}_tanh")
                self.half = sem(f"m{n}_half")
                self.gated = sem(f"m{n}_gated")
                self.hid_turned = sem(f"m{n}_hid_turned")
                self.hid_t = sem(f"m{n}_hid_t")
                self.down = sem(f"m{n}_down")
                self.outs = sem(f"m{n}_outs")

        m0, m1 = Mixture(0), Mixture(1)

        class Combine:
            def __init__(self, n):
                self.got = [sem(f"c{n}_got{i}") for i in range(4)]
                self.shared = [sem(f"c{n}_shared{i}") for i in range(4)]
                self.diag = sem(f"c{n}_diag")
                self.acc = sem(f"c{n}_acc")
                self.tanh = sem(f"c{n}_tanh")
                self.x = sem(f"c{n}_x")
                if n == 0:
                    self.base = sem("c0_base")
                    self.xn = sem("c0_xn")
                    self.turned = sem("c0_turned")
                    self.xt = sem("c0_xt")
                    self.logits = sem("c0_logits")
                else:
                    self.y_staged = sem("c1_y_staged")
                    self.y_rows = sem("c1_y_rows")

        c0, c1 = Combine(0), Combine(1)
        w1_loaded, small1_loaded, xn1_stored, out_stored = sem("w1_loaded"), sem("small1_loaded"), sem("xn1_stored"), sem("out_stored")
        xz_ready, dr_ready, bc_copied, bc_step, bc3_ready = sem("xz_ready"), sem("dr_ready"), sem("bc_copied"), sem("bc_step"), sem("bc3_ready")
        dl_psum, dl_exp, dl_max, dl_ln, dl_step, du_ready = sem("dl_psum"), sem("dl_exp"), sem("dl_max"), sem("dl_ln"), sem("dl_step"), sem("du_ready")
        a_exp, a_ready, act_step = sem("a_exp"), sem("a_ready"), sem("act_step")
        c_spread, b_spread, c_copied, da_ready = sem("c_spread"), sem("b_spread"), sem("c_copied"), sem("da_ready")
        bu_ready, scanned, hc_ready, y_added = sem("bu_ready"), sem("scanned"), sem("hc_ready"), sem("y_added")

        block = ctx.enter_context(nc.Block())

        def tiles_of(dram, t, n):
            return dram[bass.ds(t * P, n * P), :].rearrange("(j p) d -> p j d", p=P)

        @block.sync
        def _(sp):
            sp.dma_start(X[:, :, :], x).then_inc(x_loaded, 16)
            sp.dma_start(ROW4, rows4[None, :, :].broadcast_to([P, 4, D])).then_inc(small_loaded, 16)
            sp.dma_start(GATE0, gate0).then_inc(small_loaded, 16)
            sp.dma_start(W_QVU, w_qvu).then_inc(attn_w_loaded, 16)
            sp.dma_start(B_QVU, b_qvu[None, :].broadcast_to([P, 3 * D])).then_inc(attn_w_loaded, 16)
            sp.dma_start(W_O, w_o).then_inc(attn_w_loaded, 16)
            sp.wait_ge(zero_ready, 1)
            for j in range(R0 // 4):
                sp.dma_start(tiles_of(rows0, NT + 4 * j, 4), OUTS).then_inc(zero_filled, 16)
            sp.dma_start(W[:, 0:LATE0 * WIDTH0], moe0[:, 0:LATE0 * WIDTH0]).then_inc(w0_loaded, 16)
            sp.wait_ge(rows_copied, NT)
            sp.dma_start(tiles_of(rows0, 0, NT), H).then_inc(h_stored, 16)
            sp.wait_ge(s_ready, NT)

            def load_w0(first, n):
                at = bass.ds(first * WIDTH0, n * WIDTH0)
                sp.dma_start(W[:, at], moe0[:, at]).then_inc(w0_late, 16)

            def run_mixture(m, rows, outs, tiles, first_ready, routed_ready, between):
                def load(t, c):
                    if later(t, 4):
                        sp.wait_ge(m.turned, t - 2)
                    sp.dma_start(ROWS[:, c:c + 2, :], tiles_of(rows, t, 2)).then_inc(m.loaded[c // 2], 16)

                def store(t, c):
                    sp.wait_ge(m.outs, t + 2)
                    sp.dma_start(tiles_of(outs, t, 2), OUTS[:, c:c + 2, :]).then_inc(m.stored[c // 2], 16)

                first_ready()
                load(0, 0)
                load(2, 2)
                between(0)
                load(4, 0)
                between(1)
                load(6, 2)
                between(2)

                def four_tiles(b):
                    store(4 * b - 4, 0)
                    load(4 * b + 4, 0)
                    store(4 * b - 2, 2)
                    load(4 * b + 6, 2)

                with sp.Fori(1, NT // 4 - 1, 1) as b:
                    four_tiles(b)
                    between(b + 2)
                routed_ready()
                with sp.Fori(NT // 4 - 1, tiles // 4 - 1, 1) as b:
                    four_tiles(b)
                for t in (tiles - 8, tiles - 6, tiles - 4, tiles - 2):
                    store(t, t % 4)

            def combine(c, outs, between):
                for i in range(4):
                    sp.dma_start(GOT[:, i, 0, :], outs[i * P:(i + 1) * P, :]).then_inc(c.shared[i], 16)
                with sp.Fori(1, NT // 4, 1) as b:
                    between(b)
                    for i in range(4):
                        sp.wait_ge(c.acc, 4 * b + (i - 3))
                        sp.dma_start(GOT[:, i, 0, :], outs[bass.ds((4 * b + i) * P, P), :]).then_inc(c.shared[i], 16)

            def load_w1(slot):
                at = bass.ds(slot * WIDTH1, WIDTH1)
                sp.dma_start(W[:, at], moe1[:, at]).then_inc(w1_loaded, 16)

            def first0():
                sp.wait_ge(h_stored, 16)

            def routed0():
                sp.wait_ge(zero_filled, 16 * R0 // 4)
                sp.wait_ge(r0.scattered, 16 * NT * K0)
                sp.wait_ge(h_stored, 16)

            late_slots = SLOTS0 - LATE0 - 5

            def late_w0(step):
                if isinstance(step, int):
                    load_w0(LATE0 + (0, 3, 4)[step], (3, 1, 1)[step])
                else:
                    load_w0(LATE0 + 5 + (step - 3) * (late_slots // 2), late_slots // 2)

            assert late_slots % 2 == 0
            run_mixture(m0, rows0, outs0, TILES0, first0, routed0, late_w0)

            sp.wait_ge(m0.down, TILES0)
            sp.dma_start(W_DT, w_dt).then_inc(small1_loaded, 16)
            sp.dma_start(W_XP, w_xproj).then_inc(small1_loaded, 16)
            sp.dma_start(WR, wr).then_inc(small1_loaded, 16)
            sp.dma_start(A_NEG, per_channel[:, 2 * KD:].rearrange("p (k n) -> p k n", k=KD)).then_inc(small1_loaded, 16)
            sp.dma_start(B_DT, per_channel[:, 0:KD]).then_inc(small1_loaded, 16)
            sp.dma_start(D_SKIP, per_channel[:, KD:2 * KD]).then_inc(small1_loaded, 16)
            for i in range(2):
                sp.wait_ge(m0.stored[i], 4 * TILES0)
            def two_w1(b):
                load_w1(2 * b - 2)
                load_w1(2 * b - 1)

            combine(c0, outs0, two_w1)
            for slot in range(NT // 2 - 2, SLOTS1):
                load_w1(slot)
            sp.wait_ge(c0.xn, NT)
            sp.dma_start(tiles_of(rows1, 0, NT), XN1).then_inc(xn1_stored, 16)

            def first1():
                sp.wait_ge(xn1_stored, 16)

            def routed1():
                sp.wait_ge(r1.scattered, 16 * NT * K1)

            run_mixture(m1, rows1, outs1, TILES1, first1, routed1, lambda step: None)
            sp.wait_ge(y_added, UNITS)
            for i in range(2):
                sp.wait_ge(m1.stored[i], 4 * TILES1)
            combine(c1, outs1, lambda b: None)
            for g in range(4):
                sp.wait_ge(c1.x, 4 * g + 4)
                sp.dma_start(out[:, 4 * g:4 * g + 4, :], X[:, 4 * g:4 * g + 4, :]).then_inc(out_stored, 16)
            sp.wait_ge(out_stored, 64)

        @block.gpsimd
        def _(pool):
            pool.memset(OUTS, 0.0).then_inc(zero_ready, 1)
            pool.memset(IDENT, 0.0)
            pool.memset(HALF, 0.0)
            pool.memset(BLOCKS, 0.5)
            pool.memset(BELOW, 0.0)
            pool.memset(ONES, 1.0)
            pool.memset(EPS_COL, EPS_LN)
            pool.memset(W_AT[0:1, :], 0)
            pool.memset(PICK, 0.0).then_inc(consts_cleared, 1)
            pool.wait_ge(consts_cleared, 1)
            pool.affine_select(out=IDENT, in_=IDENT, compare_op=ALU.not_equal, fill=1.0, base=0,
                               pattern=[[-1, P]], channel_multiplier=1)
            pool.affine_select(out=HALF, in_=HALF, compare_op=ALU.not_equal, fill=0.5, base=0,
                               pattern=[[-1, P]], channel_multiplier=1)
            pool.affine_select(out=BELOW, in_=BELOW, compare_op=ALU.is_ge, fill=1.0, base=0,
                               pattern=[[-1, P]], channel_multiplier=1)
            v = BLOCKS.rearrange("p (b j) -> p b j", j=HEAD)
            pool.affine_select(out=v, in_=v, compare_op=ALU.is_ge, fill=0.0, base=0,
                               pattern=[[-HEAD, P // HEAD], [0, HEAD]], channel_multiplier=1).then_inc(consts_cleared, 1)
            pool.wait_ge(consts_cleared, 2)
            for q in range(3):
                w = PICK[32 * q:32 * q + 32, :]
                pool.affine_select(out=w, in_=w, compare_op=ALU.not_equal, fill=1.0, base=0,
                                   pattern=[[-1, 2 * N_STATE]], channel_multiplier=1).then_inc(consts_cleared, 1)
                pool.wait_ge(consts_cleared, 3 + q)
            pool.affine_select(out=v, in_=v, compare_op=ALU.is_ge, fill=0.0, base=HEAD - 1,
                               pattern=[[HEAD, P // HEAD], [0, HEAD]], channel_multiplier=-1)
            pool.iota(IOTA_E, pattern=[[1, E0]], base=0, channel_multiplier=0, allow_small_or_imprecise_dtypes=True)
            pool.iota(IOTA_T, pattern=[[1, R0]], base=0, channel_multiplier=0, allow_small_or_imprecise_dtypes=True)
            pool.iota(STEPS, pattern=[[P, NT]], base=0, channel_multiplier=0,
                      allow_small_or_imprecise_dtypes=True).then_inc(consts_ready, 1)

            def keep_h(t, c):
                pool.wait_ge(h_ready, t + 1)
                pool.wait_ge(consts_ready, 1)
                pool.tensor_copy(H[:, bass.ds(t, 1), :], H_S[:, c:c + 1, :]).then_inc(rows_copied, 1)

            pipeline(pool, NT, 2, (0, keep_h))

            def scatter(src, rows, choices, tiles, done):
                for t in range(NT):
                    for k in range(choices):
                        pool.indirect_dma_start(
                            out=rows, out_offset=bass.IndirectOffsetOnAxis(ap=SLOT_IN[:, k, t:t + 1], axis=0),
                            in_=src[:, t, :], in_offset=None,
                            bounds_check=tiles * P - 1, oob_is_err=False).then_inc(done, 16)

            pool.wait_ge(r0.slots, 1)
            pool.wait_ge(zero_filled, 16 * R0 // 4)
            pool.wait_ge(rows_copied, NT)
            scatter(H, rows0, K0, TILES0, r0.scattered)

            def gather(c, outs, choices):
                for t in range(NT):
                    i = t % 4
                    if t >= 4:
                        pool.wait_ge(c.acc, t - 3)
                    for k in range(choices):
                        pool.indirect_dma_start(
                            out=GOT[:, i, 1 + k, :], out_offset=None, in_=outs,
                            in_offset=bass.IndirectOffsetOnAxis(ap=SLOT_OUT[:, k, t:t + 1], axis=0)).then_inc(c.got[i], 16)

            for i in range(2):
                pool.wait_ge(m0.stored[i], 4 * TILES0)
            gather(c0, outs0, K0)

            pool.wait_ge(r1.slots, 1)
            pool.wait_ge(c0.xn, NT)
            scatter(XN1, rows1, K1, TILES1, r1.scattered)

            def times_c(u, c):
                pool.wait_ge(scanned, u + 1)
                pool.wait_ge(c_copied, u + 2 - c % 2)
                pool.tensor_tensor(Z[:, c % 2, :], Z[:, c % 2, :], C_SB[:, c // 2, :], ALU.mult).then_inc(hc_ready, 1)

            pipeline(pool, UNITS, 4, (0, times_c))
            pool.wait_ge(y_added, UNITS)
            for i in range(2):
                pool.wait_ge(m1.stored[i], 4 * TILES1)
            gather(c1, outs1, K1)

        def mixture_outs(eng, m):
            bank = MIX_BANKS[m is m1]

            def copy_outs(t, c):
                eng.wait_ge(m.down, t + 1)
                if later(t, 4):
                    eng.wait_ge(m.stored[c // 2], 4 * t - 4 * c)
                src = PS[:, bank["outs"][c % 2], 0:D]
                copy = eng.tensor_copy(OUTS[:, c, :], src) if m is m0 else eng.copy(OUTS[:, c, :], src)
                copy.then_inc(m.outs, 1)

            return copy_outs

        def mixture_scalar(act, m, hidden, blocks, part):
            bank = MIX_BANKS[m is m1]

            def copy_rows_t(t, c):
                act.wait_ge(m.turned, t + 1)
                if later(t, 2):
                    act.wait_ge(m.hidden, t - 1)
                act.copy(ROWS_T[:, c % 2, :], PS[:, bank["rows"][c % 2], 0:D]).then_inc(m.rows_t, 1)

            def tanh(t, c):
                act.wait_ge(m.hidden, t + 1)
                if later(t, 2):
                    act.wait_ge(m.hid_turned, t - 1)
                act.activation(HID[:, c % 2, 0:hidden], PS[:, bank["up"][c % 2], 0:hidden], ACT.Tanh,
                               scale=0.5).then_inc(m.tanh, 1)

            def copy_hid_t(t, c):
                act.wait_ge(m.hid_turned, t + 1)
                if later(t, 2):
                    act.wait_ge(m.down, t - 1)
                act.copy(HID_T[0:part, c % 2, 0:blocks * P], PS[0:part, bank["hid"], 0:blocks * P]).then_inc(m.hid_t, 1)

            return copy_rows_t, tanh, copy_hid_t

        @block.scalar
        def _(act):
            def save_t(t, c):
                act.wait_ge(turned0, t + 1)
                if later(t, 2):
                    act.wait_ge(logits0, t - 1)
                act.copy(HT_S[:, c, :], PS[:, c, D:2 * D])
                act.copy(XT[:, :, bass.ds(t * P, P)],
                         PS[:, c, 0:D].rearrange("p (k n) -> p k n", k=KD)).then_inc(evac0, 1)

            pipeline(act, NT, 2, (0, save_t))

            def softmax(r, top, choices):
                act.wait_ge(r.diff, 1)
                act.activation(WEIGHT[:, :, 0:choices], WEIGHT[:, :, 0:choices], ACT.Exp).then_inc(r.exps, 1)

            softmax(r0, TOP, K0)

            half = NT // BATCH

            def stage_xt(t, c):
                if later(t, 2):
                    act.wait_ge(qvu_ready, t - 1)
                act.wait_ge(evac0, NT)
                act.copy(XT_S[:, c, :].rearrange("p (k n) -> p k n", k=KD),
                         XT[:, :, bass.ds(t * P, P)]).then_inc(xt_staged, 1)

            def tables(t, c):
                act.wait_ge(pre_ready, t + 1)
                if later(t, 2):
                    act.wait_ge(qv_ready, t - 1)
                act.activation(TH[:, c, :], PRE[:, c, D:3 * D], ACT.Tanh, scale=0.5)
                act.activation(ELU[:, c, :], ELU[:, c, :], ACT.Exp).then_inc(th_ready, 1)

            def save_qt(t, c):
                act.wait_ge(q_turned, t + 1)
                act.wait_ge(xt_staged, t + 1)
                act.wait_ge(evac0, NT)
                act.copy(XT[:, :, bass.ds(t * P, P)],
                         PS[:, 6 + c, 0:D].rearrange("p (k n) -> p k n", k=KD)).then_inc(qt_saved, 1)

            for b in range(BATCH):
                pipeline(act, half, 2, (2, lambda t, c: stage_xt(t + b * half, c)),
                         (1, lambda t, c: tables(t + b * half, c)), (0, lambda t, c: save_qt(t + b * half, c)))

            def stage_qt(t, c):
                if later(t, 2):
                    act.wait_ge(o_ready, t - 1)
                act.wait_ge(qt_saved, NT)
                act.copy(QT_S[:, c % 2, :].rearrange("p (k n) -> p k n", k=KD),
                         XT[:, :, bass.ds(t * P, P)]).then_inc(qt_staged, 1)

            def copy_zt(t, c):
                act.wait_ge(z_turned, t + 1)
                if later(t, 2):
                    act.wait_ge(wo_done, t - 1)
                act.copy(ZT_S[:, c % 2, :], PS[:, 2 + c % 2, 0:D]).then_inc(zt_ready, 1)

            def deviation(t, c):
                act.wait_ge(o_stats, t + 1)
                act.activation(STAT[:, 2 + c % 2, 2:3], STAT[:, 2 + c % 2, 1:2], ACT.Sqrt, bias=EPS_COL).then_inc(o_dev, 1)

            pipeline(act, NT, 4, (3, stage_qt), (1, deviation), (0, copy_zt))

            rows_t, tanh, hid_t = mixture_scalar(act, m0, I0, 1, P)
            pipeline(act, TILES0, UNROLL, (2, rows_t), (1, tanh), (0, hid_t))

            def tanh_acc(cm, t, c):
                act.wait_ge(cm.acc, t + 1)
                if later(t, 2):
                    act.wait_ge(cm.x, t - 1)
                act.activation(TANH[:, c % 2, :], PS[:, SUM_BANK + c, 0:D], ACT.Tanh, scale=0.5).then_inc(cm.tanh, 1)

            def diagonals(cm, m, t, i, choices, tiles):
                act.wait_ge(consts_ready, 1)
                if later(t, 2):
                    act.wait_ge(cm.acc, t - 1)
                else:
                    act.wait_ge(m.turned, tiles)
                for k in range(choices):
                    last = act.activation(DIAG[:, i, k * P:(k + 1) * P], IDENT, ACT.Copy, scale=WEIGHT[:, t, k:k + 1])
                last.then_inc(cm.diag, 1)

            def save_xt1(t, i):
                act.wait_ge(c0.turned, t + 1)
                if later(t, 2):
                    act.wait_ge(c0.logits, t - 1)
                act.copy(XT1_S[:, i, :], PS[:, i, 0:D])
                act.copy(XT[:, :, bass.ds(t * P, P)],
                         PS[:, i, 0:D].rearrange("p (k n) -> p k n", k=KD)).then_inc(c0.xt, 1)

            pipeline(act, NT, 4, (2, lambda t, c: diagonals(c0, m0, t, c % 2, K0, TILES0)),
                     (0, lambda t, c: tanh_acc(c0, t, c)), (-4, lambda t, c: save_xt1(t, c % 2)))

            act.wait_ge(small1_loaded, 96)
            act.activation(A_NEG, A_NEG, ACT.Exp).then_inc(a_exp, 1)
            softmax(r1, TOP1, K1)
            for j in range(4):
                act.wait_ge(xz_ready, j + 1)
                act.wait_ge(r1.experts, 1)
                act.copy(DELTA_R[:, 512 * j:512 * j + 512], PS[:, j % 2, :])
                act.copy(BC[0:96, 512 * j:512 * j + 512], PS[0:96, 2 + j % 2, :]).then_inc(dr_ready, 1)
            for k in range(KD):
                for j in range(4):
                    n = 4 * k + j
                    act.wait_ge(dl_max, n + 1)
                    part = DU[:, k, 512 * j:512 * j + 512]
                    act.activation(part, PS[:, 4 + n % 4, :], ACT.Abs, bias=B_DT[:, k:k + 1]).then_inc(act_step, 1)
                    act.wait_ge(act_step, n + 1)
                    act.activation(part, part, ACT.Exp, scale=-1.0).then_inc(dl_exp, 1)
            act.wait_ge(dl_step, KD)
            for k in range(KD):
                act.activation(DU[:, k, :], DU[:, k, :], ACT.Ln).then_inc(dl_ln, 1)

            def copy_c(u, c):
                act.wait_ge(c_spread, u + 1)
                if later(u, 4):
                    act.wait_ge(hc_ready, u - c % 2 - 2)
                h = 512 * (c % 2)
                act.copy(C_SB[:, c // 2, h:h + 512], PS[:, C_BANK, :]).then_inc(c_copied, 1)

            def decay(u, c):
                act.wait_ge(a_ready, 1)
                act.wait_ge(du_ready, 1)
                if later(u, 2):
                    act.wait_ge(scanned, u - 1)
                n = (u - c) // 4
                act.activation(DA[:, c % 2, :], DELTA[:, c % 2, (c // 2) * SEQ:(c // 2 + 1) * SEQ], ACT.Exp,
                               scale=A_NEG[:, c % 2, bass.ds(n, 1)]).then_inc(da_ready, 1)

            rows_t, tanh, hid_t = mixture_scalar(act, m1, H1P, 3, HB)
            copy_outs = mixture_outs(act, m1)
            pipeline(act, TILES1, UNROLL, (2, rows_t), (1, decay), (1, tanh), (0, hid_t), (2, copy_c), (-1, copy_outs))
            for u in range(TILES1, UNITS):
                copy_c(u, u % 4)
                decay(u, u % 4)

            def stage_y(t, i):
                if later(t, 2):
                    act.wait_ge(c1.y_rows, t - 1)
                act.wait_ge(y_added, UNITS)
                act.copy(XT1_S[:, i, :].rearrange("p (k n) -> p k n", k=KD),
                         XT[:, :, bass.ds(t * P, P)]).then_inc(c1.y_staged, 1)

            pipeline(act, NT, 4, (2, lambda t, c: diagonals(c1, m1, t, c % 2, K1, TILES1)),
                     (2, lambda t, c: stage_y(t, c % 2)), (0, lambda t, c: tanh_acc(c1, t, c)))

        def mixture_vector(dve, m, up, scale_cols):
            bank = MIX_BANKS[m is m1]

            def gate(t, c):
                dve.wait_ge(m.tanh, t + 1)
                hid = HID[:, c % 2, 0:scale_cols]
                dve.scalar_tensor_tensor(out=hid, in0=hid, scalar=1.0, in1=PS[:, bank["up"][c % 2], 0:scale_cols],
                                         op0=ALU.add, op1=ALU.mult).then_inc(m.half, 1)
                dve.wait_ge(m.half, t + 1)
                dve.tensor_tensor(hid, hid, up(c), ALU.mult).then_inc(m.gated, 1)

            return gate

        @block.vector
        def _(dve):
            steps = [0]

            def link(ins):
                steps[0] += 1
                ins.then_inc(v_step, 1)
                dve.wait_ge(v_step, steps[0])

            dve.wait_ge(x_loaded, 16)
            dve.wait_ge(small_loaded, 32)

            def chain(sem, start):
                n = [0]

                def then(ins):
                    n[0] += 1
                    ins.then_inc(sem, 1)
                    dve.wait_ge(consts_ready, 1)
                    dve.wait_ge(sem, start + n[0])
                return then, n

            def rsqrt(then, y, v, tmp):
                then(dve.tensor_scalar(y.bitcast(I32), v.bitcast(I32), 1, None, ALU.logical_shift_right))
                then(dve.tensor_scalar(y.bitcast(I32), y.bitcast(I32), -1.0, float(0x5f3759df), ALU.mult, ALU.add))
                for _ in range(3):
                    then(dve.tensor_tensor(tmp, y, y, ALU.mult))
                    then(dve.tensor_tensor(tmp, tmp, v, ALU.mult))
                    then(dve.tensor_scalar(tmp, tmp, -0.5, 1.5, ALU.mult, ALU.add))
                    then(dve.tensor_tensor(y, y, tmp, ALU.mult))

            def move(out, src):
                return dve.tensor_scalar(out, src, 1.0, None, ALU.mult)

            NORM_STEPS = 19

            def norms(g, c):
                four = bass.ds(4 * g, 4)
                then, n = chain(st_c, NORM_STEPS * g)
                for j in range(4):
                    dve.bn_stats(STAT[:, j, :], X[:, 4 * g + j, :]).then_inc(st_a, 1)
                dve.wait_ge(consts_ready, 1)
                dve.wait_ge(st_a, 4 * g + 4)
                for j in range(4):
                    dve.bn_aggr(AGGR[:, j, :], STAT[:, j, :]).then_inc(st_b, 1)
                dve.wait_ge(st_b, 4 * g + 4)
                move(MEAN_VAR[:, four, :], AGGR)
                var = AGGR[:, :, 1]
                then(dve.tensor_scalar(VARS[:, 0, :], var, EPS_LN, None, ALU.add))
                then(dve.reciprocal(PRODS[:, 0, :], VARS[:, 0, :]))
                then(dve.tensor_tensor(VARS[:, 1, :], PRODS[:, 0, :], var, ALU.mult))
                then(dve.tensor_scalar(VARS[:, 1, :], VARS[:, 1, :], EPS_RMS, None, ALU.add))
                rsqrt(then, ROOTS, VARS, PRODS)
                move(RSTD[:, four], ROOTS[:, 0, :])
                then(move(RRMS[:, four], ROOTS[:, 1, :]))
                assert n[0] == NORM_STEPS
                for j in range(4):
                    t = 4 * g + j
                    if later(t, 2):
                        dve.wait_ge(turned0, t - 1)
                        dve.wait_ge(rows_copied, t - 1)
                    dve.tensor_scalar(XN_S[:, j % 2, :], X[:, t, :], MEAN_VAR[:, t, 0:1], RSTD[:, bass.ds(t, 1)],
                                      ALU.subtract, ALU.mult).then_inc(xn_s_done, 1)
                    dve.wait_ge(xn_s_done, t + 1)
                    dve.scalar_tensor_tensor(out=H_S[:, j % 2, :], in0=XN_S[:, j % 2, :], scalar=RRMS[:, bass.ds(t, 1)],
                                             in1=NORM_W, op0=ALU.mult, op1=ALU.mult).then_inc(h_ready, 1)

            for g in range(NT // 4):
                norms(g, 0)

            def routing(r, logits, logits_ready, experts, choices, cap, routed, top, top_id, top_idf, small, area,
                        rank, count, width):
                dve.wait_ge(logits_ready, NT)

                def pick(t):
                    dve.max(top[:, t, :], logits[:, t * experts:(t + 1) * experts]).then_inc(r.top, 1)
                    dve.wait_ge(r.top, t + 1)
                    dve.max_index(top_id[:, t, :], top[:, t, :],
                                  logits[:, t * experts:(t + 1) * experts]).then_inc(r.top_id, 1)

                for t in range(NT):
                    pick(t)
                dve.wait_ge(r.top_id, NT)
                a = Area(*area)
                chosen = a.take(choices, NT, experts)
                slot = a.take(NT, experts)
                cut = a.take(NT, experts)
                mask = cut.rearrange("p t e -> p (t e)")[:, 0:NT * experts // 2].bitcast(BF16)
                w = WEIGHT[:, :, 0:choices]
                dve.tensor_tensor(w, top[:, :, 0:choices], top[:, :, 0:1].broadcast_to([P, NT, choices]),
                                  ALU.subtract).then_inc(r.diff, 1)
                link(dve.tensor_copy(top_idf, top_id))
                for k in range(choices):
                    last = dve.tensor_tensor(chosen[:, k, :, :], IOTA_E[:, None, 0:experts].broadcast_to([P, NT, experts]),
                                             top_idf[:, :, k:k + 1].broadcast_to([P, NT, experts]), ALU.is_equal)
                link(last)
                mask3 = mask.rearrange("p (t e) -> p t e", e=experts)
                if choices == 4:
                    dve.tensor_tensor(slot, chosen[:, 0, :, :], chosen[:, 1, :, :], ALU.add)
                    last = dve.tensor_tensor(cut, chosen[:, 2, :, :], chosen[:, 3, :, :], ALU.add)
                    link(last)
                    link(dve.tensor_tensor(slot, slot, cut, ALU.add))
                    dve.tensor_copy(mask3, slot).then_inc(r.mask, 1)
                else:
                    dve.tensor_tensor(mask3, chosen[:, 0, :, :], chosen[:, 1, :, :], ALU.add).then_inc(r.mask, 1)
                dve.wait_ge(r.exps, 1)
                total = small[:, 0, 0:NT] if experts >= NT else TOTAL
                link(dve.tensor_reduce(total, w, AX_X, ALU.add))
                link(dve.reciprocal(total, total))
                link(dve.tensor_scalar(total, total, 0.5, None, ALU.mult))
                link(dve.tensor_tensor(w, w, total[:, :, None].broadcast_to([P, NT, choices]), ALU.mult))
                dve.wait_ge(r.ranks, 1)
                counts, tiles, ends, start, ones = (small[:, i, :] for i in range(5))
                most = cap // P
                link(dve.tensor_scalar(counts, count, float(cap), None, ALU.min))
                above = slot.rearrange("p t e -> p (t e)")[:, 0:experts * most].rearrange("p (e m) -> p e m", m=most)
                link(dve.tensor_tensor(above, counts[:, :, None].broadcast_to([P, experts, most]),
                                       STEPS[:, None, 0:most].broadcast_to([P, experts, most]), ALU.is_gt))
                link(dve.tensor_reduce(tiles, above, AX_X, ALU.add))
                link(dve.memset(ones, 1.0))
                link(dve.tensor_tensor_scan(ends, ones, tiles, 0.0, ALU.mult, ALU.add))
                link(dve.tensor_tensor(start, ends, tiles, ALU.subtract))
                link(dve.tensor_scalar(start, start, float(P), float(TOK), ALU.mult, ALU.add))
                rank3 = rank.rearrange("p (t e) -> p t e", e=experts)
                if cap < TOK:
                    link(dve.tensor_scalar(cut, rank3, float(cap - 1), DROPPED, ALU.is_gt, ALU.mult))
                    link(dve.scalar_tensor_tensor(out=slot, in0=rank3, scalar=float(cap - 1), in1=cut,
                                                  op0=ALU.min, op1=ALU.add))
                    link(dve.tensor_tensor(slot, slot, start[:, None, :].broadcast_to([P, NT, experts]), ALU.add))
                else:
                    link(dve.tensor_tensor(slot, rank3, start[:, None, :].broadcast_to([P, NT, experts]), ALU.add))
                for k in range(choices):
                    last = dve.tensor_tensor(chosen[:, k, :, :], chosen[:, k, :, :], slot, ALU.mult)
                link(last)
                flat = slot.rearrange("p t e -> p (t e)")
                mine = flat[:, 0:choices * NT].rearrange("p (k t) -> p k t", k=choices)
                over = cut.rearrange("p t e -> p (t e)")[:, 0:choices * NT].rearrange("p (k t) -> p k t", k=choices)
                link(dve.tensor_reduce(mine, chosen, AX_X, ALU.add))
                if cap < TOK:
                    dve.tensor_scalar(over, mine, DROPPED, -DROPPED, ALU.is_ge, ALU.mult)
                    link(dve.tensor_copy(SLOT_IN[:, 0:choices, :], mine))
                    link(dve.tensor_tensor(mine, mine, over, ALU.add))
                    link(dve.tensor_copy(SLOT_OUT[:, 0:choices, :], mine))
                else:
                    dve.tensor_copy(SLOT_IN[:, 0:choices, :], mine)
                    link(dve.tensor_copy(SLOT_OUT[:, 0:choices, :], mine))
                b = Area(*area)
                past = b.take(routed, experts)[0:1, :, :]
                dve.tensor_tensor(past, IOTA_T[0:1, 0:routed, None].broadcast_to([1, routed, experts]),
                                  ends[0:1, None, :].broadcast_to([1, routed, experts]), ALU.is_ge).then_inc(r.slots, 1)
                dve.wait_ge(r.slots, 1)
                which = b.take(routed)[0:1, :]
                link(dve.tensor_reduce(which, past, AX_X, ALU.add))
                link(dve.tensor_scalar(which, which, float(experts - 1), 1.0, ALU.min, ALU.add))
                dve.tensor_scalar(W_AT[0:1, 1 + NT:1 + NT + routed], which, float(width), None, ALU.mult).then_inc(r.experts, 1)

            dve.wait_ge(consts_ready, 1)
            routing(r0, PS[:, 7, :], logits0, E0, K0, CAP0, R0, TOP, TOP_ID, TOP_IDF, SMALL, (W, RT0),
                    PS[:, 6, :], PS[:, 5, 0:E0], WIDTH0)

            dve.wait_ge(attn_w_loaded, 48)
            dve.wait_ge(r0.experts, 1)

            def bias_qvu(t, c):
                dve.wait_ge(qvu_ready, t + 1)
                if later(t, 2):
                    dve.wait_ge(qv_ready, t - 1)
                for lo, hi, bank in ((0, 2 * D, 0), (2 * D, 3 * D, 1)):
                    last = dve.tensor_tensor(PRE[:, c, lo:hi], PS[:, 2 * c + bank, 0:hi - lo], B_QVU[:, lo:hi], ALU.add)
                last.then_inc(pre_done, 1)
                dve.wait_ge(pre_done, t + 1)
                dve.tensor_scalar(ELU[:, c, :], PRE[:, c, 0:D], 0.0, None, ALU.min).then_inc(pre_ready, 1)

            def make_qvu(t, c):
                dve.wait_ge(th_ready, t + 1)
                if later(t, 2):
                    dve.wait_ge(kv_added, t - 1)
                dve.scalar_tensor_tensor(out=Q_S[:, c, :], in0=PRE[:, c, 0:D], scalar=0.0, in1=ELU[:, c, :],
                                         op0=ALU.max, op1=ALU.add).then_inc(elu_step, 1)
                dve.scalar_tensor_tensor(out=V_S[:, c, :], in0=TH[:, c, 0:D], scalar=1.0, in1=PRE[:, c, D:2 * D],
                                         op0=ALU.add, op1=ALU.mult)
                dve.scalar_tensor_tensor(out=U[:, t, :], in0=TH[:, c, D:2 * D], scalar=1.0, in1=PRE[:, c, 2 * D:3 * D],
                                         op0=ALU.add, op1=ALU.mult)
                dve.wait_ge(elu_step, t + 1)
                dve.tensor_scalar(Q_S[:, c, :], Q_S[:, c, :], -1.0, None, ALU.add).then_inc(qv_ready, 1)
                if isinstance(t, int) and t % (NT // BATCH) == NT // BATCH - 1:
                    keep_heads(t // (NT // BATCH))

            def keep_heads(b):
                dve.wait_ge(kv_added, (b + 1) * NT // BATCH)
                for k in range(KD):
                    last = dve.tensor_tensor(KV[:, b * KD + k, :], PS[:, 4 + k, 0:P], BLOCKS, ALU.mult)
                last.then_inc(kv_ready, 1)

            half = NT // BATCH
            for b in range(BATCH):
                pipeline(dve, half, 2, (0, lambda t, c: make_qvu(t + b * half, c)),
                         (1, lambda t, c: bias_qvu(t + b * half, c)))

            def centre(t, c):
                dve.wait_ge(o_dev, t + 1)
                dve.reciprocal(STAT[:, 2 + c % 2, 2:3], STAT[:, 2 + c % 2, 2:3]).then_inc(z_step, 1)
                if later(t, 2):
                    dve.wait_ge(z_turned, t - 1)
                dve.scalar_tensor_tensor(out=Z_S[:, c % 2, :], in0=PS[:, O_BANKS[c], 0:D], scalar=STAT[:, 2 + c % 2, 0:1],
                                         in1=LN_G, op0=ALU.subtract, op1=ALU.mult).then_inc(z_step, 1)

            def sums_o(t, c):
                dve.wait_ge(o_ready, t + 1)
                dve.bn_stats(STAT[:, c % 2, :], PS[:, O_BANKS[c], 0:D]).then_inc(o_sums, 1)

            def scale(t, c):
                dve.wait_ge(z_step, 3 * t + 2)
                dve.scalar_tensor_tensor(out=Z_S[:, c % 2, :], in0=Z_S[:, c % 2, :], scalar=STAT[:, 2 + c % 2, 2:3],
                                         in1=LN_B, op0=ALU.mult, op1=ALU.add).then_inc(z_step, 1)

            def stats_o(t, c):
                dve.wait_ge(consts_ready, 1)
                dve.wait_ge(o_sums, t + 1)
                dve.bn_aggr(STAT[:, 2 + c % 2, 0:2], STAT[:, c % 2, :]).then_inc(o_stats, 1)

            def times_u(t, c):
                dve.wait_ge(z_step, 3 * t + 3)
                dve.scalar_tensor_tensor(out=Z_S[:, c % 2, :], in0=Z_S[:, c % 2, :], scalar=0.5, in1=U[:, t, :],
                                         op0=ALU.mult, op1=ALU.mult).then_inc(z_ready, 1)

            def make_s(t, c):
                dve.wait_ge(wo_done, t + 1)
                dve.wait_ge(z_ready, t + 1)
                dve.tensor_tensor(U[:, t, :], PS[:, 4 + c % 2, 0:D], B_O, ALU.add).then_inc(s_ready, 1)

            pipeline(dve, NT, 4, (0, centre), (1, sums_o), (0, scale), (1, stats_o), (0, times_u), (-2, make_s))

            dve.wait_ge(zero_filled, 16 * R0 // 4)
            gate = mixture_vector(dve, m0, lambda c: PS[:, 1 + c % 2, I0:2 * I0], I0)
            copy_outs = mixture_outs(dve, m0)
            pipeline(dve, TILES0, UNROLL, (1, gate), (-1, copy_outs))

            xn_again = sem("xn_again")

            def base0(t, c):
                if later(t, 2):
                    dve.wait_ge(c0.acc, t - 1)
                else:
                    dve.wait_ge(m0.turned, TILES0)
                    dve.wait_ge(m0.hidden, TILES0)
                dve.tensor_scalar(BASE[:, c % 2, :], X[:, t, :], MEAN_VAR[:, t, 0:1], RSTD[:, bass.ds(t, 1)],
                                  ALU.subtract, ALU.mult).then_inc(xn_again, 1)
                dve.wait_ge(c0.shared[c], 4 * t - 4 * c + 16)
                dve.wait_ge(xn_again, t + 1)
                dve.scalar_tensor_tensor(out=BASE[:, c % 2, :], in0=GOT[:, c, 0, :], scalar=0.5, in1=BASE[:, c % 2, :],
                                         op0=ALU.mult, op1=ALU.add).then_inc(c0.base, 1)


            gated, sg_done = sem("gated"), sem("sg_done")

            def new_x(cm, t, c, s, gated, sg_done):
                i = c % 2
                dve.wait_ge(cm.tanh, t + 1)
                dve.scalar_tensor_tensor(out=TANH[:, i, :], in0=TANH[:, i, :], scalar=1.0, in1=PS[:, SUM_BANK + c, 0:D],
                                         op0=ALU.add, op1=ALU.mult).then_inc(gated, 1)
                dve.wait_ge(gated, t + 1)
                s(t, c).then_inc(sg_done, 1)
                dve.wait_ge(sg_done, t + 1)
                dve.scalar_tensor_tensor(out=X[:, t, :], in0=TANH[:, i, :], scalar=0.5, in1=X[:, t, :],
                                         op0=ALU.mult, op1=ALU.add).then_inc(cm.x, 1)

            xn1_made, n1, n1_sums = sem("xn1_made"), sem("n1"), sem("n1_sums")
            GROUP_STEPS = 1 + 1 + 14 + 1

            def norm1(t, i):
                if i % 4 != 3:
                    return
                first = t - 3
                then, n = chain(n1, first // 4 * GROUP_STEPS)
                dve.wait_ge(consts_ready, 1)
                dve.wait_ge(c0.x, t + 1)
                for j in range(4):
                    last = dve.bn_stats(STAT[:, j, :], X[:, first + j, :])
                last.then_inc(n1_sums, 4)
                dve.wait_ge(consts_ready, 1)
                dve.wait_ge(n1_sums, t + 1)
                for j in range(4):
                    last = dve.bn_aggr(AGGR[:, j, :], STAT[:, j, :])
                then(last)
                move(MEAN_VAR[:, bass.ds(first, 4), :], AGGR)
                then(dve.tensor_scalar(VARS[:, 0, :], AGGR[:, :, 1], EPS_LN, None, ALU.add))
                rsqrt(then, ROOTS[:, 0, :], VARS[:, 0, :], PRODS[:, 0, :])
                then(move(RSTD[:, bass.ds(first, 4)], ROOTS[:, 0, :]))
                assert n[0] == GROUP_STEPS
                for j in range(4):
                    u = first + j
                    if later(u, 4):
                        dve.wait_ge(c0.turned, u - 3)
                    else:
                        dve.wait_ge(m0.down, TILES0)
                        dve.wait_ge(m0.stored[0], 4 * TILES0)
                    dve.tensor_scalar(XN1_S[:, j, :], X[:, u, :], MEAN_VAR[:, u, 0:1], RSTD[:, bass.ds(u, 1)],
                                      ALU.subtract, ALU.mult).then_inc(xn1_made, 1)
                    dve.wait_ge(xn1_made, u + 1)
                    move(XN1[:, u, :], XN1_S[:, j, :]).then_inc(c0.xn, 1)

            pipeline(dve, NT, 4, (2, base0),
                     (0, lambda t, c: new_x(c0, t, c, lambda t, c: dve.tensor_tensor(
                         TANH[:, c % 2, :], TANH[:, c % 2, :], U[:, t, :], ALU.mult), gated, sg_done)),
                     (0, norm1))

            dve.wait_ge(a_exp, 1)
            dve.tensor_scalar(A_NEG, A_NEG, -1.0, None, ALU.mult).then_inc(a_ready, 1)
            routing(r1, PS[:, 7, :], c0.logits, E1, K1, TOK, R1, TOP1, TOP1_ID, TOP1_IDF, SMALL1, (MB.tensor, RT1),
                    PS[:, 6, 0:NT * E1], PS[:, 5, 0:E1], WIDTH1)

            for q in range(3):
                if q == 0:
                    dve.wait_ge(dr_ready, 4)
                link(dve.tensor_copy(BC_HI[0:96, :], BC[0:96, :]))
                part = BC3[32 * q:32 * q + 32, :]
                ins = dve.tensor_copy(part, BC_HI[32 * q:32 * q + 32, :])
                if q < 2:
                    link(dve.tensor_tensor(BC[0:96, :], BC[0:96, :], BC_HI[0:96, :], ALU.subtract))
                else:
                    ins.then_inc(bc3_ready, 1)
            for k in range(KD):
                for j in range(4):
                    n = 4 * k + j
                    dve.wait_ge(dl_psum, n + 1)
                    dve.tensor_scalar(DELTA[:, k, 512 * j:512 * j + 512], PS[:, 4 + n % 4, :], B_DT[:, k:k + 1], 0.0,
                                      ALU.add, ALU.max).then_inc(dl_max, 1)
            for k in range(KD):
                dve.wait_ge(dl_exp, 4 * (k + 1))
                dve.tensor_scalar(DU[:, k, :], DU[:, k, :], 1.0, None, ALU.add).then_inc(dl_step, 1)
            for k in range(KD):
                dve.wait_ge(dl_ln, k + 1)
                link(dve.tensor_tensor(DELTA[:, k, :], DELTA[:, k, :], DU[:, k, :], ALU.add))
                link(dve.tensor_tensor(DU[:, k, :], DELTA[:, k, :], XT[:, k, :], ALU.mult))
                ins = dve.tensor_scalar(XT[:, k, :], XT[:, k, :], D_SKIP[:, k:k + 1], None, ALU.mult)
            ins.then_inc(du_ready, 1)
            dve.wait_ge(du_ready, 1)

            def input_b(u, c):
                dve.wait_ge(b_spread, u + 2 - c % 2)
                if later(u, 2):
                    dve.wait_ge(y_added, u - 1)
                lo = (c // 2) * SEQ
                dve.tensor_tensor(Z[:, c % 2, :].rearrange("p (a b) -> p a b", a=2),
                                  DU[:, c % 2, lo:lo + SEQ].rearrange("p (a b) -> p a b", a=2),
                                  PS[:, B_BANK:B_BANK + 2, :], ALU.mult).then_inc(bu_ready, 1)

            def scan(u, c):
                dve.wait_ge(da_ready, u + 1)
                dve.wait_ge(bu_ready, u + 1)
                dve.tensor_tensor_scan(Z[:, c % 2, :], DA[:, c % 2, :], Z[:, c % 2, :], 0.0,
                                       ALU.mult, ALU.add).then_inc(scanned, 1)

            def add_y(u, c):
                dve.wait_ge(hc_ready, u + 1)
                if later(u, 2):
                    dve.wait_ge(y_added, u - 2)
                y = XT[:, c % 2, (c // 2) * SEQ:(c // 2 + 1) * SEQ]
                dve.tensor_tensor(y, y, Z[:, c % 2, :], ALU.add).then_inc(y_added, 1)

            gate = mixture_vector(dve, m1, lambda c: PS[:, 2, 0:H1P], H1P)
            pipeline(dve, TILES1, UNROLL, (-2, add_y), (0, input_b), (0, scan), (1, gate))
            for u in range(TILES1, UNITS + 2):
                if u - 2 >= TILES1:
                    add_y(u - 2, (u - 2) % 4)
                if u < UNITS:
                    input_b(u, u % 4)
                    scan(u, u % 4)

            gated1, sg1_done = sem("gated1"), sem("sg1_done")

            def s1(t, c):
                dve.wait_ge(c1.y_rows, t + 1)
                return dve.tensor_tensor(TANH[:, c % 2, :], TANH[:, c % 2, :], PS[:, Y_BANKS[c], 0:D], ALU.mult)

            pipeline(dve, NT, 4, (0, lambda t, c: new_x(c1, t, c, s1, gated1, sg1_done)))

        def mixture_tensor(pe, m, hidden, blocks, part, width, banks):
            bank = MIX_BANKS[m is m1]
            two = 2 if m is m0 else 1

            def turn(t, c):
                pe.wait_ge(m.loaded[c // 2], 4 * t - 4 * c + 16)
                if later(t, two):
                    pe.wait_ge(m.rows_t, t + 1 - two)
                for k in range(KD):
                    last = pe.transpose(PS[:, bank["rows"][c % 2], k * P:(k + 1) * P], ROWS[:, c, k * P:(k + 1) * P], IDENT)
                last.then_inc(m.turned, 1)

            slots = SLOTS0 if m is m0 else SLOTS1
            at = {}

            def load(first, n):
                return nc.values_load_multi_w_load_instructions(
                    W_AT[0:1, bass.ds(first + 1, n)], engines=[mybir.EngineType.PE], min_val=0,
                    max_val=(slots - 1) * width, skip_runtime_bounds_check_because="VectorE keeps the table in range")[1]

            def table(t, c):
                if not isinstance(t, int) and c == 0:
                    at.clear()
                    for j, value in enumerate(load(t - 1, UNROLL + 2)):
                        at[j - 1] = value

            def offset(t, step):
                if not isinstance(t, int):
                    return at[step]
                if t not in at:
                    n = min(UNROLL, (TILES0 if m is m0 else TILES1) - t)
                    for j, value in enumerate(load(t, n)):
                        at[t + j] = value
                return at[t]

            def up(t, c):
                e = offset(t, c or UNROLL)
                pe.wait_ge(m.rows_t, t + 1)
                if m is m0:
                    if later(t, 2):
                        pe.wait_ge(m.gated, t - 1)
                    for k in range(KD):
                        last = pe.matmul(PS[:, 1 + c % 2, 0:2 * hidden], ROWS_T[:, c % 2, k * P:(k + 1) * P],
                                         W[:, bass.ds(e + 2 * k * hidden, 2 * hidden)], start=(k == 0), stop=(k == KD - 1))
                else:
                    if later(t, 1):
                        pe.wait_ge(m.gated, t)
                    for half in range(2):
                        for k in range(KD):
                            last = pe.matmul(PS[:, 1 + half, 0:hidden], ROWS_T[:, c % 2, k * P:(k + 1) * P],
                                             W[:, bass.ds(e + (2 * k + half) * hidden, hidden)],
                                             start=(k == 0), stop=(k == KD - 1))
                last.then_inc(m.hidden, 1)

            def turn_hidden(t, c):
                pe.wait_ge(m.gated, t + 1)
                if later(t, 1):
                    pe.wait_ge(m.hid_t, t)
                for k in range(blocks):
                    last = pe.transpose(PS[0:part, bank["hid"], k * P:(k + 1) * P], HID[:, c % 2, k * part:(k + 1) * part], IDENT)
                last.then_inc(m.hid_turned, 1)

            def down(t, c):
                e = offset(t, -1 if c == UNROLL - 1 else c)
                pe.wait_ge(m.hid_t, t + 1)
                if later(t, two):
                    pe.wait_ge(m.outs, t + 1 - two)
                for k in range(blocks):
                    last = pe.matmul(PS[:, bank["outs"][c % 2], 0:D], HID_T[0:part, c % 2, k * P:(k + 1) * P],
                                     W[0:part, bass.ds(e + KD * 2 * hidden + k * D, D)],
                                     start=(k == 0), stop=(k == blocks - 1))
                last.then_inc(m.down, 1)

            return table, turn, up, turn_hidden, down

        @block.tensor
        def _(pe):
            pe.wait_ge(consts_ready, 1)

            def turn0(t, c):
                pe.wait_ge(h_ready, t + 1)
                if later(t, 2):
                    pe.wait_ge(evac0, t - 1)
                for i, rows in enumerate((XN_S, H_S)):
                    for k in range(KD):
                        last = pe.transpose(PS[:, c, i * D + k * P:i * D + (k + 1) * P],
                                            rows[:, c, k * P:(k + 1) * P], IDENT)
                last.then_inc(turned0, 1)

            def logits(t, c):
                pe.wait_ge(evac0, t + 1)
                for k in range(KD):
                    last = pe.matmul(PS[:, 7, bass.ds(t * E0, E0)], HT_S[:, c, k * P:(k + 1) * P], GATE0[:, k, :],
                                     start=(k == 0), stop=(k == KD - 1))
                last.then_inc(logits0, 1)

            pe.wait_ge(small_loaded, 32)
            pipeline(pe, NT, 2, (1, turn0), (0, logits))

            def ranks(r, area, experts, choices, rank, count):
                a = Area(*area)
                a.take(choices, NT, experts)
                a.take(NT, experts)
                mask = a.take(NT, experts).rearrange("p t e -> p (t e)")[:, 0:NT * experts // 2].bitcast(BF16)
                pe.wait_ge(r.mask, 1)
                pe.matmul(rank, BELOW, mask, start=True, stop=False)
                for i in range(NT - 1):
                    m = mask[:, i * experts:(i + 1) * experts]
                    pe.matmul(rank[:, (i + 1) * experts:].rearrange("p (t e) -> p t e", e=experts), ONES,
                              m[:, None, :].broadcast_to([P, NT - 1 - i, experts]), start=False, stop=(i == NT - 2))
                for i in range(NT):
                    last = pe.matmul(count, ONES, mask[:, i * experts:(i + 1) * experts],
                                     start=(i == 0), stop=(i == NT - 1))
                last.then_inc(r.ranks, 1)

            ranks(r0, (W, RT0), E0, K0, PS[:, 6, :], PS[:, 5, 0:E0])

            pe.wait_ge(attn_w_loaded, 48)
            pe.wait_ge(evac0, NT)

            def qvu(t, c):
                pe.wait_ge(xt_staged, t + 1)
                if later(t, 2):
                    pe.wait_ge(pre_ready, t - 1)
                for lo, hi, bank in ((0, 2 * D, 0), (2 * D, 3 * D, 1)):
                    for k in range(KD):
                        last = pe.matmul(PS[:, 2 * c + bank, 0:hi - lo], XT_S[:, c, k * P:(k + 1) * P],
                                         W_QVU[:, k, lo:hi], start=(k == 0), stop=(k == KD - 1))
                last.then_inc(qvu_ready, 1)

            half = NT // BATCH

            def add_kv(t, c):
                pe.wait_ge(qv_ready, t + 1)
                if later(t, 2):
                    pe.wait_ge(qt_saved, t - 1)
                if isinstance(t, int) and t == 0:
                    pe.wait_ge(r0.slots, 1)
                if isinstance(t, int) and t == half:
                    pe.wait_ge(kv_ready, 1)
                for k in range(KD):
                    last = pe.transpose(PS[:, 6 + c, k * P:(k + 1) * P], Q_S[:, c, k * P:(k + 1) * P], IDENT)
                last.then_inc(q_turned, 1)
                for k in range(KD):
                    last = pe.matmul(PS[:, 4 + k, 0:P], Q_S[:, c, k * P:(k + 1) * P], V_S[:, c, k * P:(k + 1) * P],
                                     start=(isinstance(t, int) and t % half == 0),
                                     stop=(isinstance(t, int) and t % half == half - 1), skip_group_check=True)
                last.then_inc(kv_added, 1)

            for b in range(BATCH):
                pipeline(pe, half, 2, (2, lambda t, c: qvu(t + b * half, c)), (0, lambda t, c: add_kv(t + b * half, c)))

            pe.wait_ge(kv_ready, 2)

            def out_heads(t, c):
                pe.wait_ge(qt_staged, t + 1)
                if later(t, 4):
                    pe.wait_ge(z_ready, t - 3)
                for k in range(KD):
                    last = pe.matmul(PS[:, O_BANKS[c], k * P:(k + 1) * P], QT_S[:, c % 2, k * P:(k + 1) * P],
                                     KV[:, t // half * KD + k, :], start=True, stop=True)
                last.then_inc(o_ready, 1)

            def turn_z(t, c):
                pe.wait_ge(z_ready, t + 1)
                if later(t, 2):
                    pe.wait_ge(zt_ready, t - 1)
                for k in range(KD):
                    last = pe.transpose(PS[:, 2 + c % 2, k * P:(k + 1) * P], Z_S[:, c % 2, k * P:(k + 1) * P], IDENT)
                last.then_inc(z_turned, 1)

            def out_proj(t, c):
                pe.wait_ge(zt_ready, t + 1)
                if later(t, 2):
                    pe.wait_ge(s_ready, t - 1)
                for k in range(KD):
                    last = pe.matmul(PS[:, 4 + c % 2, 0:D], ZT_S[:, c % 2, k * P:(k + 1) * P], W_O[:, k, :],
                                     start=(k == 0), stop=(k == KD - 1))
                last.then_inc(wo_done, 1)

            pipeline(pe, NT, 4, (2, out_heads), (0, turn_z), (-1, out_proj))

            pe.wait_ge(w0_loaded, 16)
            pe.wait_ge(s_ready, NT)
            pe.wait_ge(r0.experts, 1)
            table, turn, up, turn_hidden, down = mixture_tensor(pe, m0, I0, 1, P, WIDTH0, 2)

            def all_experts():
                pe.wait_ge(w0_late, 16 * 5)

            pipeline(pe, TILES0, UNROLL, (0, table), (2, turn), (1, up), (0, turn_hidden), (-1, down),
                     pause=(NT - UNROLL, all_experts))

            pe.wait_ge(small1_loaded, 96)
            pe.wait_ge(m0.outs, TILES0)

            def sum_rows(cm, t, c, choices):
                i = c % 2
                pe.wait_ge(cm.diag, t + 1)
                pe.wait_ge(cm.got[c], 4 * choices * (t - c) + 16 * choices)
                if later(t, 4):
                    pe.wait_ge(cm.x, t - 3)
                if cm is c0:
                    pe.wait_ge(c0.base, t + 1)
                    terms = [(IDENT, BASE[:, i, :])]
                else:
                    pe.wait_ge(c1.shared[c], 4 * t - 4 * c + 16)
                    terms = [(HALF, GOT[:, c, 0, :])]
                for k in range(choices):
                    terms.append((DIAG[:, i, k * P:(k + 1) * P], GOT[:, c, 1 + k, :]))
                for n, (weights, rows) in enumerate(terms):
                    last = pe.matmul(PS[:, SUM_BANK + c, 0:D], weights, rows, start=(n == 0), stop=(n == len(terms) - 1))
                last.then_inc(cm.acc, 1)

            def turn1(t, c):
                pe.wait_ge(c0.xn, t + 1)
                if later(t, 2):
                    pe.wait_ge(c0.xt, t - 1)
                for k in range(KD):
                    last = pe.transpose(PS[:, c % 2, k * P:(k + 1) * P], XN1_S[:, c, k * P:(k + 1) * P], IDENT)
                last.then_inc(c0.turned, 1)

            def logits1(t, c):
                pe.wait_ge(c0.xt, t + 1)
                for k in range(KD):
                    last = pe.matmul(PS[:, 7, bass.ds(t * E1, E1)], XT1_S[:, c % 2, k * P:(k + 1) * P], WR[:, k, :],
                                     start=(k == 0), stop=(k == KD - 1))
                last.then_inc(c0.logits, 1)

            pipeline(pe, NT, 4, (0, lambda t, c: sum_rows(c0, t, c, K0)), (-4, turn1), (-5, logits1))
            ranks(r1, (MB.tensor, RT1), E1, K1, PS[:, 6, 0:NT * E1], PS[:, 5, 0:E1])

            for j in range(4):
                if j >= 2:
                    pe.wait_ge(dr_ready, j - 1)
                for lo, hi, bank in ((0, RANK, j % 2), (RANK, RANK + 96, 2 + j % 2)):
                    for k in range(KD):
                        last = pe.matmul(PS[0:hi - lo, bank, :], W_XP[:, k, lo:hi], XT[:, k, 512 * j:512 * j + 512],
                                         start=(k == 0), stop=(k == KD - 1))
                last.then_inc(xz_ready, 1)
            pe.wait_ge(r1.slots, 1)
            for k in range(KD):
                for j in range(4):
                    n = 4 * k + j
                    if n < 4:
                        pe.wait_ge(dr_ready, j + 1)
                    else:
                        pe.wait_ge(act_step, n - 3)
                        pe.wait_ge(dl_max, n - 3)
                    pe.matmul(PS[:, 4 + n % 4, :], W_DT[:, k * P:(k + 1) * P], DELTA_R[:, 512 * j:512 * j + 512],
                              start=True, stop=True).then_inc(dl_psum, 1)

            pe.wait_ge(bc3_ready, 1)
            pe.wait_ge(dl_exp, 8)
            pe.wait_ge(dl_max, 8)
            pe.wait_ge(w1_loaded, 16 * SLOTS1)
            pe.wait_ge(r1.experts, 1)

            def spread(row, part, bank):
                return pe.matmul(PS[:, bank, :], PICK[0:96, bass.ds(row, 1)].broadcast_to([96, P]),
                                 BC3[0:96, part:part + 512], start=True, stop=True)

            def spread_b(u, c):
                if c % 2:
                    return
                if later(u, 2):
                    pe.wait_ge(bu_ready, u)
                for h in range(2):
                    last = spread((u - c) // 4, (c // 2) * SEQ + 512 * h, B_BANK + h)
                last.then_inc(b_spread, 2)

            def spread_c(u, c):
                if later(u, 1):
                    pe.wait_ge(c_copied, u)
                spread((u - c) // 4 + N_STATE, c * 512, C_BANK).then_inc(c_spread, 1)

            table, turn, up, turn_hidden, down = mixture_tensor(pe, m1, H1P, 3, HB, WIDTH1, 1)
            pipeline(pe, TILES1, UNROLL, (0, table), (2, turn), (1, up), (1, spread_b), (0, turn_hidden), (2, spread_c),
                     (-1, down))
            for u in range(TILES1, UNITS):
                spread_b(u, u % 4)
                spread_c(u, u % 4)

            pe.wait_ge(m1.outs, TILES1)

            def turn_y(t, c):
                pe.wait_ge(c1.y_staged, t + 1)
                if later(t, 4):
                    pe.wait_ge(c1.x, t - 3)
                for k in range(KD):
                    last = pe.transpose(PS[:, Y_BANKS[c], k * P:(k + 1) * P], XT1_S[:, c % 2, k * P:(k + 1) * P], IDENT)
                last.then_inc(c1.y_rows, 1)

            pipeline(pe, NT, 4, (1, turn_y), (0, lambda t, c: sum_rows(c1, t, c, K1)))


def kernel(**inputs):
    import numpy as np
    import concourse.bacc as bacc
    from concourse.bass_utils import run_bass_kernel_spmd

    g = {k: np.asarray(v) for k, v in inputs.items()}

    def blocks(w):
        return w.reshape(-1, P, w.shape[1]).transpose(1, 0, 2)

    def expert0(w13, w2):
        return np.concatenate([blocks(w13).reshape(P, -1), blocks(w2).reshape(P, -1)], axis=1)

    def expert1(w1, w3, w2):
        z = np.zeros((P, KD, 2, H1P), np.float32)
        z[:, :, 0, :H1] = blocks(w1.T)
        z[:, :, 1, :H1] = blocks(w3.T)
        d = np.zeros((H1P, D), np.float32)
        d[:H1] = w2.T
        e = np.zeros((P, 3, D), np.float32)
        e[:HB] = d.reshape(3, HB, D).transpose(1, 0, 2)
        return np.concatenate([z.reshape(P, -1), e.reshape(P, -1)], axis=1)

    shared0 = expert0(np.concatenate([g["L0_ffn_shared_gate_w"], g["L0_ffn_shared_up_w"]], axis=1),
                      g["L0_ffn_shared_down_w"])
    moe0 = np.concatenate([shared0] + [expert0(g["L0_ffn_w13"][e], g["L0_ffn_w2"][e]) for e in range(E0)], axis=1)
    shared1 = expert1(g["L1_ffn_sw1"], g["L1_ffn_sw3"], g["L1_ffn_sw2"])
    moe1 = np.concatenate([shared1] + [expert1(g["L1_ffn_ew1"][e], g["L1_ffn_ew3"][e], g["L1_ffn_ew2"][e])
                                       for e in range(E1)], axis=1)
    xp = g["L1_attn_W_xproj"].T
    bc = xp[:, RANK:]

    def halves(v):
        return v.reshape(KD, P, -1).transpose(1, 0, 2).reshape(P, -1)

    arrays = {
        "x": g["L0_attn_x"].reshape(NT, P, D).transpose(1, 0, 2),
        "w_qvu": blocks(np.concatenate([g["L0_attn_Wqk"], g["L0_attn_Wv"], g["L0_attn_Wu"]], axis=1)),
        "b_qvu": np.concatenate([g["L0_attn_bqk"], g["L0_attn_bv"], g["L0_attn_bu"]]),
        "w_o": blocks(g["L0_attn_Wo"]),
        "rows4": np.stack([g["L0_attn_bo"], g["L0_attn_ln_g"], g["L0_attn_ln_b"], g["L0_ffn_norm_w"]]),
        "gate0": blocks(g["L0_ffn_gate_w"].T),
        "moe0": moe0,
        "moe1": moe1,
        "w_xproj": blocks(np.concatenate([xp[:, :RANK], bc, bc, bc], axis=1)),
        "w_dt": g["L1_attn_W_dt"].T,
        "per_channel": np.concatenate([halves(g["L1_attn_b_dt"]), halves(g["L1_attn_D_param"]),
                                       halves(g["L1_attn_A_log"])], axis=1),
        "wr": blocks(g["L1_ffn_wr"].T),
    }
    arrays = {f"{k}_dram": np.ascontiguousarray(v) for k, v in arrays.items()}
    nc = bacc.Bacc("TRN2", target_bir_lowering=False, num_devices=1)
    args = [nc.dram_tensor(k, a.shape, mybir.dt.from_np(a.dtype), kind="ExternalInput").ap() for k, a in arrays.items()]
    out = nc.dram_tensor("out_dram", (P, NT, D), F32, kind="ExternalOutput").ap()
    two_layers(nc, *args, out)
    r = run_bass_kernel_spmd(nc, [arrays], core_ids=[0])
    return np.ascontiguousarray(r.results[0]["out_dram"].transpose(1, 0, 2)).reshape(BATCH, SEQ, D)
```

```python
from contextlib import ExitStack

import concourse.bass as bass
from concourse import mybir

F32 = mybir.dt.float32
BF16 = mybir.dt.bfloat16
I32 = mybir.dt.int32
U32 = mybir.dt.uint32
ALU = mybir.AluOpType
ACT = mybir.ActivationFunctionType
AX_X = mybir.AxisListType.X

P = 128
D = 256
KD = D // P
BATCH, SEQ = 2, 1024
TOK = BATCH * SEQ
NT = TOK // P
HEAD = 16

E0, K0 = 32, 4
CAP0 = 2 * TOK * K0 // E0
I0 = 128
E1, K1 = 8, 2
H1 = D * 4 // 3
HB = -(-H1 // 3)
H1P = 3 * HB
N_STATE = 16
RANK = 128

EPS_LN = 1e-5
EPS_RMS = 1e-6
DROPPED = float(1 << 20)


def routed_tiles(experts, choices, multiple):
    n = (TOK * choices + experts * (P - 1)) // P
    return -(-n // multiple) * multiple


UNROLL = 4
R0 = routed_tiles(E0, K0, UNROLL)
R1 = routed_tiles(E1, K1, UNROLL)
TILES0 = NT + R0
TILES1 = NT + R1
WIDTH0 = KD * 2 * I0 + D
WIDTH1 = KD * 2 * H1P + 3 * D
SLOTS0 = E0 + 1
SLOTS1 = E1 + 1
LATE0 = SLOTS0 - 13
UNITS = N_STATE * BATCH * KD


def later(t, k):
    assert isinstance(t, int) or t.min_val >= k, (t.min_val, k)
    return not isinstance(t, int) or t >= k


def pipeline(eng, n, unroll, *stages, pause=None):
    peel = 1 if min(lead for lead, _ in stages) >= 0 else 2
    def step(i, c):
        for lead, f in stages:
            if not isinstance(i, int) or 0 <= i + lead < n:
                f(i + lead, (c + lead) % unroll)

    for i in range(-max(lead for lead, _ in stages), peel * unroll):
        step(i, i)
    last = n - unroll
    cut = pause[0] // unroll if pause else peel
    for lo, hi in ((peel, cut), (cut, last // unroll)):
        if hi > lo:
            with eng.Fori(lo, hi, 1) as block:
                for c in range(unroll):
                    step(block * unroll + c, c)
        if pause and lo == peel:
            pause[1]()
    for i in range(last, n - min(lead for lead, _ in stages)):
        step(i, i)


def two_layers(nc, x, w_qvu, b_qvu, w_o, rows4, gate0, moe0, moe1, w_xproj, w_dt, per_channel, wr, out):
    rows0 = rows1 = nc.dram_tensor("rows", [TILES0 * P, D], F32, kind="Internal").ap()
    outs0 = nc.dram_tensor("outs0", [TILES0 * P, D], F32, kind="Internal").ap()
    outs1 = nc.dram_tensor("outs1", [TILES1 * P, D], F32, kind="Internal").ap()

    with ExitStack() as ctx:
        def sb(name, shape, dt=F32):
            return ctx.enter_context(nc.sbuf_tensor(name, shape, dt))

        def sem(name):
            return ctx.enter_context(nc.semaphore(name))

        class Area:
            def __init__(self, tensor, at=0):
                self.tensor, self.at = tensor, at

            def take(self, *shape, dt=F32, parts=P):
                n = 1
                for s in shape:
                    n *= s
                floats = n if dt in (F32, I32, U32) else n // 2
                v = self.tensor[0:parts, self.at:self.at + floats]
                self.at += floats
                if dt != F32:
                    v = v.bitcast(dt)
                if len(shape) == 2:
                    v = v.rearrange("p (a b) -> p a b", a=shape[0])
                if len(shape) == 3:
                    v = v.rearrange("p (a b c) -> p a b c", a=shape[0], b=shape[1])
                return v

        W = sb("W", [P, SLOTS0 * WIDTH0])
        X = sb("X", [P, NT, D])
        AR_H = sb("AR_H", [P, NT * D])
        AR_T = sb("AR_T", [P, NT * D])
        AR_U = sb("AR_U", [P, NT * D])
        R = sb("R", [P, 6144])
        H = AR_H[:, :].rearrange("p (t d) -> p t d", t=NT)
        U = AR_U[:, :].rearrange("p (t d) -> p t d", t=NT)
        XT = AR_T[:, :].rearrange("p (k n) -> p k n", k=KD)
        DELTA = AR_H[:, :].rearrange("p (k n) -> p k n", k=KD)
        DU = AR_U[:, :].rearrange("p (k n) -> p k n", k=KD)

        MB_SIZE = 1024 + 512 + 2 * H1P + 2 * 3 * P + 1024
        MB = Area(sb("MB", [P, MB_SIZE]))
        ROWS = MB.take(4, D)
        ROWS_T = MB.take(2, D)
        HID = MB.take(2, H1P)
        HID_T = MB.take(2, 3 * P)
        OUTS = MB.take(4, D)

        MC = Area(MB.tensor)
        DIAG = MC.take(2, K0 * P)
        BASE = MC.take(2, D)
        XN1_S = MC.take(4, D)
        TOP1 = MC.take(NT, 8)
        TOP1_ID = MC.take(NT, 8, dt=U32)
        TOP1_IDF = MC.take(NT, 8)
        SMALL1 = MC.take(5, E1)
        RT1 = MC.at
        assert RT1 + 4 * NT * E1 <= MB_SIZE

        CO_SIZE = 1266
        CO = Area(sb("CO", [P, CO_SIZE]))
        IDENT = CO.take(P)
        HALF = CO.take(P)
        BLOCKS = CO.take(P)
        BELOW = CO.take(P, dt=BF16)
        ONES = CO.take(P, dt=BF16)
        PICK = CO.take(2 * N_STATE, dt=BF16)
        IOTA_E = CO.take(E0)
        IOTA_P = CO.take(1)
        EXPERT = CO.take(1)
        STEPS = CO.take(NT)
        WEIGHT = CO.take(NT, K0)
        SLOT_IN = CO.take(K0, NT, dt=I32)
        SLOT_OUT = CO.take(K0, NT, dt=I32)
        W_AT = CO.take(TILES0 + 4, dt=I32)
        STAT = CO.take(4, 6)
        AGGR = CO.take(4, 2)
        MEAN_VAR = CO.take(NT, 2)
        RSTD = CO.take(NT)
        TOTAL = CO.take(NT)
        RRMS = CO.take(NT)
        A_NEG = CO.take(KD, N_STATE)
        B_DT = CO.take(KD)
        D_SKIP = CO.take(KD)
        VARS = CO.take(4)
        ROOTS = CO.take(4)
        PRODS = CO.take(4)
        EPS_COL = CO.take(1)
        assert CO.at <= CO_SIZE

        RA = Area(R)
        W_QVU = RA.take(KD, 3 * D)
        W_O = RA.take(KD, D)
        GATE0 = RA.take(KD, E0)
        B_QVU = RA.take(3 * D)
        ROW4 = RA.take(4, D)
        B_O, LN_G, LN_B, NORM_W = (ROW4[:, i, :] for i in range(4))
        TOP = RA.take(NT, 8)
        TOP_ID = RA.take(NT, 8, dt=U32)
        TOP_IDF = RA.take(NT, 8)
        SMALL = RA.take(5, E0)
        assert RA.at <= 6144
        RC = Area(R)
        GOT = RC.take(4, K0 + 1, D)
        TANH = RC.take(2, D)
        XT1_S = RC.take(2, D)
        assert RC.at <= 6144
        RS = Area(R)
        C_SB = RS.take(2, SEQ)
        DA = RS.take(2, SEQ)
        Z = RS.take(2, SEQ)
        RD = Area(R)
        DELTA_R = RD.take(TOK)
        BC = RD.take(TOK)
        BC_HI = RD.take(TOK, dt=BF16)
        assert RD.at <= 6144

        WA = Area(W, LATE0 * WIDTH0)
        XT_S = WA.take(2, D)
        PRE = WA.take(2, 3 * D)
        ELU = WA.take(2, D)
        TH = WA.take(2, 2 * D)
        Q_S = WA.take(2, D)
        V_S = WA.take(2, D)
        QT_S = WA.take(2, D)
        Z_S = WA.take(2, D)
        ZT_S = WA.take(2, D)
        KV = WA.take(BATCH * KD, P)
        RT0 = WA.at
        STATS_X = WA.take(NT, 6)
        VARS_X = WA.take(2, NT)
        ROOTS_X = WA.take(2, NT)
        PRODS_X = WA.take(2, NT)
        assert RT0 + R0 * (E0 + 1) <= SLOTS0 * WIDTH0

        WN = Area(W, LATE0 * WIDTH0)
        XN_S = WN.take(4, D)
        H_S = WN.take(4, D)
        HT_S = WN.take(4, D)
        assert WN.at <= RT0

        WB = Area(W, SLOTS1 * WIDTH1)
        XN1 = WB.take(NT, D)
        W_DT = WB.take(D)
        W_XP = WB.take(KD, RANK + 96)
        WR = WB.take(KD, E1)
        BC3 = WB.take(TOK, dt=BF16)
        assert WB.at <= SLOTS0 * WIDTH0

        WC = Area(W)
        GOT1 = WC.take(NT, K1 + 1, D)
        GATED1 = WC.take(NT, D)
        TAIL = UNITS - TILES1
        SUM_LAG = 2

        PS = ctx.enter_context(nc.psum_tensor("PS", [P, 8, 512], F32))

        MIX_BANKS = ({"rows": (0, 5), "up": (1, 2), "hid": 3, "outs": (4, 6)},
                     {"rows": (0, 0), "up": (1, 1), "hid": 3, "outs": (4, 4)})
        TABLE_BANK = 7
        O_BANKS = (0, 1, 6, 7)
        SUM_BANK = 2
        Y_BANKS = (0, 5, 6, 7)
        SUM1_BANK = 1
        C_BANK, B_BANK = 5, 6

        x_loaded, small_loaded, attn_w_loaded = [sem(f"x_loaded{g}") for g in range(4)], sem("small_loaded"), sem("attn_w_loaded")
        w0_loaded, w0_late = sem("w0_loaded"), sem("w0_late")
        zero_ready, zero_filled = sem("zero_ready"), sem("zero_filled")
        consts_ready, consts_cleared = sem("consts_ready"), sem("consts_cleared")
        rows_copied, h_stored = sem("rows_copied"), sem("h_stored")
        v_step = sem("v_step")
        h_ready, turned0, evac0, logits0 = sem("h_ready"), sem("turned0"), sem("evac0"), sem("logits0")
        st_a, xn_s_done = sem("st_a"), sem("xn_s_done")

        class Routing:
            def __init__(self, n):
                self.diff, self.exps = sem(f"diff{n}"), sem(f"exps{n}")
                self.mask, self.ranks = sem(f"mask{n}"), sem(f"ranks{n}")
                self.slots, self.experts = sem(f"slots{n}"), sem(f"experts{n}")
                self.expert, self.row = sem(f"expert{n}"), sem(f"row{n}")
                self.scattered = sem(f"scattered{n}")

        r0, r1 = Routing(0), Routing(1)

        xt_staged, qvu_ready, pre_ready, th_ready = sem("xt_staged"), sem("qvu_ready"), sem("pre_ready"), sem("th_ready")
        pre_done, elu_step, qv_ready = sem("pre_done"), sem("elu_step"), sem("qv_ready")
        kv_added, q_turned, qt_saved, kv_ready = sem("kv_added"), sem("q_turned"), sem("qt_saved"), sem("kv_ready")
        qt_staged, o_ready, z_step, z_ready = sem("qt_staged"), sem("o_ready"), sem("z_step"), sem("z_ready")
        z_turned, zt_ready, wo_done, s_ready = sem("z_turned"), sem("zt_ready"), sem("wo_done"), sem("s_ready")

        o_sums, o_stats, o_dev = sem("o_sums"), sem("o_stats"), sem("o_dev")

        class Mixture:
            def __init__(self, n):
                self.loaded = [sem(f"m{n}_loaded{i}") for i in range(2)]
                self.stored = [sem(f"m{n}_stored{i}") for i in range(2)]
                self.turned = sem(f"m{n}_turned")
                self.rows_t = sem(f"m{n}_rows_t")
                self.hidden = sem(f"m{n}_hidden")
                self.tanh = sem(f"m{n}_tanh")
                self.half = sem(f"m{n}_half")
                self.gated = sem(f"m{n}_gated")
                self.hid_turned = sem(f"m{n}_hid_turned")
                self.hid_t = sem(f"m{n}_hid_t")
                self.down = sem(f"m{n}_down")
                self.outs = sem(f"m{n}_outs")

        m0, m1 = Mixture(0), Mixture(1)

        class Combine:
            def __init__(self, n):
                self.got = [sem(f"c{n}_got{i}") for i in range(4)]
                self.shared = [sem(f"c{n}_shared{i}") for i in range(4)]
                self.diag = sem(f"c{n}_diag")
                self.acc = sem(f"c{n}_acc")
                self.tanh = sem(f"c{n}_tanh")
                self.x = sem(f"c{n}_x")
                if n == 0:
                    self.base = sem("c0_base")
                    self.xn = sem("c0_xn")
                    self.turned = sem("c0_turned")
                    self.xt = sem("c0_xt")
                    self.logits = sem("c0_logits")
                else:
                    self.y_rows = sem("c1_y_rows")

        c0, c1 = Combine(0), Combine(1)
        gated, sg_done = sem("gated"), sem("sg_done")
        w1_loaded, small1_loaded, xn1_stored, out_stored = sem("w1_loaded"), sem("small1_loaded"), sem("xn1_stored"), sem("out_stored")
        xz_ready, dr_ready, bc3_ready = sem("xz_ready"), sem("dr_ready"), sem("bc3_ready")
        y_started = sem("y_started")
        dl_psum, dl_exp, dl_max, dl_ln, du_ready = sem("dl_psum"), sem("dl_exp"), sem("dl_max"), sem("dl_ln"), sem("du_ready")
        a_exp, a_ready, act_step = sem("a_exp"), sem("a_ready"), sem("act_step")
        c_spread, b_spread, c_copied, da_ready = sem("c_spread"), sem("b_spread"), sem("c_copied"), sem("da_ready")
        bu_ready, scanned, hc_ready = sem("bu_ready"), sem("scanned"), sem("hc_ready")
        y_added = sem("y0_added"), sem("y1_added")

        block = ctx.enter_context(nc.Block())

        def tiles_of(dram, t, n):
            return dram[bass.ds(t * P, n * P), :].rearrange("(j p) d -> p j d", p=P)

        def sums_and_y(first, on_sum, on_y):
            y = 0
            for t in range(first, NT):
                on_sum(t)
                while y <= t and y < 2 * (t - first) + 2:
                    on_y(y)
                    y += 1
            for t in range(y, NT):
                on_y(t)

        @block.sync
        def _(sp):
            for g in range(4):
                sp.dma_start(X[:, 4 * g:4 * g + 4, :], x[:, 4 * g:4 * g + 4, :]).then_inc(x_loaded[g], 16)
            sp.dma_start(ROW4, rows4[None, :, :].broadcast_to([P, 4, D])).then_inc(small_loaded, 16)
            sp.dma_start(GATE0, gate0).then_inc(small_loaded, 16)
            sp.dma_start(W_QVU, w_qvu).then_inc(attn_w_loaded, 16)
            sp.dma_start(B_QVU, b_qvu[None, :].broadcast_to([P, 3 * D])).then_inc(attn_w_loaded, 16)
            sp.dma_start(W_O, w_o).then_inc(attn_w_loaded, 16)
            sp.wait_ge(zero_ready, 1)
            for j in range(R0 // 4):
                sp.dma_start(tiles_of(rows0, NT + 4 * j, 4), OUTS).then_inc(zero_filled, 16)
            sp.dma_start(W[:, 0:LATE0 * WIDTH0], moe0[:, 0:LATE0 * WIDTH0]).then_inc(w0_loaded, 16)
            sp.wait_ge(rows_copied, NT)
            sp.dma_start(tiles_of(rows0, 0, NT), H).then_inc(h_stored, 16)
            sp.wait_ge(s_ready, NT)

            def load_w0(first, n):
                at = bass.ds(first * WIDTH0, n * WIDTH0)
                sp.dma_start(W[:, at], moe0[:, at]).then_inc(w0_late, 16)

            def run_mixture(m, rows, outs, tiles, first_ready, routed_ready, between):
                def load(t, c):
                    if later(t, 4):
                        sp.wait_ge(m.turned, t - 2)
                    sp.dma_start(ROWS[:, c:c + 2, :], tiles_of(rows, t, 2)).then_inc(m.loaded[c // 2], 16)

                def store(t, c):
                    sp.wait_ge(m.outs, t + 2)
                    sp.dma_start(tiles_of(outs, t, 2), OUTS[:, c:c + 2, :]).then_inc(m.stored[c // 2], 16)

                first_ready()
                load(0, 0)
                load(2, 2)
                between(0)
                load(4, 0)
                between(1)
                load(6, 2)
                between(2)

                def four_tiles(b):
                    store(4 * b - 4, 0)
                    load(4 * b + 4, 0)
                    store(4 * b - 2, 2)
                    load(4 * b + 6, 2)

                with sp.Fori(1, NT // 4 - 1, 1) as b:
                    four_tiles(b)
                    between(b + 2)
                routed_ready()
                with sp.Fori(NT // 4 - 1, tiles // 4 - 1, 1) as b:
                    four_tiles(b)
                for t in (tiles - 8, tiles - 6, tiles - 4, tiles - 2):
                    store(t, t % 4)

            def combine(c, outs, between):
                for i in range(4):
                    sp.dma_start(GOT[:, i, 0, :], outs[i * P:(i + 1) * P, :]).then_inc(c.shared[i], 16)
                with sp.Fori(1, NT // 4, 1) as b:
                    between(b)
                    for i in range(4):
                        sp.wait_ge(c.acc, 4 * b + (i - 3))
                        sp.dma_start(GOT[:, i, 0, :], outs[bass.ds((4 * b + i) * P, P), :]).then_inc(c.shared[i], 16)

            def load_w1(slot):
                at = bass.ds(slot * WIDTH1, WIDTH1)
                sp.dma_start(W[:, at], moe1[:, at]).then_inc(w1_loaded, 16)

            def first0():
                sp.wait_ge(h_stored, 16)

            def routed0():
                sp.wait_ge(zero_filled, 16 * R0 // 4)
                sp.wait_ge(r0.scattered, 16 * NT * K0)
                sp.wait_ge(h_stored, 16)

            late_slots = SLOTS0 - LATE0 - 5

            def late_w0(step):
                if isinstance(step, int):
                    load_w0(LATE0 + (0, 3, 4)[step], (3, 1, 1)[step])
                else:
                    load_w0(LATE0 + 5 + (step - 3) * (late_slots // 2), late_slots // 2)

            assert late_slots % 2 == 0
            run_mixture(m0, rows0, outs0, TILES0, first0, routed0, late_w0)

            sp.wait_ge(m0.down, TILES0)
            sp.dma_start(W_DT, w_dt).then_inc(small1_loaded, 16)
            sp.dma_start(W_XP, w_xproj).then_inc(small1_loaded, 16)
            sp.dma_start(WR, wr).then_inc(small1_loaded, 16)
            sp.dma_start(A_NEG, per_channel[:, 2 * KD:].rearrange("p (k n) -> p k n", k=KD)).then_inc(small1_loaded, 16)
            sp.dma_start(B_DT, per_channel[:, 0:KD]).then_inc(small1_loaded, 16)
            sp.dma_start(D_SKIP, per_channel[:, KD:2 * KD]).then_inc(small1_loaded, 16)
            for i in range(2):
                sp.wait_ge(m0.stored[i], 4 * TILES0)
            def two_w1(b):
                load_w1(2 * b - 2)
                load_w1(2 * b - 1)

            combine(c0, outs0, two_w1)
            for slot in range(NT // 2 - 2, SLOTS1):
                load_w1(slot)
            sp.wait_ge(c0.xn, NT)
            sp.dma_start(tiles_of(rows1, 0, NT), XN1).then_inc(xn1_stored, 16)

            def first1():
                sp.wait_ge(xn1_stored, 16)

            def routed1():
                sp.wait_ge(r1.scattered, 16 * NT * K1)

            run_mixture(m1, rows1, outs1, TILES1, first1, routed1, lambda step: None)
            for i in range(2):
                sp.wait_ge(m1.stored[i], 4 * TILES1)
            sp.dma_start(GOT1[:, :, 0, :], tiles_of(outs1, 0, NT)).then_inc(c1.shared[0], 16)
            for g in range(4):
                sp.wait_ge(c1.x, 4 * g + 4)
                sp.dma_start(out[:, 4 * g:4 * g + 4, :], X[:, 4 * g:4 * g + 4, :]).then_inc(out_stored, 16)
            sp.wait_ge(out_stored, 64)

        def pair(u, c):
            return (u - c) // 4 * 2 + c // 2

        def add_y(eng, half, u, c):
            if c % 2 != half:
                return
            eng.wait_ge(hc_ready, u + 1)
            if not later(u, 4):
                eng.wait_ge(y_started, KD)
            else:
                eng.wait_ge(y_added[half], pair(u, c))
            y = XT[:, half, (c // 2) * SEQ:(c // 2 + 1) * SEQ]
            eng.tensor_tensor(y, y, Z[:, half, :], ALU.add).then_inc(y_added[half], 1)

        @block.gpsimd
        def _(pool):
            pool.memset(OUTS, 0.0).then_inc(zero_ready, 1)
            pool.memset(IDENT, 0.0)
            pool.memset(HALF, 0.0)
            pool.memset(BLOCKS, 0.5)
            pool.memset(BELOW, 0.0)
            pool.memset(ONES, 1.0)
            pool.memset(EPS_COL, EPS_LN)
            pool.memset(W_AT[0:1, :], 0)
            pool.memset(PICK, 0.0).then_inc(consts_cleared, 1)
            pool.wait_ge(consts_cleared, 1)
            pool.affine_select(out=IDENT, in_=IDENT, compare_op=ALU.not_equal, fill=1.0, base=0,
                               pattern=[[-1, P]], channel_multiplier=1)
            pool.affine_select(out=HALF, in_=HALF, compare_op=ALU.not_equal, fill=0.5, base=0,
                               pattern=[[-1, P]], channel_multiplier=1)
            pool.affine_select(out=BELOW, in_=BELOW, compare_op=ALU.is_ge, fill=1.0, base=0,
                               pattern=[[-1, P]], channel_multiplier=1)
            v = BLOCKS.rearrange("p (b j) -> p b j", j=HEAD)
            pool.affine_select(out=v, in_=v, compare_op=ALU.is_ge, fill=0.0, base=0,
                               pattern=[[-HEAD, P // HEAD], [0, HEAD]], channel_multiplier=1).then_inc(consts_cleared, 1)
            pool.wait_ge(consts_cleared, 2)
            for q in range(3):
                w = PICK[32 * q:32 * q + 32, :]
                pool.affine_select(out=w, in_=w, compare_op=ALU.not_equal, fill=1.0, base=0,
                                   pattern=[[-1, 2 * N_STATE]], channel_multiplier=1).then_inc(consts_cleared, 1)
                pool.wait_ge(consts_cleared, 3 + q)
            pool.affine_select(out=v, in_=v, compare_op=ALU.is_ge, fill=0.0, base=HEAD - 1,
                               pattern=[[HEAD, P // HEAD], [0, HEAD]], channel_multiplier=-1)
            pool.iota(IOTA_E, pattern=[[1, E0]], base=0, channel_multiplier=0, allow_small_or_imprecise_dtypes=True)
            pool.iota(IOTA_P, pattern=[[0, 1]], base=0, channel_multiplier=1, allow_small_or_imprecise_dtypes=True)
            pool.iota(STEPS, pattern=[[P, NT]], base=0, channel_multiplier=0,
                      allow_small_or_imprecise_dtypes=True).then_inc(consts_ready, 1)

            def keep_h(t, c):
                pool.wait_ge(h_ready, t + 1)
                pool.wait_ge(consts_ready, 1)
                pool.tensor_copy(H[:, bass.ds(t, 1), :], H_S[:, c:c + 1, :]).then_inc(rows_copied, 1)

            pipeline(pool, NT, 4, (0, keep_h))

            def scatter(src, rows, choices, tiles, done):
                for t in range(NT):
                    for k in range(choices):
                        pool.indirect_dma_start(
                            out=rows, out_offset=bass.IndirectOffsetOnAxis(ap=SLOT_IN[:, k, t:t + 1], axis=0),
                            in_=src[:, t, :], in_offset=None,
                            bounds_check=tiles * P - 1, oob_is_err=False).then_inc(done, 16)

            pool.wait_ge(r0.slots, 1)
            pool.wait_ge(zero_filled, 16 * R0 // 4)
            pool.wait_ge(rows_copied, NT)
            scatter(H, rows0, K0, TILES0, r0.scattered)

            def gather(c, outs, choices):
                for t in range(NT):
                    i = t % 4
                    if t >= 4:
                        pool.wait_ge(c.acc, t - 3)
                    for k in range(choices):
                        pool.indirect_dma_start(
                            out=GOT[:, i, 1 + k, :], out_offset=None, in_=outs,
                            in_offset=bass.IndirectOffsetOnAxis(ap=SLOT_OUT[:, k, t:t + 1], axis=0)).then_inc(c.got[i], 16)

            for i in range(2):
                pool.wait_ge(m0.stored[i], 4 * TILES0)
            gather(c0, outs0, K0)

            pool.wait_ge(r1.slots, 1)
            pool.wait_ge(c0.xn, NT)
            scatter(XN1, rows1, K1, TILES1, r1.scattered)

            def times_c(u, c):
                pool.wait_ge(scanned, u + 1)
                pool.wait_ge(c_copied, u + 2 - c % 2)
                pool.tensor_tensor(Z[:, c % 2, :], Z[:, c % 2, :], C_SB[:, c // 2, :], ALU.mult).then_inc(hc_ready, 1)

            pipeline(pool, TILES1, 4, (0, times_c), (0, lambda u, c: add_y(pool, 1, u, c)))

            def gather1(t):
                if t >= 4:
                    pool.wait_ge(c1.acc, t - 3)
                for k in range(K1):
                    pool.indirect_dma_start(
                        out=GOT1[:, t, 1 + k, :], out_offset=None, in_=outs1,
                        in_offset=bass.IndirectOffsetOnAxis(ap=SLOT_OUT[:, k, t:t + 1], axis=0)).then_inc(c1.got[t % 4], 16)

            for v in range(TAIL):
                times_c(TILES1 + v, (TILES1 + v) % 4)
                if v == 0:
                    for i in range(2):
                        pool.wait_ge(m1.stored[i], 4 * TILES1)
                gather1(v)
            for t in range(TAIL, NT):
                gather1(t)

        def mixture_outs(eng, m):
            bank = MIX_BANKS[m is m1]

            def copy_outs(t, c):
                eng.wait_ge(m.down, t + 1)
                if later(t, 4):
                    eng.wait_ge(m.stored[c // 2], 4 * t - 4 * c)
                src = PS[:, bank["outs"][c % 2], 0:D]
                copy = eng.tensor_copy(OUTS[:, c, :], src) if m is m0 else eng.copy(OUTS[:, c, :], src)
                copy.then_inc(m.outs, 1)

            return copy_outs

        def mixture_scalar(act, m, hidden, blocks, part):
            bank = MIX_BANKS[m is m1]

            def copy_rows_t(t, c):
                act.wait_ge(m.turned, t + 1)
                if later(t, 2):
                    act.wait_ge(m.hidden, t - 1)
                act.copy(ROWS_T[:, c % 2, :], PS[:, bank["rows"][c % 2], 0:D]).then_inc(m.rows_t, 1)

            def tanh(t, c):
                act.wait_ge(m.hidden, t + 1)
                if later(t, 2):
                    act.wait_ge(m.hid_turned, t - 1)
                act.activation(HID[:, c % 2, 0:hidden], PS[:, bank["up"][c % 2], 0:hidden], ACT.Tanh,
                               scale=0.5).then_inc(m.tanh, 1)

            def copy_hid_t(t, c):
                act.wait_ge(m.hid_turned, t + 1)
                if later(t, 2):
                    act.wait_ge(m.down, t - 1)
                act.copy(HID_T[0:part, c % 2, 0:blocks * P], PS[0:part, bank["hid"], 0:blocks * P]).then_inc(m.hid_t, 1)

            return copy_rows_t, tanh, copy_hid_t

        @block.scalar
        def _(act):
            def save_t(t, c):
                act.wait_ge(turned0, t + 1)
                if later(t, 4):
                    act.wait_ge(logits0, t - 3)
                act.copy(HT_S[:, c, :], PS[:, c, D:2 * D])
                act.copy(XT[:, :, bass.ds(t * P, P)],
                         PS[:, c, 0:D].rearrange("p (k n) -> p k n", k=KD)).then_inc(evac0, 1)

            pipeline(act, NT, 4, (0, save_t))

            def softmax(r, top, choices):
                act.wait_ge(r.diff, 1)
                act.activation(WEIGHT[:, :, 0:choices], WEIGHT[:, :, 0:choices], ACT.Exp).then_inc(r.exps, 1)

            softmax(r0, TOP, K0)

            half = NT // BATCH

            def stage_xt(t, c):
                c = c % 2
                act.wait_ge(evac0, NT)
                if later(t, 2):
                    act.wait_ge(qvu_ready, t - 1)
                act.copy(XT_S[:, c, :].rearrange("p (k n) -> p k n", k=KD),
                         XT[:, :, bass.ds(t * P, P)]).then_inc(xt_staged, 1)

            def tables(t, c):
                c = c % 2
                act.wait_ge(pre_ready, t + 1)
                if later(t, 2):
                    act.wait_ge(qv_ready, t - 1)
                act.activation(TH[:, c, :], PRE[:, c, D:3 * D], ACT.Tanh, scale=0.5)
                act.activation(ELU[:, c, :], ELU[:, c, :], ACT.Exp).then_inc(th_ready, 1)

            def save_qt(t, c):
                c = c % 2
                act.wait_ge(evac0, NT)
                act.wait_ge(q_turned, t + 1)
                act.wait_ge(xt_staged, t + 1)
                act.copy(XT[:, :, bass.ds(t * P, P)],
                         PS[:, 6 + c, 0:D].rearrange("p (k n) -> p k n", k=KD)).then_inc(qt_saved, 1)

            pipeline(act, NT, 4, (3, stage_xt), (0, save_qt), (2, tables))

            def stage_qt(t, c):
                if later(t, 2):
                    act.wait_ge(o_ready, t - 1)
                act.wait_ge(qt_saved, NT)
                act.copy(QT_S[:, c % 2, :].rearrange("p (k n) -> p k n", k=KD),
                         XT[:, :, bass.ds(t * P, P)]).then_inc(qt_staged, 1)

            def copy_zt(t, c):
                act.wait_ge(z_turned, t + 1)
                if later(t, 2):
                    act.wait_ge(wo_done, t - 1)
                act.copy(ZT_S[:, c % 2, :], PS[:, 2 + c % 2, 0:D]).then_inc(zt_ready, 1)

            def deviation(t, c):
                act.wait_ge(o_stats, t + 1)
                act.activation(STAT[:, 2 + c % 2, 2:3], STAT[:, 2 + c % 2, 1:2], ACT.Sqrt, bias=EPS_COL).then_inc(o_dev, 1)

            pipeline(act, NT, 4, (3, stage_qt), (1, deviation), (0, copy_zt))

            rows_t, tanh, hid_t = mixture_scalar(act, m0, I0, 1, P)
            pipeline(act, TILES0, UNROLL, (2, rows_t), (1, tanh), (0, hid_t))

            def tanh_acc(cm, t, c):
                act.wait_ge(cm.acc, t + 1)
                if later(t, 2):
                    act.wait_ge(cm.x, t - 1)
                act.activation(TANH[:, c % 2, :], PS[:, SUM_BANK + c, 0:D], ACT.Tanh, scale=0.5).then_inc(cm.tanh, 1)

            def diagonals(cm, m, t, i, choices, tiles):
                act.wait_ge(consts_ready, 1)
                if later(t, 2):
                    act.wait_ge(cm.acc, t - 1)
                else:
                    act.wait_ge(m.turned, tiles)
                for k in range(choices):
                    last = act.activation(DIAG[:, i, k * P:(k + 1) * P], IDENT, ACT.Copy, scale=WEIGHT[:, t, k:k + 1])
                last.then_inc(cm.diag, 1)

            def save_xt1(t, i):
                act.wait_ge(c0.turned, t + 1)
                if later(t, 2):
                    act.wait_ge(c0.logits, t - 1)
                act.copy(XT1_S[:, i, :], PS[:, i, 0:D])
                act.copy(XT[:, :, bass.ds(t * P, P)],
                         PS[:, i, 0:D].rearrange("p (k n) -> p k n", k=KD)).then_inc(c0.xt, 1)

            pipeline(act, NT, 4, (2, lambda t, c: diagonals(c0, m0, t, c % 2, K0, TILES0)),
                     (0, lambda t, c: tanh_acc(c0, t, c)), (-4, lambda t, c: save_xt1(t, c % 2)))

            act.wait_ge(small1_loaded, 96)
            act.activation(A_NEG, A_NEG, ACT.Exp).then_inc(a_exp, 1)
            for j in range(4):
                if j == 2:
                    softmax(r1, TOP1, K1)
                act.wait_ge(xz_ready, j + 1)
                act.copy(DELTA_R[:, 512 * j:512 * j + 512], PS[:, j % 2, :])
                act.copy(BC[0:96, 512 * j:512 * j + 512], PS[0:96, 2 + j % 2, :]).then_inc(dr_ready, 1)
            for n in range(8):
                k, j = n // 4, n % 4
                act.wait_ge(dl_max, n + 1)
                part = DU[:, k, 512 * j:512 * j + 512]
                act.activation(part, PS[:, j, :], ACT.Abs, bias=B_DT[:, k:k + 1]).then_inc(act_step, 1)
                act.wait_ge(act_step, n + 1)
                act.activation(part, part, ACT.Exp, scale=-1.0).then_inc(dl_exp, 1)
            act.wait_ge(dl_exp, 8)
            for k in range(KD):
                act.activation(DU[:, k, :], DU[:, k, :], ACT.Ln, bias=1.0).then_inc(dl_ln, 1)

            for k in range(KD):
                act.wait_ge(du_ready, k + 1)
                act.activation(XT[:, k, :], XT[:, k, :], ACT.Copy, scale=D_SKIP[:, k:k + 1]).then_inc(y_started, 1)

            def copy_c(u, c):
                act.wait_ge(c_spread, u + 1)
                if later(u, 4):
                    act.wait_ge(hc_ready, u - c % 2 - 2)
                h = 512 * (c % 2)
                act.copy(C_SB[:, c // 2, h:h + 512], PS[:, C_BANK, :]).then_inc(c_copied, 1)

            def decay(u, c):
                act.wait_ge(a_ready, 1)
                act.wait_ge(du_ready, KD)
                if later(u, 2):
                    act.wait_ge(scanned, u - 1)
                n = (u - c) // 4
                act.activation(DA[:, c % 2, :], DELTA[:, c % 2, (c // 2) * SEQ:(c // 2 + 1) * SEQ], ACT.Exp,
                               scale=A_NEG[:, c % 2, bass.ds(n, 1)]).then_inc(da_ready, 1)

            rows_t, tanh, hid_t = mixture_scalar(act, m1, H1P, 3, HB)
            copy_outs = mixture_outs(act, m1)
            pipeline(act, TILES1, UNROLL, (2, rows_t), (1, decay), (1, tanh), (0, hid_t), (2, copy_c), (-1, copy_outs))

            def tanh1(t):
                act.wait_ge(c1.acc, t + 1)
                act.activation(GATED1[:, t, :], PS[:, SUM1_BANK + t % 4, 0:D], ACT.Tanh, scale=0.5).then_inc(c1.tanh, 1)

            diagonals(c1, m1, 0, 0, K1, TILES1)
            for v in range(NT + SUM_LAG):
                if v < TAIL:
                    copy_c(TILES1 + v, (TILES1 + v) % 4)
                    decay(TILES1 + v, (TILES1 + v) % 4)
                t = v - SUM_LAG
                if t >= 0:
                    if t + 1 < NT:
                        diagonals(c1, m1, t + 1, (t + 1) % 2, K1, TILES1)
                    tanh1(t)

        def mixture_vector(dve, m, up, scale_cols):
            bank = MIX_BANKS[m is m1]

            def gate(t, c):
                dve.wait_ge(m.tanh, t + 1)
                hid = HID[:, c % 2, 0:scale_cols]
                dve.scalar_tensor_tensor(out=hid, in0=hid, scalar=1.0, in1=PS[:, bank["up"][c % 2], 0:scale_cols],
                                         op0=ALU.add, op1=ALU.mult).then_inc(m.half, 1)
                dve.wait_ge(m.half, t + 1)
                dve.tensor_tensor(hid, hid, up(c), ALU.mult).then_inc(m.gated, 1)

            return gate

        @block.vector
        def _(dve):
            steps = [0]

            def link(ins):
                steps[0] += 1
                ins.then_inc(v_step, 1)
                dve.wait_ge(v_step, steps[0])


            def chain(sem, start):
                n = [0]

                def then(ins):
                    n[0] += 1
                    ins.then_inc(sem, 1)
                    dve.wait_ge(consts_ready, 1)
                    dve.wait_ge(sem, start + n[0])
                return then, n

            def rsqrt(then, y, v, tmp):
                then(dve.tensor_scalar(y.bitcast(I32), v.bitcast(I32), 1, None, ALU.logical_shift_right))
                then(dve.tensor_scalar(y.bitcast(I32), y.bitcast(I32), -1.0, float(0x5f3759df), ALU.mult, ALU.add))
                for _ in range(3):
                    then(dve.tensor_tensor(tmp, y, y, ALU.mult))
                    then(dve.tensor_tensor(tmp, tmp, v, ALU.mult))
                    then(dve.tensor_scalar(tmp, tmp, -0.5, 1.5, ALU.mult, ALU.add))
                    then(dve.tensor_tensor(y, y, tmp, ALU.mult))

            def move(out, src):
                return dve.tensor_scalar(out, src, 1.0, None, ALU.mult)

            for t in range(NT):
                if t % 4 == 0:
                    dve.wait_ge(x_loaded[t // 4], 16)
                dve.bn_stats(STATS_X[:, t, :], X[:, t, :]).then_inc(st_a, 1)
            for t in range(NT):
                dve.wait_ge(st_a, t + 1)
                last = dve.bn_aggr(MEAN_VAR[:, t, :], STATS_X[:, t, :])
            link(last)
            var = MEAN_VAR[:, :, 1]
            link(dve.tensor_scalar(VARS_X[:, 0, :], var, EPS_LN, None, ALU.add))
            link(dve.reciprocal(PRODS_X[:, 0, :], VARS_X[:, 0, :]))
            link(dve.tensor_tensor(VARS_X[:, 1, :], PRODS_X[:, 0, :], var, ALU.mult))
            link(dve.tensor_scalar(VARS_X[:, 1, :], VARS_X[:, 1, :], EPS_RMS, None, ALU.add))
            rsqrt(link, ROOTS_X, VARS_X, PRODS_X)
            dve.tensor_copy(RSTD, ROOTS_X[:, 0, :])
            link(dve.tensor_copy(RRMS, ROOTS_X[:, 1, :]))
            dve.wait_ge(small_loaded, 32)

            def rows_xn(t, c):
                if later(t, 4):
                    dve.wait_ge(turned0, t - 3)
                dve.tensor_scalar(XN_S[:, c, :], X[:, t, :], MEAN_VAR[:, t, 0:1], RSTD[:, bass.ds(t, 1)],
                                  ALU.subtract, ALU.mult).then_inc(xn_s_done, 1)

            def rows_h(t, c):
                if later(t, 4):
                    dve.wait_ge(rows_copied, t - 3)
                dve.wait_ge(xn_s_done, t + 1)
                dve.scalar_tensor_tensor(out=H_S[:, c, :], in0=XN_S[:, c, :], scalar=RRMS[:, bass.ds(t, 1)],
                                         in1=NORM_W, op0=ALU.mult, op1=ALU.mult).then_inc(h_ready, 1)

            pipeline(dve, NT, 4, (1, rows_xn), (0, rows_h))

            def maps(area, experts, choices):
                a = Area(*area)
                chosen = a.take(choices, NT, experts)
                slot = a.take(NT, experts)
                cut = a.take(NT, experts)
                mask = cut.rearrange("p t e -> p (t e)")[:, 0:NT * experts // 2].bitcast(BF16)
                return chosen, slot, cut, mask

            def choose(r, logits, logits_ready, experts, choices, top, top_id, top_idf, area):
                dve.wait_ge(logits_ready, NT)

                for t in range(NT):
                    link(dve.max(top[:, t, :], logits[:, t * experts:(t + 1) * experts]))
                    last = dve.max_index(top_id[:, t, :], top[:, t, :], logits[:, t * experts:(t + 1) * experts])
                link(last)
                chosen, slot, cut, mask = maps(area, experts, choices)
                w = WEIGHT[:, :, 0:choices]
                dve.tensor_tensor(w, top[:, :, 0:choices], top[:, :, 0:1].broadcast_to([P, NT, choices]),
                                  ALU.subtract).then_inc(r.diff, 1)
                link(dve.tensor_copy(top_idf, top_id))
                for k in range(choices):
                    last = dve.tensor_tensor(chosen[:, k, :, :], IOTA_E[:, None, 0:experts].broadcast_to([P, NT, experts]),
                                             top_idf[:, :, k:k + 1].broadcast_to([P, NT, experts]), ALU.is_equal)
                link(last)
                mask3 = mask.rearrange("p (t e) -> p t e", e=experts)
                if choices == 4:
                    dve.tensor_tensor(slot, chosen[:, 0, :, :], chosen[:, 1, :, :], ALU.add)
                    last = dve.tensor_tensor(cut, chosen[:, 2, :, :], chosen[:, 3, :, :], ALU.add)
                    link(last)
                    link(dve.tensor_tensor(slot, slot, cut, ALU.add))
                    dve.tensor_copy(mask3, slot).then_inc(r.mask, 1)
                else:
                    dve.tensor_tensor(mask3, chosen[:, 0, :, :], chosen[:, 1, :, :], ALU.add).then_inc(r.mask, 1)

            def place(r, experts, choices, cap, small, area, rank, count, width):
                chosen, slot, cut, _ = maps(area, experts, choices)
                w = WEIGHT[:, :, 0:choices]
                dve.wait_ge(r.exps, 1)
                total = small[:, 0, 0:NT] if experts >= NT else TOTAL
                link(dve.tensor_reduce(total, w, AX_X, ALU.add))
                link(dve.reciprocal(total, total))
                link(dve.tensor_scalar(total, total, 0.5, None, ALU.mult))
                link(dve.tensor_tensor(w, w, total[:, :, None].broadcast_to([P, NT, choices]), ALU.mult))
                dve.wait_ge(r.ranks, 1)
                counts, tiles, ends, start, ones = (small[:, i, :] for i in range(5))
                most = cap // P
                link(dve.tensor_scalar(counts, count, float(cap), None, ALU.min))
                above = slot.rearrange("p t e -> p (t e)")[:, 0:experts * most].rearrange("p (e m) -> p e m", m=most)
                link(dve.tensor_tensor(above, counts[:, :, None].broadcast_to([P, experts, most]),
                                       STEPS[:, None, 0:most].broadcast_to([P, experts, most]), ALU.is_gt))
                link(dve.tensor_reduce(tiles, above, AX_X, ALU.add))
                link(dve.memset(ones, 1.0))
                link(dve.tensor_tensor_scan(ends, ones, tiles, 0.0, ALU.mult, ALU.add))
                link(dve.tensor_tensor(start, ends, tiles, ALU.subtract))
                link(dve.tensor_scalar(start, start, float(P), float(TOK), ALU.mult, ALU.add))
                rank3 = rank.rearrange("p (t e) -> p t e", e=experts)
                if cap < TOK:
                    link(dve.tensor_scalar(cut, rank3, float(cap - 1), DROPPED, ALU.is_gt, ALU.mult))
                    link(dve.scalar_tensor_tensor(out=slot, in0=rank3, scalar=float(cap - 1), in1=cut,
                                                  op0=ALU.min, op1=ALU.add))
                    link(dve.tensor_tensor(slot, slot, start[:, None, :].broadcast_to([P, NT, experts]), ALU.add))
                else:
                    link(dve.tensor_tensor(slot, rank3, start[:, None, :].broadcast_to([P, NT, experts]), ALU.add))
                for k in range(choices):
                    last = dve.tensor_tensor(chosen[:, k, :, :], chosen[:, k, :, :], slot, ALU.mult)
                link(last)
                flat = slot.rearrange("p t e -> p (t e)")
                mine = flat[:, 0:choices * NT].rearrange("p (k t) -> p k t", k=choices)
                over = cut.rearrange("p t e -> p (t e)")[:, 0:choices * NT].rearrange("p (k t) -> p k t", k=choices)
                link(dve.tensor_reduce(mine, chosen, AX_X, ALU.add))
                if cap < TOK:
                    dve.tensor_scalar(over, mine, DROPPED, -DROPPED, ALU.is_ge, ALU.mult)
                    link(dve.tensor_copy(SLOT_IN[:, 0:choices, :], mine))
                    link(dve.tensor_tensor(mine, mine, over, ALU.add))
                    link(dve.tensor_copy(SLOT_OUT[:, 0:choices, :], mine))
                else:
                    dve.tensor_copy(SLOT_IN[:, 0:choices, :], mine)
                    link(dve.tensor_copy(SLOT_OUT[:, 0:choices, :], mine))
                b = Area(*area)
                past, at = b.take(experts), b.take(1)
                dve.tensor_tensor(past, IOTA_P.broadcast_to([P, experts]), ends, ALU.is_ge).then_inc(r.slots, 1)
                dve.wait_ge(r.slots, 1)
                link(dve.tensor_reduce(at, past, AX_X, ALU.add))
                link(dve.tensor_scalar(at, at, float(experts - 1), 1.0, ALU.min, ALU.add))
                dve.tensor_scalar(EXPERT, at, float(width), None, ALU.mult).then_inc(r.expert, 1)

            def table(r, routed):
                dve.wait_ge(r.row, 1)
                dve.tensor_copy(W_AT[0:1, 1 + NT:1 + NT + routed], PS[0:1, TABLE_BANK, 0:routed]).then_inc(r.experts, 1)

            dve.wait_ge(consts_ready, 1)
            choose(r0, PS[:, 7, :], logits0, E0, K0, TOP, TOP_ID, TOP_IDF, (W, RT0))
            place(r0, E0, K0, CAP0, SMALL, (W, RT0), PS[:, 6, :], PS[:, 5, 0:E0], WIDTH0)

            dve.wait_ge(attn_w_loaded, 48)
            dve.wait_ge(rows_copied, NT)
            dve.wait_ge(r0.expert, 1)

            def bias_qvu(t, c):
                dve.wait_ge(qvu_ready, t + 1)
                if later(t, 2):
                    dve.wait_ge(qv_ready, t - 1)
                for lo, hi, bank in ((0, 2 * D, 0), (2 * D, 3 * D, 1)):
                    last = dve.tensor_tensor(PRE[:, c, lo:hi], PS[:, 2 * c + bank, 0:hi - lo], B_QVU[:, lo:hi], ALU.add)
                last.then_inc(pre_done, 1)
                dve.wait_ge(pre_done, t + 1)
                dve.tensor_scalar(ELU[:, c, :], PRE[:, c, 0:D], 0.0, None, ALU.min).then_inc(pre_ready, 1)

            def make_qvu(t, c):
                dve.wait_ge(th_ready, t + 1)
                if later(t, 2):
                    dve.wait_ge(kv_added, t - 1)
                dve.scalar_tensor_tensor(out=Q_S[:, c, :], in0=PRE[:, c, 0:D], scalar=0.0, in1=ELU[:, c, :],
                                         op0=ALU.max, op1=ALU.add).then_inc(elu_step, 1)
                dve.scalar_tensor_tensor(out=V_S[:, c, :], in0=TH[:, c, 0:D], scalar=1.0, in1=PRE[:, c, D:2 * D],
                                         op0=ALU.add, op1=ALU.mult)
                dve.scalar_tensor_tensor(out=U[:, t, :], in0=TH[:, c, D:2 * D], scalar=1.0, in1=PRE[:, c, 2 * D:3 * D],
                                         op0=ALU.add, op1=ALU.mult)
                dve.wait_ge(elu_step, t + 1)
                dve.tensor_scalar(Q_S[:, c, :], Q_S[:, c, :], -1.0, None, ALU.add).then_inc(qv_ready, 1)
                if isinstance(t, int) and t % (NT // BATCH) == NT // BATCH - 1:
                    keep_heads(t // (NT // BATCH))

            def keep_heads(b):
                dve.wait_ge(kv_added, (b + 1) * NT // BATCH)
                for k in range(KD):
                    last = dve.tensor_tensor(KV[:, b * KD + k, :], PS[:, 4 + k, 0:P], BLOCKS, ALU.mult)
                last.then_inc(kv_ready, 1)

            half = NT // BATCH
            for b in range(BATCH):
                pipeline(dve, half, 2, (0, lambda t, c: make_qvu(t + b * half, c)),
                         (2, lambda t, c: bias_qvu(t + b * half, c)))

            def centre(t, c):
                dve.wait_ge(o_dev, t + 1)
                dve.reciprocal(STAT[:, 2 + c % 2, 2:3], STAT[:, 2 + c % 2, 2:3]).then_inc(z_step, 1)
                if later(t, 2):
                    dve.wait_ge(z_turned, t - 1)
                dve.scalar_tensor_tensor(out=Z_S[:, c % 2, :], in0=PS[:, O_BANKS[c], 0:D], scalar=STAT[:, 2 + c % 2, 0:1],
                                         in1=LN_G, op0=ALU.subtract, op1=ALU.mult).then_inc(z_step, 1)

            def sums_o(t, c):
                dve.wait_ge(o_ready, t + 1)
                dve.bn_stats(STAT[:, c % 2, :], PS[:, O_BANKS[c], 0:D]).then_inc(o_sums, 1)

            def scale(t, c):
                dve.wait_ge(z_step, 3 * t + 2)
                dve.scalar_tensor_tensor(out=Z_S[:, c % 2, :], in0=Z_S[:, c % 2, :], scalar=STAT[:, 2 + c % 2, 2:3],
                                         in1=LN_B, op0=ALU.mult, op1=ALU.add).then_inc(z_step, 1)

            def stats_o(t, c):
                dve.wait_ge(consts_ready, 1)
                dve.wait_ge(o_sums, t + 1)
                dve.bn_aggr(STAT[:, 2 + c % 2, 0:2], STAT[:, c % 2, :]).then_inc(o_stats, 1)

            def times_u(t, c):
                dve.wait_ge(z_step, 3 * t + 3)
                dve.scalar_tensor_tensor(out=Z_S[:, c % 2, :], in0=Z_S[:, c % 2, :], scalar=0.5, in1=U[:, t, :],
                                         op0=ALU.mult, op1=ALU.mult).then_inc(z_ready, 1)

            def make_s(t, c):
                dve.wait_ge(wo_done, t + 1)
                dve.wait_ge(z_ready, t + 1)
                dve.tensor_tensor(U[:, t, :], PS[:, 4 + c % 2, 0:D], B_O, ALU.add).then_inc(s_ready, 1)

            pipeline(dve, NT, 4, (0, centre), (1, sums_o), (0, scale), (1, stats_o), (0, times_u), (-2, make_s))

            dve.wait_ge(zero_filled, 16 * R0 // 4)
            table(r0, R0)
            gate = mixture_vector(dve, m0, lambda c: PS[:, 1 + c % 2, I0:2 * I0], I0)
            copy_outs = mixture_outs(dve, m0)
            pipeline(dve, TILES0, UNROLL, (1, gate), (-1, copy_outs))

            xn_again = sem("xn_again")

            def base0(t, c):
                if later(t, 2):
                    dve.wait_ge(c0.acc, t - 1)
                else:
                    dve.wait_ge(m0.turned, TILES0)
                    dve.wait_ge(m0.hidden, TILES0)
                dve.tensor_scalar(BASE[:, c % 2, :], X[:, t, :], MEAN_VAR[:, t, 0:1], RSTD[:, bass.ds(t, 1)],
                                  ALU.subtract, ALU.mult).then_inc(xn_again, 1)
                dve.wait_ge(c0.shared[c], 4 * t - 4 * c + 16)
                dve.wait_ge(xn_again, t + 1)
                dve.scalar_tensor_tensor(out=BASE[:, c % 2, :], in0=GOT[:, c, 0, :], scalar=0.5, in1=BASE[:, c % 2, :],
                                         op0=ALU.mult, op1=ALU.add).then_inc(c0.base, 1)



            def new_x(cm, t, c, s):
                i = c % 2
                dve.wait_ge(cm.tanh, t + 1)
                dve.scalar_tensor_tensor(out=TANH[:, i, :], in0=TANH[:, i, :], scalar=1.0, in1=PS[:, SUM_BANK + c, 0:D],
                                         op0=ALU.add, op1=ALU.mult).then_inc(gated, 1)
                dve.wait_ge(gated, t + 1)
                s(t, c).then_inc(sg_done, 1)
                dve.wait_ge(sg_done, t + 1)
                dve.scalar_tensor_tensor(out=X[:, t, :], in0=TANH[:, i, :], scalar=0.5, in1=X[:, t, :],
                                         op0=ALU.mult, op1=ALU.add).then_inc(cm.x, 1)

            xn1_made, n1, n1_sums = sem("xn1_made"), sem("n1"), sem("n1_sums")
            GROUP_STEPS = 1 + 1 + 14 + 1

            def norm1(t, i):
                if i % 4 != 3:
                    return
                first = t - 3
                then, n = chain(n1, first // 4 * GROUP_STEPS)
                dve.wait_ge(consts_ready, 1)
                dve.wait_ge(c0.x, t + 1)
                for j in range(4):
                    last = dve.bn_stats(STAT[:, j, :], X[:, first + j, :])
                last.then_inc(n1_sums, 4)
                dve.wait_ge(consts_ready, 1)
                dve.wait_ge(n1_sums, t + 1)
                for j in range(4):
                    last = dve.bn_aggr(AGGR[:, j, :], STAT[:, j, :])
                then(last)
                move(MEAN_VAR[:, bass.ds(first, 4), :], AGGR)
                then(dve.tensor_scalar(VARS, AGGR[:, :, 1], EPS_LN, None, ALU.add))
                rsqrt(then, ROOTS, VARS, PRODS)
                then(move(RSTD[:, bass.ds(first, 4)], ROOTS))
                assert n[0] == GROUP_STEPS
                for j in range(4):
                    u = first + j
                    if later(u, 4):
                        dve.wait_ge(c0.turned, u - 3)
                    else:
                        dve.wait_ge(m0.down, TILES0)
                        dve.wait_ge(m0.stored[0], 4 * TILES0)
                    dve.tensor_scalar(XN1_S[:, j, :], X[:, u, :], MEAN_VAR[:, u, 0:1], RSTD[:, bass.ds(u, 1)],
                                      ALU.subtract, ALU.mult).then_inc(xn1_made, 1)
                    dve.wait_ge(xn1_made, u + 1)
                    move(XN1[:, u, :], XN1_S[:, j, :]).then_inc(c0.xn, 1)

            pipeline(dve, NT, 4, (2, base0),
                     (0, lambda t, c: new_x(c0, t, c, lambda t, c: dve.tensor_tensor(
                         TANH[:, c % 2, :], TANH[:, c % 2, :], U[:, t, :], ALU.mult))),
                     (0, norm1))

            dve.wait_ge(a_exp, 1)
            dve.tensor_scalar(A_NEG, A_NEG, -1.0, None, ALU.mult).then_inc(a_ready, 1)
            choose(r1, PS[:, 7, :], c0.logits, E1, K1, TOP1, TOP1_ID, TOP1_IDF, (MB.tensor, RT1))

            place(r1, E1, K1, TOK, SMALL1, (MB.tensor, RT1), PS[:, 6, 0:NT * E1], PS[:, 5, 0:E1], WIDTH1)

            def positive_part(n):
                k, j = n // 4, n % 4
                dve.wait_ge(dl_psum, n + 1)
                dve.tensor_scalar(DELTA[:, k, 512 * j:512 * j + 512], PS[:, j, :], B_DT[:, k:k + 1], 0.0,
                                  ALU.add, ALU.max).then_inc(dl_max, 1)

            def bc_part(q):
                if q == 0:
                    dve.wait_ge(dr_ready, 4)
                link(dve.tensor_copy(BC_HI[0:96, :], BC[0:96, :]))
                dve.tensor_copy(BC3[32 * q:32 * q + 32, :], BC_HI[32 * q:32 * q + 32, :]).then_inc(bc3_ready, 1)
                if q < 2:
                    link(dve.tensor_tensor(BC[0:96, :], BC[0:96, :], BC_HI[0:96, :], ALU.subtract))
                    dve.wait_ge(bc3_ready, q + 1)

            for n in range(4):
                positive_part(n)
            bc_part(0)
            positive_part(4)
            positive_part(5)
            bc_part(1)
            positive_part(6)
            positive_part(7)
            bc_part(2)
            for k in range(KD):
                dve.wait_ge(dl_ln, k + 1)
                link(dve.tensor_tensor(DELTA[:, k, :], DELTA[:, k, :], DU[:, k, :], ALU.add))
                dve.tensor_tensor(DU[:, k, :], DELTA[:, k, :], XT[:, k, :], ALU.mult).then_inc(du_ready, 1)
            dve.wait_ge(du_ready, KD)

            def input_b(u, c):
                dve.wait_ge(b_spread, u + 2 - c % 2)
                if later(u, 2):
                    dve.wait_ge(y_added[c % 2], pair(u, c))
                lo = (c // 2) * SEQ
                dve.tensor_tensor(Z[:, c % 2, :].rearrange("p (a b) -> p a b", a=2),
                                  DU[:, c % 2, lo:lo + SEQ].rearrange("p (a b) -> p a b", a=2),
                                  PS[:, B_BANK:B_BANK + 2, :], ALU.mult).then_inc(bu_ready, 1)

            def scan(u, c):
                dve.wait_ge(da_ready, u + 1)
                dve.wait_ge(bu_ready, u + 1)
                dve.tensor_tensor_scan(Z[:, c % 2, :], DA[:, c % 2, :], Z[:, c % 2, :], 0.0,
                                       ALU.mult, ALU.add).then_inc(scanned, 1)

            table(r1, R1)
            gate = mixture_vector(dve, m1, lambda c: PS[:, 2, 0:H1P], H1P)
            pipeline(dve, TILES1, UNROLL, (-2, lambda u, c: add_y(dve, 0, u, c)), (0, input_b), (0, scan), (1, gate))

            def gate1(t):
                dve.wait_ge(c1.tanh, t + 1)
                dve.scalar_tensor_tensor(out=GATED1[:, t, :], in0=GATED1[:, t, :], scalar=1.0,
                                         in1=PS[:, SUM1_BANK + t % 4, 0:D], op0=ALU.add, op1=ALU.mult).then_inc(gated, 1)

            def x_out(t):
                dve.wait_ge(c1.y_rows, t + 1)
                dve.wait_ge(gated, NT + t + 1)
                dve.tensor_tensor(GATED1[:, t, :], GATED1[:, t, :], PS[:, Y_BANKS[t % 4], 0:D], ALU.mult).then_inc(sg_done, 1)
                dve.wait_ge(sg_done, NT + t + 1)
                dve.scalar_tensor_tensor(out=X[:, t, :], in0=GATED1[:, t, :], scalar=0.5, in1=X[:, t, :],
                                         op0=ALU.mult, op1=ALU.add).then_inc(c1.x, 1)

            for v in range(TAIL + 2):
                u = TILES1 + v
                if v >= 2:
                    add_y(dve, u % 2, u - 2, (u - 2) % 4)
                if v < TAIL:
                    input_b(u, u % 4)
                    scan(u, u % 4)
                if v > SUM_LAG:
                    gate1(v - SUM_LAG - 1)
            sums_and_y(TAIL + 2 - SUM_LAG - 1, gate1, x_out)

        def mixture_tensor(pe, m, hidden, blocks, part, width, banks):
            bank = MIX_BANKS[m is m1]
            two = 2 if m is m0 else 1

            def turn(t, c):
                pe.wait_ge(m.loaded[c // 2], 4 * t - 4 * c + 16)
                if later(t, two):
                    pe.wait_ge(m.rows_t, t + 1 - two)
                for k in range(KD):
                    last = pe.transpose(PS[:, bank["rows"][c % 2], k * P:(k + 1) * P], ROWS[:, c, k * P:(k + 1) * P], IDENT)
                last.then_inc(m.turned, 1)

            slots = SLOTS0 if m is m0 else SLOTS1
            at = {}

            def load(first, n):
                return nc.values_load_multi_w_load_instructions(
                    W_AT[0:1, bass.ds(first + 1, n)], engines=[mybir.EngineType.PE], min_val=0,
                    max_val=(slots - 1) * width, skip_runtime_bounds_check_because="VectorE keeps the table in range")[1]

            def table(t, c):
                if not isinstance(t, int) and c == 0:
                    at.clear()
                    for j, value in enumerate(load(t - 1, UNROLL + 2)):
                        at[j - 1] = value

            def offset(t, step):
                if not isinstance(t, int):
                    return at[step]
                if t not in at:
                    n = min(UNROLL, (TILES0 if m is m0 else TILES1) - t)
                    for j, value in enumerate(load(t, n)):
                        at[t + j] = value
                return at[t]

            def up(t, c):
                e = offset(t, c or UNROLL)
                pe.wait_ge(m.rows_t, t + 1)
                if m is m0:
                    if later(t, 2):
                        pe.wait_ge(m.gated, t - 1)
                    for k in range(KD):
                        last = pe.matmul(PS[:, 1 + c % 2, 0:2 * hidden], ROWS_T[:, c % 2, k * P:(k + 1) * P],
                                         W[:, bass.ds(e + 2 * k * hidden, 2 * hidden)], start=(k == 0), stop=(k == KD - 1))
                else:
                    if later(t, 1):
                        pe.wait_ge(m.gated, t)
                    for half in range(2):
                        for k in range(KD):
                            last = pe.matmul(PS[:, 1 + half, 0:hidden], ROWS_T[:, c % 2, k * P:(k + 1) * P],
                                             W[:, bass.ds(e + (2 * k + half) * hidden, hidden)],
                                             start=(k == 0), stop=(k == KD - 1))
                last.then_inc(m.hidden, 1)

            def turn_hidden(t, c):
                pe.wait_ge(m.gated, t + 1)
                if later(t, 1):
                    pe.wait_ge(m.hid_t, t)
                for k in range(blocks):
                    last = pe.transpose(PS[0:part, bank["hid"], k * P:(k + 1) * P], HID[:, c % 2, k * part:(k + 1) * part], IDENT)
                last.then_inc(m.hid_turned, 1)

            def down(t, c):
                e = offset(t, -1 if c == UNROLL - 1 else c)
                pe.wait_ge(m.hid_t, t + 1)
                if later(t, two):
                    pe.wait_ge(m.outs, t + 1 - two)
                for k in range(blocks):
                    last = pe.matmul(PS[:, bank["outs"][c % 2], 0:D], HID_T[0:part, c % 2, k * P:(k + 1) * P],
                                     W[0:part, bass.ds(e + KD * 2 * hidden + k * D, D)],
                                     start=(k == 0), stop=(k == blocks - 1))
                last.then_inc(m.down, 1)

            return table, turn, up, turn_hidden, down

        @block.tensor
        def _(pe):
            pe.wait_ge(consts_ready, 1)

            def turn0(t, c):
                pe.wait_ge(h_ready, t + 1)
                if later(t, 4):
                    pe.wait_ge(evac0, t - 3)
                for i, rows in enumerate((XN_S, H_S)):
                    for k in range(KD):
                        last = pe.transpose(PS[:, c, i * D + k * P:i * D + (k + 1) * P],
                                            rows[:, c, k * P:(k + 1) * P], IDENT)
                last.then_inc(turned0, 1)

            def logits(t, c):
                pe.wait_ge(evac0, t + 1)
                for k in range(KD):
                    last = pe.matmul(PS[:, 7, bass.ds(t * E0, E0)], HT_S[:, c, k * P:(k + 1) * P], GATE0[:, k, :],
                                     start=(k == 0), stop=(k == KD - 1))
                last.then_inc(logits0, 1)

            pe.wait_ge(small_loaded, 32)
            pipeline(pe, NT, 4, (2, turn0), (0, logits))

            def ranks(r, area, experts, choices, rank, count):
                a = Area(*area)
                a.take(choices, NT, experts)
                a.take(NT, experts)
                mask = a.take(NT, experts).rearrange("p t e -> p (t e)")[:, 0:NT * experts // 2].bitcast(BF16)
                pe.wait_ge(r.mask, 1)
                pe.matmul(rank, BELOW, mask, start=True, stop=False)
                for i in range(NT - 1):
                    m = mask[:, i * experts:(i + 1) * experts]
                    pe.matmul(rank[:, (i + 1) * experts:].rearrange("p (t e) -> p t e", e=experts), ONES,
                              m[:, None, :].broadcast_to([P, NT - 1 - i, experts]), start=False, stop=(i == NT - 2))
                for i in range(NT):
                    last = pe.matmul(count, ONES, mask[:, i * experts:(i + 1) * experts],
                                     start=(i == 0), stop=(i == NT - 1))
                last.then_inc(r.ranks, 1)

            ranks(r0, (W, RT0), E0, K0, PS[:, 6, :], PS[:, 5, 0:E0])

            pe.wait_ge(attn_w_loaded, 48)
            pe.wait_ge(evac0, NT)

            def qvu(t, c):
                pe.wait_ge(xt_staged, t + 1)
                if later(t, 2):
                    pe.wait_ge(pre_ready, t - 1)
                for lo, hi, bank in ((0, 2 * D, 0), (2 * D, 3 * D, 1)):
                    for k in range(KD):
                        last = pe.matmul(PS[:, 2 * c + bank, 0:hi - lo], XT_S[:, c, k * P:(k + 1) * P],
                                         W_QVU[:, k, lo:hi], start=(k == 0), stop=(k == KD - 1))
                last.then_inc(qvu_ready, 1)

            half = NT // BATCH

            def add_kv(t, c):
                pe.wait_ge(qv_ready, t + 1)
                if later(t, 2):
                    pe.wait_ge(qt_saved, t - 1)
                if isinstance(t, int) and t == 0:
                    pe.wait_ge(r0.slots, 1)
                if isinstance(t, int) and t == half:
                    pe.wait_ge(kv_ready, 1)
                for k in range(KD):
                    last = pe.transpose(PS[:, 6 + c, k * P:(k + 1) * P], Q_S[:, c, k * P:(k + 1) * P], IDENT)
                last.then_inc(q_turned, 1)
                for k in range(KD):
                    last = pe.matmul(PS[:, 4 + k, 0:P], Q_S[:, c, k * P:(k + 1) * P], V_S[:, c, k * P:(k + 1) * P],
                                     start=(isinstance(t, int) and t % half == 0),
                                     stop=(isinstance(t, int) and t % half == half - 1), skip_group_check=True)
                last.then_inc(kv_added, 1)

            for b in range(BATCH):
                pipeline(pe, half, 2, (2, lambda t, c: qvu(t + b * half, c)), (0, lambda t, c: add_kv(t + b * half, c)))

            pe.wait_ge(kv_ready, 2)

            def out_heads(t, c):
                pe.wait_ge(qt_staged, t + 1)
                if later(t, 4):
                    pe.wait_ge(z_ready, t - 3)
                for k in range(KD):
                    last = pe.matmul(PS[:, O_BANKS[c], k * P:(k + 1) * P], QT_S[:, c % 2, k * P:(k + 1) * P],
                                     KV[:, t // half * KD + k, :], start=True, stop=True)
                last.then_inc(o_ready, 1)

            def turn_z(t, c):
                pe.wait_ge(z_ready, t + 1)
                if later(t, 2):
                    pe.wait_ge(zt_ready, t - 1)
                for k in range(KD):
                    last = pe.transpose(PS[:, 2 + c % 2, k * P:(k + 1) * P], Z_S[:, c % 2, k * P:(k + 1) * P], IDENT)
                last.then_inc(z_turned, 1)

            def out_proj(t, c):
                pe.wait_ge(zt_ready, t + 1)
                if later(t, 2):
                    pe.wait_ge(s_ready, t - 1)
                for k in range(KD):
                    last = pe.matmul(PS[:, 4 + c % 2, 0:D], ZT_S[:, c % 2, k * P:(k + 1) * P], W_O[:, k, :],
                                     start=(k == 0), stop=(k == KD - 1))
                last.then_inc(wo_done, 1)

            pipeline(pe, NT, 4, (2, out_heads), (0, turn_z), (-1, out_proj))

            def table_row(r, routed):
                pe.wait_ge(r.expert, 1)
                pe.matmul(PS[0:1, TABLE_BANK, 0:routed], EXPERT, IDENT[:, 0:routed], start=True, stop=True).then_inc(r.row, 1)

            pe.wait_ge(w0_loaded, 16)
            pe.wait_ge(s_ready, NT)
            table_row(r0, R0)
            table, turn, up, turn_hidden, down = mixture_tensor(pe, m0, I0, 1, P, WIDTH0, 2)

            def all_experts():
                pe.wait_ge(w0_late, 16 * 5)
                pe.wait_ge(r0.experts, 1)

            pipeline(pe, TILES0, UNROLL, (0, table), (2, turn), (1, up), (0, turn_hidden), (-1, down),
                     pause=(NT - UNROLL, all_experts))

            pe.wait_ge(small1_loaded, 96)
            pe.wait_ge(m0.outs, TILES0)

            def sum_rows(cm, t, c, choices):
                i = c % 2
                pe.wait_ge(cm.diag, t + 1)
                pe.wait_ge(cm.got[c], 4 * choices * (t - c) + 16 * choices)
                if later(t, 4):
                    pe.wait_ge(cm.x, t - 3)
                pe.wait_ge(c0.base, t + 1)
                terms = [(IDENT, BASE[:, i, :])]
                for k in range(choices):
                    terms.append((DIAG[:, i, k * P:(k + 1) * P], GOT[:, c, 1 + k, :]))
                for n, (weights, rows) in enumerate(terms):
                    last = pe.matmul(PS[:, SUM_BANK + c, 0:D], weights, rows, start=(n == 0), stop=(n == len(terms) - 1))
                last.then_inc(cm.acc, 1)

            def turn1(t, c):
                pe.wait_ge(c0.xn, t + 1)
                if later(t, 2):
                    pe.wait_ge(c0.xt, t - 1)
                for k in range(KD):
                    last = pe.transpose(PS[:, c % 2, k * P:(k + 1) * P], XN1_S[:, c, k * P:(k + 1) * P], IDENT)
                last.then_inc(c0.turned, 1)

            def logits1(t, c):
                pe.wait_ge(c0.xt, t + 1)
                for k in range(KD):
                    last = pe.matmul(PS[:, 7, bass.ds(t * E1, E1)], XT1_S[:, c % 2, k * P:(k + 1) * P], WR[:, k, :],
                                     start=(k == 0), stop=(k == KD - 1))
                last.then_inc(c0.logits, 1)

            pipeline(pe, NT, 4, (0, lambda t, c: sum_rows(c0, t, c, K0)), (-4, turn1), (-5, logits1))
            for j in range(4):
                if j == 2:
                    ranks(r1, (MB.tensor, RT1), E1, K1, PS[:, 6, 0:NT * E1], PS[:, 5, 0:E1])
                if j >= 2:
                    pe.wait_ge(dr_ready, j - 1)
                for lo, hi, bank in ((0, RANK, j % 2), (RANK, RANK + 96, 2 + j % 2)):
                    for k in range(KD):
                        last = pe.matmul(PS[0:hi - lo, bank, :], W_XP[:, k, lo:hi], XT[:, k, 512 * j:512 * j + 512],
                                         start=(k == 0), stop=(k == KD - 1))
                last.then_inc(xz_ready, 1)

            def low_rank(n):
                k, j = n // 4, n % 4
                if n >= 4:
                    pe.wait_ge(act_step, n - 3)
                pe.matmul(PS[:, j, :], W_DT[:, k * P:(k + 1) * P], DELTA_R[:, 512 * j:512 * j + 512],
                          start=True, stop=True).then_inc(dl_psum, 1)

            pe.wait_ge(dr_ready, 4)
            for n in range(8):
                low_rank(n)

            pe.wait_ge(bc3_ready, 3)
            pe.wait_ge(dl_exp, 8)
            pe.wait_ge(dl_max, 8)
            pe.wait_ge(w1_loaded, 16 * SLOTS1)
            table_row(r1, R1)

            def spread(row, part, bank):
                return pe.matmul(PS[:, bank, :], PICK[0:96, bass.ds(row, 1)].broadcast_to([96, P]),
                                 BC3[0:96, part:part + 512], start=True, stop=True)

            def spread_b(u, c):
                if c % 2:
                    return
                if later(u, 2):
                    pe.wait_ge(bu_ready, u)
                for h in range(2):
                    last = spread((u - c) // 4, (c // 2) * SEQ + 512 * h, B_BANK + h)
                last.then_inc(b_spread, 2)

            def spread_c(u, c):
                if later(u, 1):
                    pe.wait_ge(c_copied, u)
                spread((u - c) // 4 + N_STATE, c * 512, C_BANK).then_inc(c_spread, 1)

            table, turn, up, turn_hidden, down = mixture_tensor(pe, m1, H1P, 3, HB, WIDTH1, 1)
            pe.wait_ge(r1.experts, 1)
            pipeline(pe, TILES1, UNROLL, (0, table), (2, turn), (1, up), (1, spread_b), (0, turn_hidden), (2, spread_c),
                     (-1, down))

            def sum1(t):
                if t == 0:
                    pe.wait_ge(c1.shared[0], 16)
                    pe.wait_ge(m1.outs, TILES1)
                pe.wait_ge(c1.diag, t + 1)
                pe.wait_ge(c1.got[t % 4], 16 * K1 * (t // 4 + 1))
                if t >= 4:
                    pe.wait_ge(gated, NT + t - 3)
                bank = PS[:, SUM1_BANK + t % 4, 0:D]
                pe.matmul(bank, HALF, GOT1[:, t, 0, :], start=True, stop=False)
                for k in range(K1):
                    last = pe.matmul(bank, DIAG[:, t % 2, k * P:(k + 1) * P], GOT1[:, t, 1 + k, :], start=False,
                                     stop=(k == K1 - 1))
                last.then_inc(c1.acc, 1)

            def turn_y(t):
                if t == 0:
                    for half in range(KD):
                        pe.wait_ge(y_added[half], UNITS // KD)
                if t >= 4:
                    pe.wait_ge(c1.x, t - 3)
                for k in range(KD):
                    last = pe.transpose(PS[:, Y_BANKS[t % 4], k * P:(k + 1) * P], XT[:, k, t * P:(t + 1) * P], IDENT)
                last.then_inc(c1.y_rows, 1)

            for v in range(TAIL):
                spread_b(TILES1 + v, (TILES1 + v) % 4)
                spread_c(TILES1 + v, (TILES1 + v) % 4)
                if v >= SUM_LAG:
                    sum1(v - SUM_LAG)
            sums_and_y(TAIL - SUM_LAG, sum1, turn_y)


def kernel(**inputs):
    import numpy as np
    import concourse.bacc as bacc
    from concourse.bass_utils import run_bass_kernel_spmd

    g = {k: np.asarray(v) for k, v in inputs.items()}

    def blocks(w):
        return w.reshape(-1, P, w.shape[1]).transpose(1, 0, 2)

    def expert0(w13, w2):
        return np.concatenate([blocks(w13).reshape(P, -1), blocks(w2).reshape(P, -1)], axis=1)

    def expert1(w1, w3, w2):
        z = np.zeros((P, KD, 2, H1P), np.float32)
        z[:, :, 0, :H1] = blocks(w1.T)
        z[:, :, 1, :H1] = blocks(w3.T)
        d = np.zeros((H1P, D), np.float32)
        d[:H1] = w2.T
        e = np.zeros((P, 3, D), np.float32)
        e[:HB] = d.reshape(3, HB, D).transpose(1, 0, 2)
        return np.concatenate([z.reshape(P, -1), e.reshape(P, -1)], axis=1)

    shared0 = expert0(np.concatenate([g["L0_ffn_shared_gate_w"], g["L0_ffn_shared_up_w"]], axis=1),
                      g["L0_ffn_shared_down_w"])
    moe0 = np.concatenate([shared0] + [expert0(g["L0_ffn_w13"][e], g["L0_ffn_w2"][e]) for e in range(E0)], axis=1)
    shared1 = expert1(g["L1_ffn_sw1"], g["L1_ffn_sw3"], g["L1_ffn_sw2"])
    moe1 = np.concatenate([shared1] + [expert1(g["L1_ffn_ew1"][e], g["L1_ffn_ew3"][e], g["L1_ffn_ew2"][e])
                                       for e in range(E1)], axis=1)
    xp = g["L1_attn_W_xproj"].T
    bc = xp[:, RANK:]

    def halves(v):
        return v.reshape(KD, P, -1).transpose(1, 0, 2).reshape(P, -1)

    arrays = {
        "x": g["L0_attn_x"].reshape(NT, P, D).transpose(1, 0, 2),
        "w_qvu": blocks(np.concatenate([g["L0_attn_Wqk"], g["L0_attn_Wv"], g["L0_attn_Wu"]], axis=1)),
        "b_qvu": np.concatenate([g["L0_attn_bqk"], g["L0_attn_bv"], g["L0_attn_bu"]]),
        "w_o": blocks(g["L0_attn_Wo"]),
        "rows4": np.stack([g["L0_attn_bo"], g["L0_attn_ln_g"], g["L0_attn_ln_b"], g["L0_ffn_norm_w"]]),
        "gate0": blocks(g["L0_ffn_gate_w"].T),
        "moe0": moe0,
        "moe1": moe1,
        "w_xproj": blocks(np.concatenate([xp[:, :RANK], bc, bc, bc], axis=1)),
        "w_dt": g["L1_attn_W_dt"].T,
        "per_channel": np.concatenate([halves(g["L1_attn_b_dt"]), halves(g["L1_attn_D_param"]),
                                       halves(g["L1_attn_A_log"])], axis=1),
        "wr": blocks(g["L1_ffn_wr"].T),
    }
    arrays = {f"{k}_dram": np.ascontiguousarray(v) for k, v in arrays.items()}
    nc = bacc.Bacc("TRN2", target_bir_lowering=False, num_devices=1)
    args = [nc.dram_tensor(k, a.shape, mybir.dt.from_np(a.dtype), kind="ExternalInput").ap() for k, a in arrays.items()]
    out = nc.dram_tensor("out_dram", (P, NT, D), F32, kind="ExternalOutput").ap()
    two_layers(nc, *args, out)
    r = run_bass_kernel_spmd(nc, [arrays], core_ids=[0])
    return np.ascontiguousarray(r.results[0]["out_dram"].transpose(1, 0, 2)).reshape(BATCH, SEQ, D)
```
